# Optimizing a Trainium2 kernel written in Bass

```python
import numpy as np
import jax
import jax.numpy as jnp

def _softmax(x, axis=-1):
    return jax.nn.softmax(x, axis=axis)

def _gelu(x):
    return jax.nn.gelu(x, approximate=True)

def _silu(x):
    return jax.nn.silu(x)

def _sigmoid(x):
    return jax.nn.sigmoid(x)

def _layernorm(x, axis=-1, eps=1e-05):
    m = jnp.mean(x, axis=axis, keepdims=True)
    v = jnp.var(x, axis=axis, keepdims=True)
    return (x - m) / jnp.sqrt(v + eps)

def _scatter_add(tgt, idx, src, axis=0):
    return tgt.at[idx].add(src)

def _segment_sum(src, seg, n):
    return jax.ops.segment_sum(src, seg, n)
kernel_name = 'mk_gnn_preln_d2_gnn_r8_d6076e'

def setup_inputs(seed: int=0):
    np.random.seed(seed)
    _w = jnp.asarray

    def _rec_inputs():
        import jax
        import jax.numpy as jnp
        _gk = jax.random.key(seed)
        x = -0.0009044 + 1 * jax.random.normal(jax.random.fold_in(_gk, 1), (12500, 16), jnp.float32)
        src = jax.random.randint(jax.random.fold_in(_gk, 2), (400000,), 0, 12500, jnp.int32)
        dst = jax.random.randint(jax.random.fold_in(_gk, 3), (400000,), 0, 12500, jnp.int32)
        _o = jnp.argsort(dst, stable=True)
        src = src[_o]
        dst = dst[_o]
        edge_attr_8 = -0.00019784 + 0.999804 * jax.random.normal(jax.random.fold_in(_gk, 12), (400000, 8), jnp.float32)
        return (x, src, dst, edge_attr_8)
    x, src, dst, edge_attr_8 = _rec_inputs()

    def _L0_gnn_setup():
        import jax, jax.numpy as jnp
        import numpy as np
        N_NODES = 12500
        key = jax.random.key(seed)
        k1, k2, k3 = jax.random.split(key, 3)
        features = jax.random.normal(k1, (N_NODES, 16), dtype=jnp.float32)
        src = jax.random.randint(k2, (625000,), 0, N_NODES, dtype=jnp.int64)
        dst = jax.random.randint(k3, (625000,), 0, N_NODES, dtype=jnp.int64)
        return {'features': features, 'src': src, 'dst': dst}
    _L0_gnn_all = _L0_gnn_setup()
    _L0_gnn_in = {k: v for k, v in _L0_gnn_all.items() if k in ()}
    del _L0_gnn_all

    def _L1_gnn_setup():
        import jax, jax.numpy as jnp
        import numpy as np
        N = 6250
        E = 100000
        S = 2
        D_NODE_IN, D_EDGE_IN, D, H, D_OUT = (16, 8, 64, 64, 16)
        LN_EPS = 1e-05

        def _mlp(x, w0, b0, w1, b1):
            return jax.nn.silu(x @ w0 + b0) @ w1 + b1

        def _ln(x, g, b):
            m = jnp.mean(x, axis=-1, keepdims=True)
            v = jnp.var(x, axis=-1, keepdims=True)
            return (x - m) * jax.lax.rsqrt(v + LN_EPS) * g + b
        key = jax.random.key(seed)
        ks = iter(jax.random.split(key, 40))
        p = lambda shape: jax.random.normal(next(ks), shape, dtype=jnp.float32) * 0.1
        inp = {'node_feat': jax.random.normal(next(ks), (N, D_NODE_IN), dtype=jnp.float32), 'edge_feat': jax.random.normal(next(ks), (E, D_EDGE_IN), dtype=jnp.float32), 'senders': jax.random.randint(next(ks), (E,), 0, N, dtype=jnp.int32), 'receivers': jax.random.randint(next(ks), (E,), 0, N, dtype=jnp.int32), 'node_enc_w0': p((D_NODE_IN, H)), 'node_enc_b0': p((H,)), 'node_enc_w1': p((H, D)), 'node_enc_b1': p((D,)), 'node_enc_g': jnp.ones((D,), jnp.float32), 'node_enc_beta': jnp.zeros((D,), jnp.float32), 'edge_enc_w0': p((D_EDGE_IN, H)), 'edge_enc_b0': p((H,)), 'edge_enc_w1': p((H, D)), 'edge_enc_b1': p((D,)), 'edge_enc_g': jnp.ones((D,), jnp.float32), 'edge_enc_beta': jnp.zeros((D,), jnp.float32), 'edge_blk_w0': p((S, 3 * D, H)), 'edge_blk_b0': p((S, H)), 'edge_blk_w1': p((S, H, D)), 'edge_blk_b1': p((S, D)), 'edge_blk_g': jnp.ones((S, D), jnp.float32), 'edge_blk_beta': jnp.zeros((S, D), jnp.float32), 'node_blk_w0': p((S, 2 * D, H)), 'node_blk_b0': p((S, H)), 'node_blk_w1': p((S, H, D)), 'node_blk_b1': p((S, D)), 'node_blk_g': jnp.ones((S, D), jnp.float32), 'node_blk_beta': jnp.zeros((S, D), jnp.float32), 'dec_w0': p((D, H)), 'dec_b0': p((H,)), 'dec_w1': p((H, D_OUT)), 'dec_b1': p((D_OUT,))}
        return inp
    _L1_gnn_all = _L1_gnn_setup()
    _L1_gnn_in = {k: v for k, v in _L1_gnn_all.items() if k in ('node_enc_w0', 'node_enc_b0', 'node_enc_w1', 'node_enc_b1', 'node_enc_g', 'node_enc_beta', 'edge_enc_w0', 'edge_enc_b0', 'edge_enc_w1', 'edge_enc_b1', 'edge_enc_g', 'edge_enc_beta', 'edge_blk_w0', 'edge_blk_b0', 'edge_blk_w1', 'edge_blk_b1', 'edge_blk_g', 'edge_blk_beta', 'node_blk_w0', 'node_blk_b0', 'node_blk_w1', 'node_blk_b1', 'node_blk_g', 'node_blk_beta', 'dec_w0', 'dec_b0', 'dec_w1', 'dec_b1')}
    del _L1_gnn_all
    return {'x': x, 'src': src, 'dst': dst, 'edge_attr_8': edge_attr_8, 'L1_gnn_node_enc_w0': _L1_gnn_in['node_enc_w0'], 'L1_gnn_node_enc_b0': _L1_gnn_in['node_enc_b0'], 'L1_gnn_node_enc_w1': _L1_gnn_in['node_enc_w1'], 'L1_gnn_node_enc_b1': _L1_gnn_in['node_enc_b1'], 'L1_gnn_node_enc_g': _L1_gnn_in['node_enc_g'], 'L1_gnn_node_enc_beta': _L1_gnn_in['node_enc_beta'], 'L1_gnn_edge_enc_w0': _L1_gnn_in['edge_enc_w0'], 'L1_gnn_edge_enc_b0': _L1_gnn_in['edge_enc_b0'], 'L1_gnn_edge_enc_w1': _L1_gnn_in['edge_enc_w1'], 'L1_gnn_edge_enc_b1': _L1_gnn_in['edge_enc_b1'], 'L1_gnn_edge_enc_g': _L1_gnn_in['edge_enc_g'], 'L1_gnn_edge_enc_beta': _L1_gnn_in['edge_enc_beta'], 'L1_gnn_edge_blk_w0': _L1_gnn_in['edge_blk_w0'], 'L1_gnn_edge_blk_b0': _L1_gnn_in['edge_blk_b0'], 'L1_gnn_edge_blk_w1': _L1_gnn_in['edge_blk_w1'], 'L1_gnn_edge_blk_b1': _L1_gnn_in['edge_blk_b1'], 'L1_gnn_edge_blk_g': _L1_gnn_in['edge_blk_g'], 'L1_gnn_edge_blk_beta': _L1_gnn_in['edge_blk_beta'], 'L1_gnn_node_blk_w0': _L1_gnn_in['node_blk_w0'], 'L1_gnn_node_blk_b0': _L1_gnn_in['node_blk_b0'], 'L1_gnn_node_blk_w1': _L1_gnn_in['node_blk_w1'], 'L1_gnn_node_blk_b1': _L1_gnn_in['node_blk_b1'], 'L1_gnn_node_blk_g': _L1_gnn_in['node_blk_g'], 'L1_gnn_node_blk_beta': _L1_gnn_in['node_blk_beta'], 'L1_gnn_dec_w0': _L1_gnn_in['dec_w0'], 'L1_gnn_dec_b0': _L1_gnn_in['dec_b0'], 'L1_gnn_dec_w1': _L1_gnn_in['dec_w1'], 'L1_gnn_dec_b1': _L1_gnn_in['dec_b1']}

def reference(x, src, dst, edge_attr_8, L1_gnn_node_enc_w0, L1_gnn_node_enc_b0, L1_gnn_node_enc_w1, L1_gnn_node_enc_b1, L1_gnn_node_enc_g, L1_gnn_node_enc_beta, L1_gnn_edge_enc_w0, L1_gnn_edge_enc_b0, L1_gnn_edge_enc_w1, L1_gnn_edge_enc_b1, L1_gnn_edge_enc_g, L1_gnn_edge_enc_beta, L1_gnn_edge_blk_w0, L1_gnn_edge_blk_b0, L1_gnn_edge_blk_w1, L1_gnn_edge_blk_b1, L1_gnn_edge_blk_g, L1_gnn_edge_blk_beta, L1_gnn_node_blk_w0, L1_gnn_node_blk_b0, L1_gnn_node_blk_w1, L1_gnn_node_blk_b1, L1_gnn_node_blk_g, L1_gnn_node_blk_beta, L1_gnn_dec_w0, L1_gnn_dec_b0, L1_gnn_dec_w1, L1_gnn_dec_b1):
    import jax
    import jax.numpy as jnp

    def _L0_gnn_ref(features, src, dst):
        import jax, jax.numpy as jnp
        import numpy as np
        N_NODES = 12500
        n = features.shape[0]
        ones = jnp.ones(src.shape[0], dtype=features.dtype)
        out_deg = jnp.zeros(n, dtype=features.dtype).at[src].add(ones)
        out_deg = jnp.clip(out_deg, 1.0, None)
        in_deg = jnp.zeros(n, dtype=features.dtype).at[dst].add(ones)
        in_deg = jnp.clip(in_deg, 1.0, None)
        x = features * (out_deg ** (-0.5))[:, None]
        agg = jnp.zeros_like(features).at[dst].add(x[src])
        return agg * (in_deg ** (-0.5))[:, None]

    def _L1_gnn_ref(node_feat, edge_feat, senders, receivers, node_enc_w0, node_enc_b0, node_enc_w1, node_enc_b1, node_enc_g, node_enc_beta, edge_enc_w0, edge_enc_b0, edge_enc_w1, edge_enc_b1, edge_enc_g, edge_enc_beta, edge_blk_w0, edge_blk_b0, edge_blk_w1, edge_blk_b1, edge_blk_g, edge_blk_beta, node_blk_w0, node_blk_b0, node_blk_w1, node_blk_b1, node_blk_g, node_blk_beta, dec_w0, dec_b0, dec_w1, dec_b1):
        import jax, jax.numpy as jnp
        import numpy as np
        N = 6250
        E = 100000
        S = 2
        D_NODE_IN, D_EDGE_IN, D, H, D_OUT = (16, 8, 64, 64, 16)
        LN_EPS = 1e-05

        def _mlp(x, w0, b0, w1, b1):
            return jax.nn.silu(x @ w0 + b0) @ w1 + b1

        def _ln(x, g, b):
            m = jnp.mean(x, axis=-1, keepdims=True)
            v = jnp.var(x, axis=-1, keepdims=True)
            return (x - m) * jax.lax.rsqrt(v + LN_EPS) * g + b
        num_nodes = node_feat.shape[0]
        n = _ln(_mlp(node_feat, node_enc_w0, node_enc_b0, node_enc_w1, node_enc_b1), node_enc_g, node_enc_beta)
        e = _ln(_mlp(edge_feat, edge_enc_w0, edge_enc_b0, edge_enc_w1, edge_enc_b1), edge_enc_g, edge_enc_beta)
        for s in range(S):
            ce = jnp.concatenate([e, n[senders], n[receivers]], axis=-1)
            e = e + _ln(_mlp(ce, edge_blk_w0[s], edge_blk_b0[s], edge_blk_w1[s], edge_blk_b1[s]), edge_blk_g[s], edge_blk_beta[s])
            agg = jax.ops.segment_sum(e.astype(jnp.float32), receivers, num_segments=num_nodes)
            cn = jnp.concatenate([n, agg.astype(n.dtype)], axis=-1)
            n = n + _ln(_mlp(cn, node_blk_w0[s], node_blk_b0[s], node_blk_w1[s], node_blk_b1[s]), node_blk_g[s], node_blk_beta[s])
        return _mlp(n, dec_w0, dec_b0, dec_w1, dec_b1)
    h = jnp.maximum(_layernorm(x, axis=-1), 0.0)
    x = x + _L0_gnn_ref(h, src, dst)
    h = jnp.maximum(_layernorm(x, axis=-1), 0.0)
    x = x + _L1_gnn_ref(h, edge_attr_8, src, dst, L1_gnn_node_enc_w0, L1_gnn_node_enc_b0, L1_gnn_node_enc_w1, L1_gnn_node_enc_b1, L1_gnn_node_enc_g, L1_gnn_node_enc_beta, L1_gnn_edge_enc_w0, L1_gnn_edge_enc_b0, L1_gnn_edge_enc_w1, L1_gnn_edge_enc_b1, L1_gnn_edge_enc_g, L1_gnn_edge_enc_beta, L1_gnn_edge_blk_w0, L1_gnn_edge_blk_b0, L1_gnn_edge_blk_w1, L1_gnn_edge_blk_b1, L1_gnn_edge_blk_g, L1_gnn_edge_blk_beta, L1_gnn_node_blk_w0, L1_gnn_node_blk_b0, L1_gnn_node_blk_w1, L1_gnn_node_blk_b1, L1_gnn_node_blk_g, L1_gnn_node_blk_beta, L1_gnn_dec_w0, L1_gnn_dec_b0, L1_gnn_dec_w1, L1_gnn_dec_b1)
    return x

_drawn_inputs = setup_inputs


def setup_inputs(seed=0):
    import zlib

    import numpy as np

    out = dict(_drawn_inputs(seed))
    spreads = {'L1_gnn_node_enc_g': (1.0, 0.2),
     'L1_gnn_node_enc_beta': (0.0, 0.1),
     'L1_gnn_edge_enc_g': (1.0, 0.2),
     'L1_gnn_edge_enc_beta': (0.0, 0.1),
     'L1_gnn_edge_blk_g': (1.0, 0.2),
     'L1_gnn_edge_blk_beta': (0.0, 0.1),
     'L1_gnn_node_blk_g': (1.0, 0.2),
     'L1_gnn_node_blk_beta': (0.0, 0.1)}
    factors = {'L1_gnn_node_blk_b0': 47.755, 'L1_gnn_node_blk_b1': 32.799, 'L1_gnn_dec_b0': 2.767}
    for name, (base, spread) in spreads.items():
        noise = np.random.default_rng([zlib.crc32(name.encode()), seed]).standard_normal(out[name].shape)
        drawn = base * np.exp(spread * noise) if base else spread * noise
        out[name] = jnp.asarray(drawn.astype(out[name].dtype))
    for name, factor in factors.items():
        out[name] = (out[name] * factor).astype(out[name].dtype)
    return out
```

```python
from contextlib import ExitStack, contextmanager

import concourse.bass as bass
from concourse import mybir

ALU = mybir.AluOpType
ACT = mybir.ActivationFunctionType
AX_X = mybir.AxisListType.X
F32 = mybir.dt.float32
BF16 = mybir.dt.bfloat16
I32 = mybir.dt.int32
U32 = mybir.dt.uint32
P = 128

N_NODES, N_EDGES, X_DIM, E_DIM, D, OUT_DIM, STEPS = 12500, 400000, 16, 8, 64, 16, 2
TILES = 4
CHUNK = TILES * P
ROUND = 2 * CHUNK
WIN = 64
HALF = 6656
NODES = 2 * HALF
HI = NODES // P
NT = HALF // 512
PAD_NODE = N_NODES
PAD_DST = 20000
LAST_BASE = 12544
BLOCK_E = P * P
FAST_ROUNDS = 2 * -(-N_EDGES // (2 * ROUND))
FAST_BLOCKS = -(-FAST_ROUNDS * ROUND // BLOCK_E)
WINDOWS = -(-N_NODES // WIN)
SLOT_CHUNKS = -(-N_EDGES // CHUNK) + WINDOWS
MAX_BLOCKS = -(-SLOT_CHUNKS * CHUNK // BLOCK_E)
SLOTS = MAX_BLOCKS * BLOCK_E
MAX_ROUNDS = SLOTS // ROUND
EPS = 1e-5

VEC = ["edge_enc", "edge_blk0", "edge_blk1", "node_enc", "node_blk0", "node_blk1"]


def vcol(mlp, what):
    return 4 * VEC.index(mlp) + ["b0", "b1", "g", "beta"].index(what)


DEC_B0 = 4 * len(VEC)
NVEC = DEC_B0 + 1


@contextmanager
def semaphores(nc, tag):
    made = []

    def sem(name):
        made.append(nc.alloc_semaphore(name=tag + name))
        return made[-1]

    yield sem
    nc.clear_and_free_semaphores(made)
    nc.all_engine_barrier()


class Slot:

    def __init__(self, m, b):
        self.m, self.b = m, b

    def back(self, k):
        q = self.b - k
        return Slot(self.m + q // 2, q % 2)

    def exists(self):
        return not isinstance(self.m, int) or self.m >= 0

    @property
    def n(self):
        return self.m * 2 + self.b


def wait(eng, sem, slot, per=1):
    if slot.exists():
        eng.wait_ge(sem, slot.n * per + per)


def landed(eng, sems, slot, per=16):
    if slot.exists():
        eng.wait_ge(sems[slot.b], slot.m * per + per)


def held(eng, passed):
    eng.sem_inc(passed, 1)


def rounds(eng, body, pairs):
    body(Slot(0, 0))
    body(Slot(0, 1))
    with eng.Fori(1, pairs) as m:
        body(Slot(m, 0))
        body(Slot(m, 1))


def gnn_kernel(nc, x, src, dst, edge_attr, w, out):
    with ExitStack() as ctx:
        def sb(name, shape, dt=F32):
            return ctx.enter_context(nc.sbuf_tensor(name, shape, dt))

        def dram(name, shape, dt=F32):
            return nc.dram_tensor(name, shape, dt, kind="Internal").ap()

        src_d = dram("src_slots", (SLOTS,), I32)
        dst_d = dram("dst_slots", (SLOTS,), I32)
        attr_d = dram("attr_slots", (SLOTS, E_DIM))
        local_d = dram("local_dst", (SLOTS,), BF16)
        lists_d = dram("tile_lists", (MAX_ROUNDS, P, 16), I32)
        xg_d = dram("sender_x", (NODES, 32))
        ps_d = dram("sender_part", (NODES, D))
        pr_d = dram("receiver_part", (NODES, D))
        edge_d = dram("edge_state", (MAX_ROUNDS, P, CHUNK))

        part_f = sb("part_f", [P, 1])
        part64 = sb("part64", [P, 1])
        row_f = sb("row_f", [P, P])
        row_bf = sb("row_bf", [P, P], BF16)
        ident = sb("ident", [P, P])
        mean_w = sb("mean_w", [P, P])
        sum_ab = sb("sum_ab", [P, 32])
        eps_c = sb("eps_c", [P, 1])
        vecs = sb("vecs", [P, NVEC])
        vmean = sb("vmean", [P, NVEC])
        dec_b1 = sb("dec_b1", [P, OUT_DIM])
        enc_w0 = sb("enc_w0", [64, TILES, P])
        nenc_w0 = sb("nenc_w0", [32, P])
        w1 = {k: sb("w1_" + k, [P, P]) for k in VEC}
        ew0 = [sb(f"ew0_{s}", [P, P]) for s in range(STEPS)]
        proj_w = [sb(f"proj_w{s}", [P, P]) for s in range(STEPS)]
        nw0 = [sb(f"nw0_{s}", [P, P]) for s in range(STEPS)]
        aw0 = [sb(f"aw0_{s}", [P, D]) for s in range(STEPS)]
        dec_w0 = sb("dec_w0", [P, P])
        dec_w1 = sb("dec_w1", [P, OUT_DIM])
        wmean = sb("wmean", [P, len(VEC)])
        agg = sb("agg", [P, NODES])
        node = sb("node", [P, HALF])
        x1 = sb("x1", [P, HI, X_DIM])
        base_sb = sb("base_sb", [1, 2 * MAX_ROUNDS], I32)
        deg = sb("deg", [P, HI])

        def halves(eng, dst_tile, ap, sem):
            eng.dma_start(dst_tile[0:64, 0:64], ap).then_inc(sem, 16)
            eng.dma_start(dst_tile[64:128, 64:128], ap).then_inc(sem, 16)
            return 2

        n_ld = [0]
        with ExitStack() as c1:
            sem = c1.enter_context(semaphores(nc, "set_"))
            s_zero, s_ld, s_io, s_c, s_vm, s_cp, s_pad = (sem(k) for k in (
                "zeroed", "weights_landed", "iota_done", "const_step", "vec_means", "lists_copied", "pad_made"))
            iota_i = c1.enter_context(nc.sbuf_tensor("iota_i", [P, P], I32))
            iota_p = c1.enter_context(nc.sbuf_tensor("iota_p", [P, 1], I32))
            tmp = c1.enter_context(nc.sbuf_tensor("tmp", [P, P], F32))
            hi_p = c1.enter_context(nc.sbuf_tensor("hi_p", [P, 1], F32))
            pad_s = c1.enter_context(nc.sbuf_tensor("pad_s", [P, 1024], I32))
            pad_t = c1.enter_context(nc.sbuf_tensor("pad_t", [P, 1024], I32))
            pad_a = c1.enter_context(nc.sbuf_tensor("pad_a", [P, 8 * 1024], F32))
            vm_ps = c1.enter_context(nc.psum_tensor("vm_ps", [P, 512], F32))
            zero_list = [enc_w0, nenc_w0, dec_w0, *w1.values(), *ew0, *nw0]
            with nc.Block() as block:
                @block.sync
                def _(sp):
                    def load(t, ap):
                        sp.dma_start(t, ap).then_inc(s_ld, 16)
                        n_ld[0] += 1

                    for k in VEC:
                        key, s = (k[:-1], int(k[-1])) if k[-1] in "01" else (k, None)
                        for what in ("b0", "b1", "g", "beta"):
                            v = w[f"{key}_{what}"]
                            v = v if s is None else v[s]
                            for h in range(2):
                                load(vecs[64 * h:64 * h + 64, vcol(k, what):vcol(k, what) + 1],
                                     v.rearrange("(d a) -> d a", a=1))
                    for h in range(2):
                        load(vecs[64 * h:64 * h + 64, DEC_B0:DEC_B0 + 1], w["dec_b0"].rearrange("(d a) -> d a", a=1))
                        load(dec_w1[64 * h:64 * h + 64, :], w["dec_w1"])
                        for s in range(STEPS):
                            for q in range(2):
                                load(proj_w[s][64 * h:64 * h + 64, 64 * q:64 * q + 64],
                                     w["edge_blk_w0"][s, D * (q + 1):D * (q + 2), :])
                            load(aw0[s][64 * h:64 * h + 64, :], w["node_blk_w0"][s, D:2 * D, :])
                    load(dec_b1[:, :], w["dec_b1"].rearrange("(a d) -> a d", a=1).broadcast_to([P, OUT_DIM]))
                    sp.wait_ge(s_zero, len(zero_list))
                    for h in range(2):
                        for t in range(TILES):
                            r = 8 * (t + TILES * h)
                            load(enc_w0[r:r + 8, t, 64 * h:64 * h + 64], w["edge_enc_w0"])
                        load(nenc_w0[16 * h:16 * h + 16, 64 * h:64 * h + 64], w["node_enc_w0"])
                        q = slice(64 * h, 64 * h + 64)
                        load(dec_w0[q, q], w["dec_w0"])
                        load(w1["edge_enc"][q, q], w["edge_enc_w1"])
                        load(w1["node_enc"][q, q], w["node_enc_w1"])
                        for s in range(STEPS):
                            load(ew0[s][q, q], w["edge_blk_w0"][s, 0:D, :])
                            load(nw0[s][q, q], w["node_blk_w0"][s, 0:D, :])
                            load(w1[f"edge_blk{s}"][q, q], w["edge_blk_w1"][s])
                            load(w1[f"node_blk{s}"][q, q], w["node_blk_w1"][s])
                    sp.wait_ge(s_ld, 16 * n_ld[0])

                @block.scalar
                def _(act):
                    q = N_EDGES // P
                    act.dma_start(src_d[0:N_EDGES].rearrange("(p q) -> p q", p=P),
                                  src.rearrange("(p q) -> p q", p=P)).then_inc(s_cp, 16)
                    act.dma_start(dst_d[0:N_EDGES].rearrange("(p q) -> p q", p=P),
                                  dst.rearrange("(p q) -> p q", p=P)).then_inc(s_cp, 16)
                    act.dma_start(attr_d[0:N_EDGES, :].rearrange("(p q) c -> p (q c)", p=P),
                                  edge_attr.rearrange("(p q) c -> p (q c)", p=P)).then_inc(s_cp, 16)
                    q = (SLOTS - N_EDGES) // P
                    act.wait_ge(s_pad, 3)
                    act.dma_start(src_d[N_EDGES:].rearrange("(p q) -> p q", p=P), pad_s[:, 0:q]).then_inc(s_cp, 16)
                    act.dma_start(dst_d[N_EDGES:].rearrange("(p q) -> p q", p=P), pad_t[:, 0:q]).then_inc(s_cp, 16)
                    act.dma_start(attr_d[N_EDGES:, :].rearrange("(p q) c -> p (q c)", p=P),
                                  pad_a[:, 0:8 * q]).then_inc(s_cp, 16)
                    act.wait_ge(s_cp, 96)

                @block.gpsimd
                def _(pool):
                    nc.gpsimd.iota(iota_i[:, :], pattern=[[1, P]], base=0, channel_multiplier=0).then_inc(s_io, 1)
                    nc.gpsimd.iota(iota_p[:, :], pattern=[[0, 1]], base=0, channel_multiplier=1).then_inc(s_io, 1)
                    for t in zero_list:
                        nc.gpsimd.memset(t[:], 0.0).then_inc(s_zero, 1)
                    nc.gpsimd.memset(pad_s[:, :], PAD_NODE).then_inc(s_pad, 1)
                    nc.gpsimd.memset(pad_t[:, :], PAD_DST).then_inc(s_pad, 1)
                    nc.gpsimd.memset(pad_a[:, :], 0.0).then_inc(s_pad, 1)

                @block.vector
                def _(dve):
                    k = [0]

                    def step(ins):
                        k[0] += 1
                        ins.then_inc(s_c, 1)
                        dve.wait_ge(s_c, k[0])

                    v = nc.vector
                    dve.wait_ge(s_io, 2)
                    step(v.memset(eps_c[:, :], EPS))
                    step(v.tensor_copy(row_f[:, :], iota_i[:, :]))
                    step(v.tensor_copy(row_bf[:, :], iota_i[:, :]))
                    step(v.tensor_copy(part_f[:, :], iota_p[:, :]))
                    step(v.tensor_scalar(ident[:, :], row_f[:, :], part_f[:, 0:1], None, ALU.is_equal))
                    step(v.tensor_scalar(hi_p[:, :], part_f[:, :], 64.0, None, ALU.is_ge))
                    step(v.scalar_tensor_tensor(part64[:, :], hi_p[:, :], -64.0, part_f[:, :], ALU.mult, ALU.add))
                    step(v.tensor_scalar(tmp[:, :], row_f[:, :], 64.0, None, ALU.is_ge))
                    step(v.tensor_scalar(mean_w[:, :], tmp[:, :], hi_p[:, 0:1], 1.0 / D, ALU.is_equal, ALU.mult))
                    step(v.tensor_scalar(sum_ab[:, :], row_f[:, 0:32], part64[:, 0:1], None, ALU.is_equal))
                    dve.wait_ge(s_ld, 16 * n_ld[0])
                    for i, name in enumerate(VEC):
                        step(v.tensor_reduce(wmean[:, i:i + 1], w1[name][:, :], AX_X, ALU.add))
                    step(v.tensor_scalar(wmean[:, :], wmean[:, :], -1.0 / D, None, ALU.mult))
                    for i, name in enumerate(VEC):
                        for h in range(2):
                            q = slice(64 * h, 64 * h + 64)
                            step(v.tensor_scalar(w1[name][q, q], w1[name][q, q], wmean[q, i:i + 1], None, ALU.add))
                    dve.wait_ge(s_vm, 1)
                    step(v.tensor_copy(vmean[:, :], vm_ps[:, 0:NVEC]))
                    for name in VEC:
                        c = vcol(name, "b1")
                        step(v.tensor_tensor(vecs[:, c:c + 1], vecs[:, c:c + 1], vmean[:, c:c + 1], ALU.subtract))

                @block.tensor
                def _(pe):
                    pe.wait_ge(s_ld, 16 * n_ld[0])
                    pe.wait_ge(s_c, 10)
                    nc.tensor.matmul(vm_ps[:, 0:NVEC], mean_w[:, :], vecs[:, :], start=True, stop=True).then_inc(s_vm, 1)

        pairs, blocks = FAST_ROUNDS // 2, FAST_BLOCKS

        edge_lists(nc, src_d, dst_d, local_d, lists_d, base_sb, deg, row_bf, ident, blocks)
        scaled_senders(nc, x, x1, deg, xg_d, eps_c)
        first_layer(nc, lists_d, attr_d, xg_d, edge_d, base_sb, agg, enc_w0, w1["edge_enc"], mean_w, ident,
                    row_f, vecs, eps_c, pairs)
        vv = dict(nc=nc, agg=agg, node=node, x1=x1, vecs=vecs, mean_w=mean_w, ident=ident, eps_c=eps_c,
                  ps_d=ps_d, pr_d=pr_d)
        node_phase(**vv, mlp="node_enc", w_in=nenc_w0, w_mid=w1["node_enc"], proj=proj_w[0], sum_ab=sum_ab)
        for s in range(STEPS):
            edge_step(nc, lists_d, local_d, edge_d, ps_d, pr_d, base_sb, agg, ew0[s], w1[f"edge_blk{s}"], mean_w,
                      ident, row_f, part64, vecs, eps_c, f"edge_blk{s}", s < STEPS - 1, pairs)
            node_phase(**vv, mlp=f"node_blk{s}", w_in=nw0[s], w_mid=w1[f"node_blk{s}"], w_agg=aw0[s],
                       proj=proj_w[s + 1] if s < STEPS - 1 else None,
                       dec=(dec_w0, dec_w1, dec_b1, out) if s == STEPS - 1 else None)


def edge_lists(nc, src_d, dst_d, local_d, lists_d, base_sb, deg, row_bf, ident, blocks):
    with ExitStack() as ctx:
        def sb(name, shape, dt=F32):
            return ctx.enter_context(nc.sbuf_tensor("el_" + name, shape, dt))

        sem = ctx.enter_context(semaphores(nc, "el_"))

        base_col = sb("base_col", [P, MAX_BLOCKS], I32)
        base_f = sb("base_f", [P, MAX_BLOCKS])
        srow = sb("srow", [P, P], I32)
        drow = sb("drow", [P, P], I32)
        srow_f = sb("srow_f", [P, P])
        local_f = sb("local_f", [P, P])
        local_bf = sb("local_bf", [P, P], BF16)
        lists = sb("lists", [P, 16, 16], I32)
        s_lo = sb("s_lo", [P, P], I32)
        s_hi = sb("s_hi", [P, P], I32)
        lo_f = sb("lo_f", [P, P])
        hi_f = sb("hi_f", [P, P])
        NR = 4
        one_lo = [sb(f"one_lo{i}", [P, 8, P], BF16) for i in range(2)]
        one_hi = [sb(f"one_hi{i}", [P, 8, HI], BF16) for i in range(2)]
        zeros = sb("zeros", [P, P], BF16)
        t_ps = ctx.enter_context(nc.psum_tensor("el_tps", [P, 512], F32))
        d_ps = ctx.enter_context(nc.psum_tensor("el_dps", [P, 512], F32))
        base_in, base_ok, rows_in, rows_f, tr_done, lists_ok, idx_ok, lists_out, onehots, hist, local_ok, zero_ok, taken, deg_ok = (
            sem(k) for k in ("base_in", "base_ok", "rows_in", "rows_f", "transposed", "lists_ok", "idx_ok", "lists_out",
                             "onehots", "hist", "local_ok", "zero_ok", "lists_taken", "deg_ok"))
        passed = sem("passed")
        G = P // 8
        with nc.Block() as block:
            @block.sync
            def _(sp):
                sp.dma_start(base_sb[0:1, :], dst_d.rearrange("(c e) -> e c", e=CHUNK)[0:1, :],
                             allow_slow_non_contiguous=True).then_inc(base_in, 16)
                for j in range(TILES):
                    sp.dma_start(base_col[j:P:TILES, :],
                                 dst_d.rearrange("(k c e) -> e c k", e=CHUNK, k=MAX_BLOCKS)[0],
                                 allow_slow_non_contiguous=True).then_inc(base_in, 16)
                with sp.Fori(0, blocks) as k:
                    sp.wait_ge(tr_done, k)
                    sp.wait_ge(local_ok, k)
                    sp.dma_start(srow[:, :], src_d.rearrange("(k t p) -> k t p", p=P, t=P)[bass.ds(k, 1)].rearrange(
                        "a t p -> (a t) p")).then_inc(rows_in, 16)
                    sp.dma_start(drow[:, :], dst_d.rearrange("(k t p) -> k t p", p=P, t=P)[bass.ds(k, 1)].rearrange(
                        "a t p -> (a t) p")).then_inc(rows_in, 16)
                    sp.wait_ge(local_ok, k + 1)
                    held(sp, passed)
                    sp.dma_start(local_d.rearrange("(k t p) -> k t p", p=P, t=P)[bass.ds(k, 1)].rearrange(
                        "a t p -> (a t) p"), local_bf[:, :]).then_inc(lists_out, 16)
                    sp.wait_ge(lists_ok, k + 1)
                    sp.dma_start(lists_d.rearrange("r p c -> p r c")[:, bass.ds(k * 16, 16), :],
                                 lists[:, :, :]).then_inc(lists_out, 16)
                    sp.wait_ge(lists_out, k * 32 + 32)
                    sp.sem_inc(taken, 1)

            @block.vector
            def _(dve):
                v = nc.vector
                v.memset(zeros[:, :], 0.0).then_inc(zero_ok, 1)
                dve.wait_ge(base_in, 16 * (TILES + 1))
                v.tensor_scalar(base_sb[:, :], base_sb[:, :], LAST_BASE, None, ALU.min)
                v.tensor_scalar(base_f[:, :], base_col[:, :], LAST_BASE, None, ALU.min).then_inc(base_ok, 1)
                dve.wait_ge(base_ok, 1)
                with dve.Fori(0, blocks) as k:
                    dve.wait_ge(rows_in, k * 32 + 32)
                    dve.wait_ge(taken, k)
                    dve.wait_ge(tr_done, k)
                    v.tensor_copy(srow_f[:, :], srow[:, :])
                    v.tensor_tensor(local_f[:, :], drow[:, :], base_f[:, bass.ds(k, 1)].broadcast_to([P, P]),
                                    ALU.subtract).then_inc(rows_f, 1)
                    dve.wait_ge(rows_f, k + 1)
                    v.tensor_copy(local_bf[:, :], local_f[:, :]).then_inc(local_ok, 1)
                    dve.wait_ge(tr_done, k + 1)
                    v.tensor_copy(lists[:, :, 0:8], t_ps[:, 0:P].rearrange("p (r j) -> p r j", j=8)).then_inc(idx_ok, 1)
                    v.tensor_copy(lists[:, :, 8:16].bitcast(F32),
                                  t_ps[:, P:2 * P].rearrange("p (r j) -> p r j", j=8)).then_inc(lists_ok, 1)
                    dve.wait_ge(idx_ok, k * 3 + 1)
                    v.tensor_scalar(s_lo[:, :].rearrange("p (r j) -> p r j", j=8), lists[:, :, 0:8], 127, None,
                                    ALU.bitwise_and)
                    v.tensor_scalar(s_hi[:, :].rearrange("p (r j) -> p r j", j=8), lists[:, :, 0:8], 7, None,
                                    ALU.logical_shift_right).then_inc(idx_ok, 1)
                    dve.wait_ge(idx_ok, k * 3 + 2)
                    v.tensor_copy(lo_f[:, :], s_lo[:, :])
                    v.tensor_copy(hi_f[:, :], s_hi[:, :]).then_inc(idx_ok, 1)
                    dve.wait_ge(idx_ok, k * 3 + 3)
                    for g in range(G):
                        if g >= 2:
                            dve.wait_ge(hist, k * G + (g - 1))
                        else:
                            dve.wait_ge(hist, k * G)
                        for j in range(8):
                            t = 8 * g + j
                            v.tensor_scalar(one_lo[g % 2][:, j, :], row_bf[:, :], lo_f[:, t:t + 1], None, ALU.is_equal)
                            ins = v.tensor_scalar(one_hi[g % 2][:, j, :], row_bf[:, 0:HI], hi_f[:, t:t + 1], None,
                                                  ALU.is_equal)
                        ins.then_inc(onehots, 1)
                dve.wait_ge(deg_ok, 1)
                v.tensor_copy(deg[:, :], d_ps[:, 0:HI]).then_inc(zero_ok, 1)
                dve.wait_ge(zero_ok, 2)

            @block.tensor
            def _(pe):
                pe.wait_ge(zero_ok, 1)
                nc.tensor.matmul(d_ps[:, 0:HI], zeros[:, :], zeros[:, 0:HI], start=True, stop=False, skip_group_check=True)
                with pe.Fori(0, blocks) as k:
                    pe.wait_ge(rows_f, k + 1)
                    pe.wait_ge(idx_ok, k * 3)
                    pe.wait_ge(lists_ok, k)
                    nc.tensor.transpose(t_ps[:, 0:P], srow_f[:, :], ident[:, :])
                    nc.tensor.transpose(t_ps[:, P:2 * P], local_f[:, :], ident[:, :]).then_inc(tr_done, 1)
                    for g in range(G):
                        pe.wait_ge(onehots, k * G + (g + 1))
                        for j in range(8):
                            ins = nc.tensor.matmul(d_ps[:, 0:HI], one_lo[g % 2][:, j, :], one_hi[g % 2][:, j, :],
                                                   start=False, stop=False, skip_group_check=True)
                        ins.then_inc(hist, 1)
                nc.tensor.matmul(d_ps[:, 0:HI], zeros[:, :], zeros[:, 0:HI], start=False, stop=True,
                                 skip_group_check=True).then_inc(deg_ok, 1)


def norm_rows(nc, dve_step, act_step, h, t_in, sq, red, rinv, eps_c, n):
    v = nc.vector
    bc = lambda a: a.rearrange("p (r j) -> p r j", j=1).broadcast_to([P, n, X_DIM])
    dve_step(v.tensor_reduce(red, t_in, AX_X, ALU.add))
    dve_step(v.tensor_scalar(red, red, 1.0 / X_DIM, None, ALU.mult))
    dve_step(v.tensor_tensor(h, t_in, bc(red), ALU.subtract))
    dve_step(v.tensor_tensor(sq, h, h, ALU.mult))
    dve_step(v.tensor_reduce(red, sq, AX_X, ALU.add))
    act_step(lambda: nc.scalar.activation(rinv, red, ACT.Sqrt, bias=eps_c[:, 0:1], scale=1.0 / X_DIM))
    dve_step(v.reciprocal(rinv, rinv))
    dve_step(v.tensor_tensor(h, h, bc(rinv), ALU.mult))
    dve_step(v.tensor_scalar(h, h, 0.0, None, ALU.max))


def scaled_senders(nc, x, x1, deg, xg_d, eps_c):
    with ExitStack() as ctx:
        def sb(name, shape, dt=F32):
            return ctx.enter_context(nc.sbuf_tensor("ss_" + name, shape, dt))

        sem = ctx.enter_context(semaphores(nc, "ss_"))

        h, sq = sb("h", [P, HI, X_DIM]), sb("sq", [P, HI, X_DIM])
        red, rinv, rs = sb("red", [P, HI]), sb("rinv", [P, HI]), sb("rs", [P, HI])
        rows = sb("rows", [P, HI, 32])
        x_in, dstep, astep, zeroed, out_done = (sem(k) for k in ("x_in", "dve_step", "act_step", "zeroed", "rows_out"))
        nd, na = [0], [0]
        jobs = []
        full = N_NODES // P
        rest = N_NODES - full * P
        with nc.Block() as block:
            @block.gpsimd
            def _(pool):
                nc.gpsimd.memset(x1[:, full:, :], 0.0).then_inc(zeroed, 1)
                nc.gpsimd.memset(rows[:, :, X_DIM:], 0.0).then_inc(zeroed, 1)

            @block.sync
            def _(sp):
                sp.dma_start(x1[:, 0:full, :], x[0:full * P, :].rearrange("(k p) c -> p k c", p=P)).then_inc(x_in, 16)
                sp.wait_ge(zeroed, 1)
                sp.dma_start(x1[0:rest, full, :], x[full * P:, :]).then_inc(x_in, 16)
                sp.wait_ge(out_done, 1)
                sp.dma_start(xg_d.rearrange("(k p) c -> p k c", p=P), rows[:, :, :]).then_inc(x_in, 16)
                sp.wait_ge(x_in, 48)

            @block.vector
            def _(dve):
                v = nc.vector

                def dve_step(ins):
                    nd[0] += 1
                    ins.then_inc(dstep, 1)
                    dve.wait_ge(dstep, nd[0])

                def act_step(ins):
                    na[0] += 1
                    jobs.append((nd[0], ins))
                    dve.wait_ge(astep, na[0])

                dve.wait_ge(x_in, 32)
                dve.wait_ge(zeroed, 2)
                norm_rows(nc, dve_step, act_step, h[:, :, :], x1[:, :, :], sq[:, :, :], red[:, :], rinv[:, :], eps_c, HI)
                dve_step(v.tensor_scalar(rs[:, :], deg[:, :], 1.0, None, ALU.max))
                act_step(lambda: nc.scalar.activation(rs[:, :], rs[:, :], ACT.Sqrt))
                dve_step(v.reciprocal(rs[:, :], rs[:, :]))
                dve_step(v.memset(rows[:, :, X_DIM:X_DIM + 1], 1.0))
                v.tensor_tensor(rows[:, :, 0:X_DIM], h[:, :, :],
                                rs[:, :].rearrange("p (r j) -> p r j", j=1).broadcast_to([P, HI, X_DIM]),
                                ALU.mult).then_inc(out_done, 1)

            @block.scalar
            def _(act):
                for at, ins in jobs:
                    act.wait_ge(dstep, at)
                    ins().then_inc(astep, 1)


def first_layer(nc, lists_d, attr_d, xg_d, edge_d, base_sb, agg, enc_w0, w_mid, mean_w, ident, row_f, vecs, eps_c, pairs):
    with ExitStack() as ctx:
        def sb(name, shape, dt=F32):
            return ctx.enter_context(nc.sbuf_tensor("fl_" + name, shape, dt))

        def two(name, shape, dt=F32):
            return [sb(f"{name}{i}", shape, dt) for i in range(2)]

        def ps(name):
            return ctx.enter_context(nc.psum_tensor("fl_" + name, [P, 512], F32))

        sem = ctx.enter_context(semaphores(nc, "fl_"))

        lst = two("lst", [P, 16], I32)
        attr = two("attr", [P, 8, E_DIM])
        attr_t = sb("attr_t", [64, P])
        g = two("g", [P, 8, 32])
        ohb = two("ohb", [P, 8, WIN])
        h, sq, lnv, t = (sb(k, [P, CHUNK]) for k in ("h", "sq", "lnv", "t"))
        rstd = two("rstd", [P, CHUNK])
        e = two("e", [P, CHUNK])
        at_ps, h_ps, var_ps, agg_ps = ps("atps"), ps("hps"), ps("varps"), ps("aggps")
        y_ps = [ps("yps0"), ps("yps1")]
        list_in, attr_in, g_in, e_out = ([sem(f"{k}{i}") for i in range(2)] for k in ("list_in", "attr_in", "g_in", "e_out"))
        passed = sem("passed")
        zeroed, turned, turned_sb, pre, h_ok, y_ok, sq_ok, var_ok, ln_ok, r_ok, t_ok, e_ok, oh_ok, sum_ok, added = (
            sem(k) for k in ("zeroed", "turned", "turned_sb", "pre", "h_ok", "y_ok", "sq_ok", "var_ok", "ln_ok", "r_ok",
                             "t_ok", "e_ok", "oh_ok", "sum_ok", "added"))
        attr_v = attr_d.rearrange("(r j p) c -> r p j c", p=P, j=8)
        col = lambda what: vecs[:, vcol("edge_enc", what):vcol("edge_enc", what) + 1]
        last = Slot(pairs, 0)
        with nc.Block() as block:
            @block.sync
            def _(sp):
                def store(n):
                    if n.exists():
                        wait(sp, e_ok, n)
                        sp.dma_start(edge_d[bass.ds(n.n, 1)].rearrange("a p c -> (a p) c"), e[n.b][:, :]).then_inc(e_out[n.b], 16)

                def body(n):
                    wait(sp, oh_ok, n.back(2))
                    landed(sp, g_in, n.back(2), 128)
                    sp.dma_start(lst[n.b][:, :], lists_d[bass.ds(n.n, 1)].rearrange("a p c -> (a p) c")).then_inc(list_in[n.b], 16)
                    wait(sp, turned, n.back(2))
                    sp.dma_start(attr[n.b][:, :, :], attr_v[bass.ds(n.n, 1)].rearrange("a p j c -> (a p) j c")).then_inc(attr_in[n.b], 16)
                    store(n.back(2))

                rounds(sp, body, pairs)
                store(last.back(2))
                store(last.back(1))
                landed(sp, e_out, last.back(2))
                landed(sp, e_out, last.back(1))

            @block.gpsimd
            def _(pool):
                def body(n):
                    landed(pool, list_in, n)
                    wait(pool, sum_ok, n.back(2))
                    held(pool, passed)
                    for j in range(8):
                        pool.indirect_dma_start(
                            out=g[n.b][:, j, :], out_offset=None, in_=xg_d,
                            in_offset=bass.IndirectOffsetOnAxis(ap=lst[n.b][:, j:j + 1].bitcast(U32), axis=0),
                        ).then_inc(g_in[n.b], 16)

                rounds(pool, body, pairs)

            @block.tensor
            def _(pe):
                def sums(n):
                    if not n.exists():
                        return
                    landed(pe, g_in, n, 128)
                    wait(pe, oh_ok, n)
                    wait(pe, added, n.back(1))
                    for c in range(2):
                        for i in range(TILES):
                            j = c * TILES + i
                            ins = nc.tensor.matmul(agg_ps[64 * c:64 * c + 32, 0:WIN], g[n.b][:, j, :], ohb[n.b][:, j, :],
                                                   start=i == 0, stop=i == TILES - 1)
                    ins.then_inc(sum_ok, 1)

                def body(n):
                    landed(pe, attr_in, n)
                    wait(pe, turned_sb, n.back(1))
                    held(pe, passed)
                    nc.tensor.transpose(at_ps[0:64, 0:P], attr[n.b][:, :, :].rearrange("p j c -> p (j c)"),
                                        ident[:, :]).then_inc(turned, 1)
                    sums(n.back(1))
                    wait(pe, turned_sb, n)
                    wait(pe, h_ok, n.back(1))
                    for i in range(TILES):
                        ins = nc.tensor.matmul(h_ps[:, P * i:P * i + P], enc_w0[:, i, :], attr_t[:, :], start=True, stop=True)
                    ins.then_inc(pre, 1)
                    wait(pe, h_ok, n)
                    wait(pe, t_ok, n.back(2))
                    nc.tensor.matmul(y_ps[n.b][:, :], w_mid[:, :], h[:, :], start=True, stop=True).then_inc(y_ok, 1)
                    wait(pe, sq_ok, n)
                    wait(pe, ln_ok, n.back(1))
                    nc.tensor.matmul(var_ps[:, :], mean_w[:, :], sq[:, :], start=True, stop=True).then_inc(var_ok, 1)

                rounds(pe, body, pairs)
                sums(last.back(1))

            @block.scalar
            def _(act):
                def body(n):
                    wait(act, pre, n)
                    wait(act, y_ok, n.back(1))
                    nc.scalar.activation(h[:, :], h_ps[:, :], ACT.Silu, bias=col("b0")).then_inc(h_ok, 1)
                    wait(act, y_ok, n)
                    wait(act, var_ok, n.back(1))
                    nc.scalar.activation(sq[:, :], y_ps[n.b][:, :], ACT.Square, bias=col("b1")).then_inc(sq_ok, 1)
                    wait(act, var_ok, n)
                    wait(act, r_ok, n.back(1))
                    nc.scalar.activation(lnv[:, :], var_ps[:, :], ACT.Ln, bias=eps_c[:, 0:1]).then_inc(ln_ok, 1)
                    wait(act, ln_ok, n)
                    wait(act, t_ok, n.back(2))
                    nc.scalar.activation(rstd[n.b][:, :], lnv[:, :], ACT.Exp, scale=-0.5).then_inc(r_ok, 1)

                rounds(act, body, pairs)

            @block.vector
            def _(dve):
                v = nc.vector

                def finish(n):
                    if not n.exists():
                        return
                    wait(dve, r_ok, n)
                    wait(dve, e_ok, n.back(1))
                    v.scalar_tensor_tensor(t[:, :], y_ps[n.b][:, :], col("b1"), rstd[n.b][:, :], ALU.add, ALU.mult).then_inc(t_ok, 1)
                    wait(dve, t_ok, n)
                    landed(dve, e_out, n.back(2))
                    v.tensor_scalar(e[n.b][:, :], t[:, :], col("g"), col("beta"), ALU.mult, ALU.add).then_inc(e_ok, 1)

                def add_sums(n):
                    if not n.exists():
                        return
                    at = [dve.value_load(base_sb[0:1, bass.ds(n.n * 2 + c, 1)], min_val=0, max_val=LAST_BASE) for c in range(2)]
                    wait(dve, sum_ok, n)
                    wait(dve, added, n.back(1))
                    for c in range(2):
                        a = agg[64 * c:64 * c + 32, bass.ds(at[c], WIN)]
                        ins = v.tensor_tensor(a, a, agg_ps[64 * c:64 * c + 32, 0:WIN], ALU.add)
                    ins.then_inc(added, 1)

                def body(n):
                    wait(dve, turned, n)
                    wait(dve, pre, n.back(1))
                    v.tensor_copy(attr_t[:, :], at_ps[0:64, 0:P]).then_inc(turned_sb, 1)
                    landed(dve, list_in, n)
                    wait(dve, sum_ok, n.back(2))
                    for j in range(8):
                        ins = v.tensor_scalar(ohb[n.b][:, j, :], row_f[:, 0:WIN], lst[n.b][:, 8 + j:9 + j].bitcast(F32), None,
                                              ALU.is_equal)
                    ins.then_inc(oh_ok, 1)
                    finish(n.back(1))
                    add_sums(n.back(1))

                v.memset(agg[:, :], 0.0).then_inc(zeroed, 1)
                dve.wait_ge(zeroed, 1)
                rounds(dve, body, pairs)
                finish(last.back(1))
                add_sums(last.back(1))


def edge_step(nc, lists_d, local_d, edge_d, ps_d, pr_d, base_sb, agg, w_in, w_mid, mean_w, ident, row_f, part64,
              vecs, eps_c, mlp, keep, pairs):
    with ExitStack() as ctx:
        tag = mlp + "_"

        def sb(name, shape, dt=F32):
            return ctx.enter_context(nc.sbuf_tensor(tag + name, shape, dt))

        def two(name, shape, dt=F32):
            return [sb(f"{name}{i}", shape, dt) for i in range(2)]

        def ps(name):
            return ctx.enter_context(nc.psum_tensor(tag + name, [P, 512], F32))

        sem = ctx.enter_context(semaphores(nc, tag))

        lst = two("lst", [P, 16], I32)
        dlb = two("dlb", [P, CHUNK], BF16)
        win = two("win", [P, P])
        g = two("g", [P, TILES, P])
        oha = two("oha", [P, CHUNK])
        ohb = two("ohb", [P, 8, WIN])
        e = two("e", [P, CHUNK])
        eb = two("eb", [P, CHUNK])
        h, sq, lnv, t = (sb(k, [P, CHUNK]) for k in ("h", "sq", "lnv", "t"))
        rstd = two("rstd", [P, CHUNK])
        new = two("new", [P, CHUNK])
        new_t = sb("new_t", [P, TILES, P])
        h_ps = [ps("hps0"), ps("hps1")]
        y_ps = [ps("yps0"), ps("yps1")]
        var_ps, t_ps, agg_ps = ps("varps"), ps("tps"), ps("aggps")
        list_in, dlb_in, win_in, g_in, e_in, e_out = (
            [sem(f"{k}{i}") for i in range(2)] for k in ("list_in", "dlb_in", "win_in", "g_in", "e_in", "e_out"))
        passed = sem("passed")
        zeroed, pre, h_ok, y_ok, sq_ok, var_ok, ln_ok, r_ok, t_ok, new_ok, eb_ok, oha_ok, ohb_ok, turned, turned_sb, sum_ok, added = (
            sem(k) for k in ("zeroed", "pre", "h_ok", "y_ok", "sq_ok", "var_ok", "ln_ok", "r_ok", "t_ok", "new_ok", "eb_ok",
                             "oha_ok", "ohb_ok", "turned", "turned_sb", "sum_ok", "added"))
        local_v = local_d.rearrange("(r c e) -> r c e", e=CHUNK, c=2)
        col = lambda what: vecs[:, vcol(mlp, what):vcol(mlp, what) + 1]
        last = Slot(pairs, 0)
        with nc.Block() as block:
            @block.sync
            def _(sp):
                def store(n):
                    if keep and n.exists():
                        wait(sp, new_ok, n)
                        sp.dma_start(edge_d[bass.ds(n.n, 1)].rearrange("a p c -> (a p) c"), new[n.b][:, :]).then_inc(e_out[n.b], 16)

                def body(n):
                    wait(sp, ohb_ok, n.back(2))
                    landed(sp, g_in, n.back(2), 128)
                    sp.dma_start(lst[n.b][:, :], lists_d[bass.ds(n.n, 1)].rearrange("a p c -> (a p) c")).then_inc(list_in[n.b], 16)
                    wait(sp, oha_ok, n.back(2))
                    for c in range(2):
                        sp.dma_start(dlb[n.b][64 * c:64 * c + 64, :],
                                     local_v[bass.ds(n.n, 1), c, :].broadcast_to([64, CHUNK])).then_inc(dlb_in[n.b], 16)
                    at = [sp.value_load(base_sb[0:1, bass.ds(n.n * 2 + c, 1)], min_val=0, max_val=LAST_BASE) for c in range(2)]
                    wait(sp, pre, n.back(2))
                    wait(sp, eb_ok, n.back(2))
                    sp.dma_start(e[n.b][:, :], edge_d[bass.ds(n.n, 1)].rearrange("a p c -> (a p) c")).then_inc(e_in[n.b], 16)
                    for c in range(2):
                        q = slice(64 * c, 64 * c + 64)
                        sp.dma_start(win[n.b][q, q], pr_d[bass.ds(at[c], WIN), :]).then_inc(win_in[n.b], 16)
                    store(n.back(2))

                sp.wait_ge(zeroed, 1)
                rounds(sp, body, pairs)
                store(last.back(2))
                store(last.back(1))
                if keep:
                    landed(sp, e_out, last.back(2))
                    landed(sp, e_out, last.back(1))

            @block.gpsimd
            def _(pool):
                def body(n):
                    landed(pool, list_in, n)
                    wait(pool, pre, n.back(2))
                    held(pool, passed)
                    for j in range(8):
                        c, i = j // TILES, j % TILES
                        pool.indirect_dma_start(
                            out=g[n.b][:, i, 64 * c:64 * c + 64], out_offset=None, in_=ps_d,
                            in_offset=bass.IndirectOffsetOnAxis(ap=lst[n.b][:, j:j + 1].bitcast(U32), axis=0),
                        ).then_inc(g_in[n.b], 16)

                rounds(pool, body, pairs)

            @block.tensor
            def _(pe):
                def turn(n):
                    if not n.exists():
                        return
                    wait(pe, new_ok, n)
                    wait(pe, turned_sb, n.back(1))
                    for i in range(TILES):
                        ins = nc.tensor.transpose(t_ps[:, P * i:P * i + P], new[n.b][:, P * i:P * i + P], ident[:, :])
                    ins.then_inc(turned, 1)

                def sums(n):
                    if not n.exists():
                        return
                    wait(pe, turned_sb, n)
                    wait(pe, ohb_ok, n)
                    wait(pe, added, n.back(1))
                    for c in range(2):
                        for i in range(TILES):
                            ins = nc.tensor.matmul(agg_ps[64 * c:64 * c + 64, 0:WIN], new_t[:, i, 64 * c:64 * c + 64],
                                                   ohb[n.b][:, TILES * c + i, :], start=i == 0, stop=i == TILES - 1)
                    ins.then_inc(sum_ok, 1)

                def body(n):
                    wait(pe, h_ok, n.back(2))
                    landed(pe, e_in, n)
                    nc.tensor.matmul(h_ps[n.b][:, :], w_in[:, :], e[n.b][:, :], start=True, stop=False)
                    landed(pe, win_in, n, 32)
                    wait(pe, oha_ok, n)
                    nc.tensor.matmul(h_ps[n.b][:, :], win[n.b][:, :], oha[n.b][:, :], start=False, stop=False)
                    landed(pe, g_in, n, 128)
                    for i in range(TILES):
                        ins = nc.tensor.matmul(h_ps[n.b][:, P * i:P * i + P], g[n.b][:, i, :], ident[:, :], start=False,
                                               stop=i == TILES - 1)
                    ins.then_inc(pre, 1)
                    turn(n.back(1))
                    wait(pe, h_ok, n)
                    wait(pe, t_ok, n.back(2))
                    nc.tensor.matmul(y_ps[n.b][:, :], w_mid[:, :], h[:, :], start=True, stop=True).then_inc(y_ok, 1)
                    sums(n.back(1))
                    wait(pe, sq_ok, n)
                    wait(pe, ln_ok, n.back(1))
                    nc.tensor.matmul(var_ps[:, :], mean_w[:, :], sq[:, :], start=True, stop=True).then_inc(var_ok, 1)

                rounds(pe, body, pairs)
                turn(last.back(1))
                sums(last.back(1))

            @block.scalar
            def _(act):
                def body(n):
                    landed(act, e_in, n)
                    wait(act, new_ok, n.back(2))
                    nc.scalar.activation(eb[n.b][:, :], e[n.b][:, :], ACT.Identity, bias=col("beta")).then_inc(eb_ok, 1)
                    wait(act, pre, n)
                    wait(act, y_ok, n.back(1))
                    nc.scalar.activation(h[:, :], h_ps[n.b][:, :], ACT.Silu, bias=col("b0")).then_inc(h_ok, 1)
                    wait(act, y_ok, n)
                    wait(act, var_ok, n.back(1))
                    nc.scalar.activation(sq[:, :], y_ps[n.b][:, :], ACT.Square, bias=col("b1")).then_inc(sq_ok, 1)
                    wait(act, var_ok, n)
                    wait(act, r_ok, n.back(1))
                    nc.scalar.activation(lnv[:, :], var_ps[:, :], ACT.Ln, bias=eps_c[:, 0:1]).then_inc(ln_ok, 1)
                    wait(act, ln_ok, n)
                    wait(act, t_ok, n.back(2))
                    nc.scalar.activation(rstd[n.b][:, :], lnv[:, :], ACT.Exp, scale=-0.5).then_inc(r_ok, 1)

                rounds(act, body, pairs)

            @block.vector
            def _(dve):
                v = nc.vector

                def finish(n):
                    if not n.exists():
                        return
                    wait(dve, r_ok, n)
                    wait(dve, new_ok, n.back(1))
                    v.scalar_tensor_tensor(t[:, :], y_ps[n.b][:, :], col("b1"), rstd[n.b][:, :], ALU.add, ALU.mult).then_inc(t_ok, 1)
                    wait(dve, t_ok, n)
                    wait(dve, eb_ok, n)
                    wait(dve, turned, n.back(2))
                    if keep:
                        landed(dve, e_out, n.back(2))
                    v.scalar_tensor_tensor(new[n.b][:, :], t[:, :], col("g"), eb[n.b][:, :], ALU.mult, ALU.add).then_inc(new_ok, 1)

                def rows(n):
                    if not n.exists():
                        return
                    wait(dve, turned, n)
                    wait(dve, sum_ok, n.back(1))
                    v.tensor_copy(new_t[:, :, :], t_ps[:, :].rearrange("p (i q) -> p i q", q=P)).then_inc(turned_sb, 1)

                def add_sums(n):
                    if not n.exists():
                        return
                    at = [dve.value_load(base_sb[0:1, bass.ds(n.n * 2 + c, 1)], min_val=0, max_val=LAST_BASE) for c in range(2)]
                    wait(dve, sum_ok, n)
                    wait(dve, added, n.back(1))
                    for c in range(2):
                        a = agg[64 * c:64 * c + 64, bass.ds(at[c], WIN)]
                        ins = v.tensor_tensor(a, a, agg_ps[64 * c:64 * c + 64, 0:WIN], ALU.add)
                    ins.then_inc(added, 1)

                def body(n):
                    landed(dve, dlb_in, n, 32)
                    wait(dve, pre, n.back(2))
                    v.tensor_scalar(oha[n.b][:, :], dlb[n.b][:, :], part64[:, 0:1], None, ALU.is_equal).then_inc(oha_ok, 1)
                    landed(dve, list_in, n)
                    wait(dve, sum_ok, n.back(2))
                    for j in range(8):
                        ins = v.tensor_scalar(ohb[n.b][:, j, :], row_f[:, 0:WIN], lst[n.b][:, 8 + j:9 + j].bitcast(F32), None,
                                              ALU.is_equal)
                    ins.then_inc(ohb_ok, 1)
                    finish(n.back(1))
                    rows(n.back(1))
                    add_sums(n.back(1))

                for b in range(2):
                    v.memset(win[b][:, :], 0.0)
                v.memset(agg[:, :], 0.0).then_inc(zeroed, 1)
                dve.wait_ge(zeroed, 1)
                rounds(dve, body, pairs)
                finish(last.back(1))
                rows(last.back(1))
                add_sums(last.back(1))


def node_phase(nc, agg, node, x1, vecs, mean_w, ident, eps_c, ps_d, pr_d, mlp, w_in, w_mid, proj, sum_ab=None, w_agg=None,
               dec=None):
    first = sum_ab is not None
    with ExitStack() as ctx:
        tag = mlp + "_"

        def sb(name, shape, dt=F32):
            return ctx.enter_context(nc.sbuf_tensor(tag + name, shape, dt))

        def ps(name):
            return ctx.enter_context(nc.psum_tensor(tag + name, [P, 512], F32))

        sem = ctx.enter_context(semaphores(nc, tag))

        col = lambda what: vecs[:, vcol(mlp, what):vcol(mlp, what) + 1]
        h, sq, lnv, rstd, t, hd = (sb(k, [P, 512]) for k in ("h", "sq", "lnv", "rstd", "t", "hd"))
        stage = [sb(f"stage{i}", [P, 4, P]) for i in range(2)]
        res = [sb(f"res{i}", [P, 4, OUT_DIM]) for i in range(2)]
        h_ps, y_ps, var_ps = ps("hps"), ps("yps"), ps("varps")
        o_ps = [ps("ops0"), ps("ops1")]
        a_ps = [ps("aps0"), ps("aps1")]
        a_ok, a_taken, dstep, astep, norm_ok, turned, turned_sb, pre, h_ok, y_ok, sq_ok, var_ok, ln_ok, r_ok, t_ok, nb_ok, n_ok, o_ok, st_ok, d_ok, hd_ok = (
            sem(k) for k in ("a_ok", "a_taken", "dve_step", "act_step", "norm_ok", "turned", "turned_sb", "pre", "h_ok",
                             "y_ok", "sq_ok", "var_ok", "ln_ok", "r_ok", "t_ok", "nb_ok", "n_ok", "o_ok", "st_ok", "d_ok", "hd_ok"))
        st_out = [sem("st_out0"), sem("st_out1")]
        if first:
            hn = sb("hn", [P, NT * 4, 2, X_DIM])
            ag = sb("ag", [P, HI, 32])
            sqn = sb("sqn", [P, HI, X_DIM])
            red, rinv, din = sb("red", [P, HI]), sb("rinv", [P, HI]), sb("din", [P, HI])
            ht = sb("ht", [32, 512])
        nd, na, jobs = [0], [0], []

        def stores(q, k):
            if not dec:
                return 2 * (k + 1)
            rows = [max(0, min(512, N_NODES - HALF * q - 512 * i)) for i in range(k + 1)]
            return sum((r >= P) + (r % P > 0) for r in rows)

        AG = HI // 8
        with nc.Block() as block:
            @block.tensor
            def _(pe):
                if first:
                    for k in range(AG):
                        if k >= 2:
                            pe.wait_ge(a_taken, k - 1)
                        for i in range(8):
                            hi = 8 * k + i
                            ins = nc.tensor.matmul(a_ps[k % 2][:, 32 * i:32 * i + 32], agg[:, P * hi:P * hi + P],
                                                   sum_ab[:, :], start=True, stop=True)
                        ins.then_inc(a_ok, 1)
                    pe.wait_ge(norm_ok, 1)
                for k in range(NT):
                    c = slice(512 * k, 512 * k + 512)
                    if first:
                        if k:
                            pe.wait_ge(turned_sb, k)
                        for q in range(4):
                            ins = nc.tensor.transpose(a_ps[0][0:32, P * q:P * q + P],
                                                      hn[:, 4 * k + q, :, :].rearrange("p a c -> p (a c)"), ident[:, :])
                        ins.then_inc(turned, 1)
                        pe.wait_ge(turned_sb, k + 1)
                        if k:
                            pe.wait_ge(h_ok, k)
                        nc.tensor.matmul(h_ps[:, :], w_in[:, :], ht[:, :], start=True, stop=True).then_inc(pre, 1)
                    else:
                        if k:
                            pe.wait_ge(h_ok, k)
                        nc.tensor.matmul(h_ps[:, :], w_in[:, :], node[:, c], start=True, stop=False)
                        for q in range(2):
                            ins = nc.tensor.matmul(h_ps[64 * q:64 * q + 64, :], w_agg[:, :],
                                                   agg[:, HALF * q + 512 * k:HALF * q + 512 * k + 512], start=False, stop=True)
                        ins.then_inc(pre, 1)
                    pe.wait_ge(h_ok, k + 1)
                    if k:
                        pe.wait_ge(t_ok, k)
                    nc.tensor.matmul(y_ps[:, :], w_mid[:, :], h[:, :], start=True, stop=True).then_inc(y_ok, 1)
                    pe.wait_ge(sq_ok, k + 1)
                    if k:
                        pe.wait_ge(ln_ok, k)
                    nc.tensor.matmul(var_ps[:, :], mean_w[:, :], sq[:, :], start=True, stop=True).then_inc(var_ok, 1)
                    pe.wait_ge(n_ok, k + 1)
                    if dec:
                        if k:
                            pe.wait_ge(hd_ok, k)
                        nc.tensor.matmul(a_ps[0][:, :], dec[0][:, :], node[:, c], start=True, stop=True).then_inc(d_ok, 1)
                        pe.wait_ge(hd_ok, k + 1)
                    for q in range(2):
                        if k:
                            pe.wait_ge(st_ok, 2 * (k - 1) + q + 1)
                        r = slice(64 * q, 64 * q + 64)
                        for i in range(4):
                            if dec:
                                ins = nc.tensor.matmul(o_ps[q][:, OUT_DIM * i:OUT_DIM * i + OUT_DIM], hd[r, P * i:P * i + P],
                                                       dec[1][r, :], start=True, stop=True)
                            else:
                                ins = nc.tensor.matmul(o_ps[q][:, P * i:P * i + P], node[r, 512 * k + P * i:512 * k + P * i + P],
                                                       proj[r, :], start=True, stop=True)
                        ins.then_inc(o_ok, 1)

            @block.vector
            def _(dve):
                v = nc.vector

                def dve_step(ins):
                    nd[0] += 1
                    ins.then_inc(dstep, 1)
                    dve.wait_ge(dstep, nd[0])

                def act_step(ins):
                    na[0] += 1
                    jobs.append((nd[0], ins))
                    dve.wait_ge(astep, na[0])

                if first:
                    for k in range(AG):
                        dve.wait_ge(a_ok, k + 1)
                        v.tensor_copy(ag[:, 8 * k:8 * k + 8, :],
                                      a_ps[k % 2][:, 0:256].rearrange("p (i c) -> p i c", c=32)).then_inc(a_taken, 1)
                    dve.wait_ge(a_taken, AG)
                    dve_step(v.tensor_scalar(din[:, :], ag[:, :, X_DIM:X_DIM + 1].rearrange("p r j -> p (r j)"), 1.0, None, ALU.max))
                    act_step(lambda: nc.scalar.activation(din[:, :], din[:, :], ACT.Sqrt))
                    dve_step(v.reciprocal(din[:, :], din[:, :]))
                    dve_step(v.tensor_tensor(ag[:, :, 0:X_DIM], ag[:, :, 0:X_DIM],
                                             din[:, :].rearrange("p (r j) -> p r j", j=1).broadcast_to([P, HI, X_DIM]), ALU.mult))
                    dve_step(v.tensor_tensor(x1[:, :, :], x1[:, :, :], ag[:, :, 0:X_DIM], ALU.add))
                    norm_rows(nc, dve_step, act_step, ag[:, :, 0:X_DIM], x1[:, :, :], sqn[:, :, :], red[:, :], rinv[:, :], eps_c, HI)
                    for q in range(2):
                        ins = v.tensor_copy(hn[:, :, q, :], ag[:, 52 * q:52 * q + 52, 0:X_DIM])
                    ins.then_inc(norm_ok, 1)
                for k in range(NT):
                    c = slice(512 * k, 512 * k + 512)
                    if first:
                        dve.wait_ge(turned, k + 1)
                        if k:
                            dve.wait_ge(pre, k)
                        v.tensor_copy(ht[:, :], a_ps[0][0:32, :]).then_inc(turned_sb, 1)
                    dve.wait_ge(r_ok, k + 1)
                    v.scalar_tensor_tensor(t[:, :], y_ps[:, :], col("b1"), rstd[:, :], ALU.add, ALU.mult).then_inc(t_ok, 1)
                    dve.wait_ge(t_ok, k + 1)
                    if first:
                        v.tensor_scalar(node[:, c], t[:, :], col("g"), col("beta"), ALU.mult, ALU.add).then_inc(n_ok, 1)
                    else:
                        dve.wait_ge(nb_ok, k + 1)
                        v.scalar_tensor_tensor(node[:, c], t[:, :], col("g"), node[:, c], ALU.mult, ALU.add).then_inc(n_ok, 1)
                    for q in range(2):
                        dve.wait_ge(o_ok, 2 * k + q + 1)
                        if k:
                            dve.wait_ge(st_out[q], 16 * stores(q, k - 1))
                        if dec:
                            blk = 52 * q + 4 * k
                            dve_step(v.tensor_tensor(res[q][:, :, :], o_ps[q][:, 0:4 * OUT_DIM].rearrange("p (i c) -> p i c", c=OUT_DIM),
                                                     x1[:, blk:blk + 4, :], ALU.add))
                            for i in range(4):
                                ins = v.tensor_tensor(res[q][:, i, :], res[q][:, i, :], dec[2][:, :], ALU.add)
                            ins.then_inc(st_ok, 1)
                        else:
                            v.tensor_copy(stage[q][:, :, :], o_ps[q][:, :].rearrange("p (i c) -> p i c", c=P)).then_inc(st_ok, 1)
                if not dec:
                    dve.wait_ge(st_ok, 2 * NT)

            @block.scalar
            def _(act):
                for at, ins in jobs:
                    act.wait_ge(dstep, at)
                    ins().then_inc(astep, 1)
                for k in range(NT):
                    c = slice(512 * k, 512 * k + 512)
                    act.wait_ge(pre, k + 1)
                    if k:
                        act.wait_ge(y_ok, k)
                    nc.scalar.activation(h[:, :], h_ps[:, :], ACT.Silu, bias=col("b0")).then_inc(h_ok, 1)
                    if not first:
                        nc.scalar.activation(node[:, c], node[:, c], ACT.Identity, bias=col("beta")).then_inc(nb_ok, 1)
                    act.wait_ge(y_ok, k + 1)
                    if k:
                        act.wait_ge(var_ok, k)
                    nc.scalar.activation(sq[:, :], y_ps[:, :], ACT.Square, bias=col("b1")).then_inc(sq_ok, 1)
                    act.wait_ge(var_ok, k + 1)
                    if k:
                        act.wait_ge(r_ok, k)
                    nc.scalar.activation(lnv[:, :], var_ps[:, :], ACT.Ln, bias=eps_c[:, 0:1]).then_inc(ln_ok, 1)
                    act.wait_ge(ln_ok, k + 1)
                    if k:
                        act.wait_ge(t_ok, k)
                    nc.scalar.activation(rstd[:, :], lnv[:, :], ACT.Exp, scale=-0.5).then_inc(r_ok, 1)
                    if dec:
                        act.wait_ge(d_ok, k + 1)
                        if k:
                            act.wait_ge(o_ok, 2 * k)
                        nc.scalar.activation(hd[:, :], a_ps[0][:, :], ACT.Silu, bias=vecs[:, DEC_B0:DEC_B0 + 1]).then_inc(hd_ok, 1)

            @block.sync
            def _(sp):
                for k in range(NT):
                    for q in range(2):
                        sp.wait_ge(st_ok, 2 * k + q + 1)
                        r0 = HALF * q + 512 * k
                        if dec:
                            full = max(0, min(4, (N_NODES - r0) // P))
                            if full:
                                sp.dma_start(dec[3][r0:r0 + P * full, :].rearrange("(i p) c -> p i c", p=P),
                                             res[q][:, 0:full, :]).then_inc(st_out[q], 16)
                            rest = N_NODES - r0 - P * full
                            if full < 4 and 0 < rest < P:
                                sp.dma_start(dec[3][r0 + P * full:N_NODES, :], res[q][0:rest, full, :]).then_inc(st_out[q], 16)
                            continue
                        for i, table in enumerate((ps_d, pr_d)):
                            sp.dma_start(table[r0:r0 + 512, :].rearrange("(i p) c -> p i c", p=P),
                                         stage[q][:, :, D * i:D * i + D]).then_inc(st_out[q], 16)
                for q in range(2):
                    sp.wait_ge(st_out[q], 16 * stores(q, NT - 1))


_W = ["node_enc", "edge_enc", "edge_blk", "node_blk"]
_WNAMES = [f"{k}_{p}" for k in _W for p in ("w0", "b0", "w1", "b1", "g", "beta")] + ["dec_w0", "dec_b0", "dec_w1", "dec_b1"]
_INS = ["x", "src", "dst", "edge_attr_8"] + ["L1_gnn_" + k for k in _WNAMES]


def kernel(**inputs):
    import numpy as np
    import concourse.bacc as bacc
    from concourse.bass_utils import run_bass_kernel_spmd

    nc = bacc.Bacc("TRN2", target_bir_lowering=False, num_devices=1)
    arrays, aps = {}, {}
    for name in _INS:
        a = np.ascontiguousarray(inputs[name])
        arrays[f"in_{name}"] = a
        aps[name] = nc.dram_tensor(f"in_{name}", a.shape, mybir.dt.from_np(a.dtype), kind="ExternalInput").ap()
    out = nc.dram_tensor("out_nodes", (N_NODES, OUT_DIM), F32, kind="ExternalOutput").ap()
    gnn_kernel(nc, aps["x"], aps["src"], aps["dst"], aps["edge_attr_8"], {k: aps["L1_gnn_" + k] for k in _WNAMES}, out)
    r = run_bass_kernel_spmd(nc, [arrays], core_ids=[0])
    return r.results[0]["out_nodes"]
```

```python
from contextlib import ExitStack, contextmanager

import concourse.bass as bass
from concourse import mybir

ALU = mybir.AluOpType
ACT = mybir.ActivationFunctionType
AX_X = mybir.AxisListType.X
F32 = mybir.dt.float32
BF16 = mybir.dt.bfloat16
I32 = mybir.dt.int32
U32 = mybir.dt.uint32
P = 128

N_NODES, N_EDGES, X_DIM, E_DIM, D, OUT_DIM, STEPS = 12500, 400000, 16, 8, 64, 16, 2
TILES = 4
CHUNK = TILES * P
ROUND = 2 * CHUNK
WIN = 64
HALF = 6656
NODES = 2 * HALF
HI = NODES // P
NT = HALF // 512
PAD_NODE = N_NODES
PAD_DST = 20000
LAST_BASE = 12544
BLOCK_E = P * P
FAST_ROUNDS = 2 * -(-N_EDGES // (2 * ROUND))
FAST_BLOCKS = -(-FAST_ROUNDS * ROUND // BLOCK_E)
WINDOWS = -(-N_NODES // WIN)
SLOT_CHUNKS = -(-N_EDGES // CHUNK) + WINDOWS
MAX_BLOCKS = -(-SLOT_CHUNKS * CHUNK // BLOCK_E)
SLOTS = MAX_BLOCKS * BLOCK_E
MAX_ROUNDS = SLOTS // ROUND
EPS = 1e-5

VEC = ["edge_enc", "edge_blk0", "edge_blk1", "node_enc", "node_blk0", "node_blk1"]


def vcol(mlp, what):
    return 4 * VEC.index(mlp) + ["b0", "b1", "g", "beta"].index(what)


DEC_B0 = 4 * len(VEC)
NVEC = DEC_B0 + 1


@contextmanager
def semaphores(nc, tag):
    made = []

    def sem(name):
        made.append(nc.alloc_semaphore(name=tag + name))
        return made[-1]

    yield sem
    nc.clear_and_free_semaphores(made)
    nc.all_engine_barrier()


class Slot:

    def __init__(self, m, b):
        self.m, self.b = m, b

    def back(self, k):
        q = self.b - k
        return Slot(self.m + q // 2, q % 2)

    def exists(self):
        return not isinstance(self.m, int) or self.m >= 0

    @property
    def n(self):
        return self.m * 2 + self.b


def wait(eng, sem, slot, per=1):
    if slot.exists():
        eng.wait_ge(sem, slot.n * per + per)


def landed(eng, sems, slot, per=16):
    if slot.exists():
        eng.wait_ge(sems[slot.b], slot.m * per + per)


def held(eng, passed):
    eng.sem_inc(passed, 1)


def rounds(eng, body, pairs, first=1):
    for m in range(first):
        body(Slot(m, 0))
        body(Slot(m, 1))
    with eng.Fori(first, pairs) as m:
        body(Slot(m, 0))
        body(Slot(m, 1))


def gnn_kernel(nc, x, src, dst, edge_attr, w, out):
    with ExitStack() as ctx:
        def sb(name, shape, dt=F32):
            return ctx.enter_context(nc.sbuf_tensor(name, shape, dt))

        def dram(name, shape, dt=F32):
            return nc.dram_tensor(name, shape, dt, kind="Internal").ap()

        src_d = dram("src_slots", (SLOTS,), I32)
        dst_d = dram("dst_slots", (SLOTS,), I32)
        attr_d = dram("attr_slots", (SLOTS, E_DIM))
        local_d = dram("local_dst", (SLOTS,), BF16)
        lists_d = dram("tile_lists", (MAX_ROUNDS, P, 16), I32)
        xg_d = dram("sender_x", (NODES, 32))
        ps_d = dram("sender_part", (NODES, D))
        pr_d = dram("receiver_part", (NODES, D))
        edge_d = dram("edge_state", (MAX_ROUNDS, P, CHUNK))

        part_f = sb("part_f", [P, 1])
        part64 = sb("part64", [P, 1])
        row_f = sb("row_f", [P, P])
        row_bf = sb("row_bf", [P, P], BF16)
        ident = sb("ident", [P, P])
        mean_w = sb("mean_w", [P, P])
        sum_ab = sb("sum_ab", [P, 32])
        eps_c = sb("eps_c", [P, 1])
        vecs = sb("vecs", [P, NVEC])
        vmean = sb("vmean", [P, NVEC])
        dec_b1 = sb("dec_b1", [P, OUT_DIM])
        enc_w0 = sb("enc_w0", [64, TILES, P])
        nenc_w0 = sb("nenc_w0", [32, P])
        w1 = {k: sb("w1_" + k, [P, P]) for k in VEC}
        ew0 = [sb(f"ew0_{s}", [P, P]) for s in range(STEPS)]
        proj_w = [sb(f"proj_w{s}", [P, P]) for s in range(STEPS)]
        nw0 = [sb(f"nw0_{s}", [P, P]) for s in range(STEPS)]
        aw0 = [sb(f"aw0_{s}", [P, D]) for s in range(STEPS)]
        dec_w0 = sb("dec_w0", [P, P])
        dec_w1 = sb("dec_w1", [P, OUT_DIM])
        wmean = sb("wmean", [P, len(VEC)])
        agg = sb("agg", [P, NODES])
        node = sb("node", [P, HALF])
        x1 = sb("x1", [P, HI, X_DIM])
        base_sb = sb("base_sb", [1, 2 * MAX_ROUNDS], I32)
        deg = sb("deg", [P, HI])

        def halves(eng, dst_tile, ap, sem):
            eng.dma_start(dst_tile[0:64, 0:64], ap).then_inc(sem, 16)
            eng.dma_start(dst_tile[64:128, 64:128], ap).then_inc(sem, 16)
            return 2

        n_ld = [0]
        with ExitStack() as c1:
            sem = c1.enter_context(semaphores(nc, "set_"))
            s_zero, s_ld, s_io, s_c, s_vm, s_cp, s_pad = (sem(k) for k in (
                "zeroed", "weights_landed", "iota_done", "const_step", "vec_means", "lists_copied", "pad_made"))
            iota_i = c1.enter_context(nc.sbuf_tensor("iota_i", [P, P], I32))
            iota_p = c1.enter_context(nc.sbuf_tensor("iota_p", [P, 1], I32))
            tmp = c1.enter_context(nc.sbuf_tensor("tmp", [P, P], F32))
            hi_p = c1.enter_context(nc.sbuf_tensor("hi_p", [P, 1], F32))
            pad_s = c1.enter_context(nc.sbuf_tensor("pad_s", [P, 1024], I32))
            pad_t = c1.enter_context(nc.sbuf_tensor("pad_t", [P, 1024], I32))
            pad_a = c1.enter_context(nc.sbuf_tensor("pad_a", [P, 8 * 1024], F32))
            vm_ps = c1.enter_context(nc.psum_tensor("vm_ps", [P, 512], F32))
            zero_list = [enc_w0, nenc_w0, dec_w0, *w1.values(), *ew0, *nw0]
            with nc.Block() as block:
                @block.sync
                def _(sp):
                    def load(t, ap):
                        sp.dma_start(t, ap).then_inc(s_ld, 16)
                        n_ld[0] += 1

                    for k in VEC:
                        key, s = (k[:-1], int(k[-1])) if k[-1] in "01" else (k, None)
                        for what in ("b0", "b1", "g", "beta"):
                            v = w[f"{key}_{what}"]
                            v = v if s is None else v[s]
                            for h in range(2):
                                load(vecs[64 * h:64 * h + 64, vcol(k, what):vcol(k, what) + 1],
                                     v.rearrange("(d a) -> d a", a=1))
                    for h in range(2):
                        load(vecs[64 * h:64 * h + 64, DEC_B0:DEC_B0 + 1], w["dec_b0"].rearrange("(d a) -> d a", a=1))
                        load(dec_w1[64 * h:64 * h + 64, :], w["dec_w1"])
                        for s in range(STEPS):
                            for q in range(2):
                                load(proj_w[s][64 * h:64 * h + 64, 64 * q:64 * q + 64],
                                     w["edge_blk_w0"][s, D * (q + 1):D * (q + 2), :])
                            load(aw0[s][64 * h:64 * h + 64, :], w["node_blk_w0"][s, D:2 * D, :])
                    load(dec_b1[:, :], w["dec_b1"].rearrange("(a d) -> a d", a=1).broadcast_to([P, OUT_DIM]))
                    sp.wait_ge(s_zero, len(zero_list))
                    for h in range(2):
                        for t in range(TILES):
                            r = 8 * (t + TILES * h)
                            load(enc_w0[r:r + 8, t, 64 * h:64 * h + 64], w["edge_enc_w0"])
                        load(nenc_w0[16 * h:16 * h + 16, 64 * h:64 * h + 64], w["node_enc_w0"])
                        q = slice(64 * h, 64 * h + 64)
                        load(dec_w0[q, q], w["dec_w0"])
                        load(w1["edge_enc"][q, q], w["edge_enc_w1"])
                        load(w1["node_enc"][q, q], w["node_enc_w1"])
                        for s in range(STEPS):
                            load(ew0[s][q, q], w["edge_blk_w0"][s, 0:D, :])
                            load(nw0[s][q, q], w["node_blk_w0"][s, 0:D, :])
                            load(w1[f"edge_blk{s}"][q, q], w["edge_blk_w1"][s])
                            load(w1[f"node_blk{s}"][q, q], w["node_blk_w1"][s])
                    sp.wait_ge(s_ld, 16 * n_ld[0])

                @block.scalar
                def _(act):
                    q = N_EDGES // P
                    act.dma_start(src_d[0:N_EDGES].rearrange("(p q) -> p q", p=P),
                                  src.rearrange("(p q) -> p q", p=P)).then_inc(s_cp, 16)
                    act.dma_start(dst_d[0:N_EDGES].rearrange("(p q) -> p q", p=P),
                                  dst.rearrange("(p q) -> p q", p=P)).then_inc(s_cp, 16)
                    act.dma_start(attr_d[0:N_EDGES, :].rearrange("(p q) c -> p (q c)", p=P),
                                  edge_attr.rearrange("(p q) c -> p (q c)", p=P)).then_inc(s_cp, 16)
                    q = (SLOTS - N_EDGES) // P
                    act.wait_ge(s_pad, 3)
                    act.dma_start(src_d[N_EDGES:].rearrange("(p q) -> p q", p=P), pad_s[:, 0:q]).then_inc(s_cp, 16)
                    act.dma_start(dst_d[N_EDGES:].rearrange("(p q) -> p q", p=P), pad_t[:, 0:q]).then_inc(s_cp, 16)
                    act.dma_start(attr_d[N_EDGES:, :].rearrange("(p q) c -> p (q c)", p=P),
                                  pad_a[:, 0:8 * q]).then_inc(s_cp, 16)
                    act.wait_ge(s_cp, 96)

                @block.gpsimd
                def _(pool):
                    nc.gpsimd.iota(iota_i[:, :], pattern=[[1, P]], base=0, channel_multiplier=0).then_inc(s_io, 1)
                    nc.gpsimd.iota(iota_p[:, :], pattern=[[0, 1]], base=0, channel_multiplier=1).then_inc(s_io, 1)
                    for t in zero_list:
                        nc.gpsimd.memset(t[:], 0.0).then_inc(s_zero, 1)
                    nc.gpsimd.memset(pad_s[:, :], PAD_NODE).then_inc(s_pad, 1)
                    nc.gpsimd.memset(pad_t[:, :], PAD_DST).then_inc(s_pad, 1)
                    nc.gpsimd.memset(pad_a[:, :], 0.0).then_inc(s_pad, 1)

                @block.vector
                def _(dve):
                    k = [0]

                    def step(ins):
                        k[0] += 1
                        ins.then_inc(s_c, 1)
                        dve.wait_ge(s_c, k[0])

                    v = nc.vector
                    dve.wait_ge(s_io, 2)
                    step(v.memset(eps_c[:, :], EPS))
                    step(v.tensor_copy(row_f[:, :], iota_i[:, :]))
                    step(v.tensor_copy(row_bf[:, :], iota_i[:, :]))
                    step(v.tensor_copy(part_f[:, :], iota_p[:, :]))
                    step(v.tensor_scalar(ident[:, :], row_f[:, :], part_f[:, 0:1], None, ALU.is_equal))
                    step(v.tensor_scalar(hi_p[:, :], part_f[:, :], 64.0, None, ALU.is_ge))
                    step(v.scalar_tensor_tensor(part64[:, :], hi_p[:, :], -64.0, part_f[:, :], ALU.mult, ALU.add))
                    step(v.tensor_scalar(tmp[:, :], row_f[:, :], 64.0, None, ALU.is_ge))
                    step(v.tensor_scalar(mean_w[:, :], tmp[:, :], hi_p[:, 0:1], 1.0 / D, ALU.is_equal, ALU.mult))
                    step(v.tensor_scalar(sum_ab[:, :], row_f[:, 0:32], part64[:, 0:1], None, ALU.is_equal))
                    dve.wait_ge(s_ld, 16 * n_ld[0])
                    for i, name in enumerate(VEC):
                        step(v.tensor_reduce(wmean[:, i:i + 1], w1[name][:, :], AX_X, ALU.add))
                    step(v.tensor_scalar(wmean[:, :], wmean[:, :], -1.0 / D, None, ALU.mult))
                    for i, name in enumerate(VEC):
                        for h in range(2):
                            q = slice(64 * h, 64 * h + 64)
                            step(v.tensor_scalar(w1[name][q, q], w1[name][q, q], wmean[q, i:i + 1], None, ALU.add))
                    dve.wait_ge(s_vm, 1)
                    step(v.tensor_copy(vmean[:, :], vm_ps[:, 0:NVEC]))
                    for name in VEC:
                        c = vcol(name, "b1")
                        step(v.tensor_tensor(vecs[:, c:c + 1], vecs[:, c:c + 1], vmean[:, c:c + 1], ALU.subtract))

                @block.tensor
                def _(pe):
                    pe.wait_ge(s_ld, 16 * n_ld[0])
                    pe.wait_ge(s_c, 10)
                    nc.tensor.matmul(vm_ps[:, 0:NVEC], mean_w[:, :], vecs[:, :], start=True, stop=True).then_inc(s_vm, 1)

        pairs, blocks = FAST_ROUNDS // 2, FAST_BLOCKS

        edge_lists(nc, src_d, dst_d, local_d, lists_d, base_sb, deg, row_bf, ident, blocks)
        scaled_senders(nc, x, x1, deg, xg_d, eps_c)
        first_layer(nc, lists_d, attr_d, xg_d, edge_d, base_sb, agg, enc_w0, w1["edge_enc"], mean_w, ident,
                    row_f, vecs, eps_c, pairs)
        vv = dict(nc=nc, agg=agg, node=node, x1=x1, vecs=vecs, mean_w=mean_w, ident=ident, eps_c=eps_c,
                  ps_d=ps_d, pr_d=pr_d)
        node_phase(**vv, mlp="node_enc", w_in=nenc_w0, w_mid=w1["node_enc"], proj=proj_w[0], sum_ab=sum_ab)
        for s in range(STEPS):
            edge_step(nc, lists_d, local_d, edge_d, ps_d, pr_d, base_sb, agg, ew0[s], w1[f"edge_blk{s}"], mean_w,
                      ident, row_f, part64, vecs, eps_c, f"edge_blk{s}", s < STEPS - 1, pairs)
            node_phase(**vv, mlp=f"node_blk{s}", w_in=nw0[s], w_mid=w1[f"node_blk{s}"], w_agg=aw0[s],
                       proj=proj_w[s + 1] if s < STEPS - 1 else None,
                       dec=(dec_w0, dec_w1, dec_b1, out) if s == STEPS - 1 else None)


def edge_lists(nc, src_d, dst_d, local_d, lists_d, base_sb, deg, row_bf, ident, blocks):
    with ExitStack() as ctx:
        def sb(name, shape, dt=F32):
            return ctx.enter_context(nc.sbuf_tensor("el_" + name, shape, dt))

        sem = ctx.enter_context(semaphores(nc, "el_"))

        base_col = sb("base_col", [P, MAX_BLOCKS], I32)
        base_f = sb("base_f", [P, MAX_BLOCKS])
        srow = sb("srow", [P, P], I32)
        drow = sb("drow", [P, P], I32)
        srow_f = sb("srow_f", [P, P])
        local_f = sb("local_f", [P, P])
        local_bf = sb("local_bf", [P, P], BF16)
        lists = sb("lists", [P, 16, 16], I32)
        s_lo = sb("s_lo", [P, P], I32)
        s_hi = sb("s_hi", [P, P], I32)
        lo_b = sb("lo_b", [P, P], BF16)
        hi_b = sb("hi_b", [P, P], BF16)
        GT = 16
        NHI = -(-(N_NODES + 1) // P)
        value = sb("value", [P, P, GT], BF16)
        one_lo = [sb(f"one_lo{i}", [P, P, GT], BF16) for i in range(2)]
        one_hi = [sb(f"one_hi{i}", [P, NHI, GT], BF16) for i in range(2)]
        zeros = sb("zeros", [P, P], BF16)
        t_ps = ctx.enter_context(nc.psum_tensor("el_tps", [P, 512], F32))
        d_ps = ctx.enter_context(nc.psum_tensor("el_dps", [P, 512], F32))
        base_in, base_ok, rows_in, rows_f, tr_done, lists_ok, idx_ok, lists_out, onehots, hist, local_ok, zero_ok, deg_ok = (
            sem(k) for k in ("base_in", "base_ok", "rows_in", "rows_f", "transposed", "lists_ok", "idx_ok", "lists_out",
                             "onehots", "hist", "local_ok", "zero_ok", "deg_ok"))
        passed = sem("passed")
        G = P // GT
        with nc.Block() as block:
            @block.sync
            def _(sp):
                sp.dma_start(base_sb[0:1, :], dst_d.rearrange("(c e) -> e c", e=CHUNK)[0:1, :],
                             allow_slow_non_contiguous=True).then_inc(base_in, 16)
                for j in range(TILES):
                    sp.dma_start(base_col[j:P:TILES, :],
                                 dst_d.rearrange("(k c e) -> e c k", e=CHUNK, k=MAX_BLOCKS)[0],
                                 allow_slow_non_contiguous=True).then_inc(base_in, 16)
                def body(k):
                    at = bass.ds(k, 1)
                    if not (isinstance(k, int) and k == 0):
                        for waited, value in ((tr_done, k), (local_ok, k), (lists_out, k * 32)):
                            sp.wait_ge(waited, value)
                            held(sp, passed)
                    sp.dma_start(srow[:, :], src_d.rearrange("(k t p) -> k t p", p=P, t=P)[at].rearrange(
                        "a t p -> (a t) p")).then_inc(rows_in, 16)
                    sp.dma_start(drow[:, :], dst_d.rearrange("(k t p) -> k t p", p=P, t=P)[at].rearrange(
                        "a t p -> (a t) p")).then_inc(rows_in, 16)
                    sp.wait_ge(local_ok, k + 1)
                    held(sp, passed)
                    sp.dma_start(local_d.rearrange("(k t p) -> k t p", p=P, t=P)[at].rearrange(
                        "a t p -> (a t) p"), local_bf[:, :]).then_inc(lists_out, 16)
                    sp.wait_ge(lists_ok, k + 1)
                    held(sp, passed)
                    sp.dma_start(lists_d.rearrange("r p c -> p r c")[:, bass.ds(k * 16, 16), :],
                                 lists[:, :, :]).then_inc(lists_out, 16)

                body(0)
                with sp.Fori(1, blocks) as k:
                    body(k)
                sp.wait_ge(lists_out, blocks * 32)

            @block.vector
            def _(dve):
                v = nc.vector
                v.memset(zeros[:, :], 0.0).then_inc(zero_ok, 1)
                v.tensor_copy(value[:, :, :], row_bf[:, :].rearrange("p (w t) -> p w t", t=1).broadcast_to(
                    [P, P, GT])).then_inc(zero_ok, 1)
                v.memset(deg[:, NHI:], 0.0).then_inc(zero_ok, 1)
                dve.wait_ge(zero_ok, 3)
                dve.wait_ge(base_in, 16 * (TILES + 1))
                v.tensor_scalar(base_sb[:, :], base_sb[:, :], LAST_BASE, None, ALU.min)
                v.tensor_scalar(base_f[:, :], base_col[:, :], LAST_BASE, None, ALU.min).then_inc(base_ok, 1)
                dve.wait_ge(base_ok, 1)

                def wide(a, n):
                    return a.rearrange("p (w t) -> p w t", w=1).broadcast_to([P, n, GT])

                def body(k):
                    later = not (isinstance(k, int) and k == 0)
                    dve.wait_ge(rows_in, k * 32 + 32)
                    if later:
                        dve.wait_ge(lists_out, k * 32)
                        dve.wait_ge(tr_done, k)
                    v.tensor_copy(srow_f[:, :], srow[:, :])
                    v.tensor_tensor(local_f[:, :], drow[:, :], base_f[:, bass.ds(k, 1)].broadcast_to([P, P]),
                                    ALU.subtract).then_inc(rows_f, 1)
                    dve.wait_ge(rows_f, k + 1)
                    v.tensor_copy(local_bf[:, :], local_f[:, :]).then_inc(local_ok, 1)
                    dve.wait_ge(tr_done, k + 1)
                    v.tensor_copy(lists[:, :, 0:8], t_ps[:, 0:P].rearrange("p (r j) -> p r j", j=8)).then_inc(idx_ok, 1)
                    v.tensor_copy(lists[:, :, 8:16].bitcast(F32),
                                  t_ps[:, P:2 * P].rearrange("p (r j) -> p r j", j=8)).then_inc(lists_ok, 1)
                    dve.wait_ge(idx_ok, k * 3 + 1)
                    v.tensor_scalar(s_lo[:, :].rearrange("p (r j) -> p r j", j=8), lists[:, :, 0:8], 127, None,
                                    ALU.bitwise_and)
                    v.tensor_scalar(s_hi[:, :].rearrange("p (r j) -> p r j", j=8), lists[:, :, 0:8], 7, None,
                                    ALU.logical_shift_right).then_inc(idx_ok, 1)
                    dve.wait_ge(idx_ok, k * 3 + 2)
                    v.tensor_copy(lo_b[:, :], s_lo[:, :])
                    v.tensor_copy(hi_b[:, :], s_hi[:, :]).then_inc(idx_ok, 1)
                    dve.wait_ge(idx_ok, k * 3 + 3)
                    for g in range(G):
                        if g >= 2 or later:
                            dve.wait_ge(hist, k * G + (g - 1))
                        at = slice(GT * g, GT * g + GT)
                        v.tensor_tensor(one_lo[g % 2][:, :, :], value[:, :, :], wide(lo_b[:, at], P), ALU.is_equal)
                        v.tensor_tensor(one_hi[g % 2][:, :, :], value[:, 0:NHI, :], wide(hi_b[:, at], NHI),
                                        ALU.is_equal).then_inc(onehots, 1)

                body(0)
                with dve.Fori(1, blocks) as k:
                    body(k)
                dve.wait_ge(deg_ok, 1)
                v.tensor_copy(deg[:, 0:NHI], d_ps[:, 0:NHI]).then_inc(zero_ok, 1)
                dve.wait_ge(zero_ok, 4)

            @block.tensor
            def _(pe):
                pe.wait_ge(zero_ok, 3)
                nc.tensor.matmul(d_ps[:, 0:NHI], zeros[:, :], zeros[:, 0:NHI], start=True, stop=False, skip_group_check=True)

                def body(k):
                    pe.wait_ge(rows_f, k + 1)
                    if not (isinstance(k, int) and k == 0):
                        pe.wait_ge(idx_ok, k * 3)
                        pe.wait_ge(lists_ok, k)
                    nc.tensor.transpose(t_ps[:, 0:P], srow_f[:, :], ident[:, :])
                    nc.tensor.transpose(t_ps[:, P:2 * P], local_f[:, :], ident[:, :]).then_inc(tr_done, 1)
                    for g in range(G):
                        pe.wait_ge(onehots, k * G + (g + 1))
                        for j in range(GT):
                            ins = nc.tensor.matmul(d_ps[:, 0:NHI], one_lo[g % 2][:, :, j], one_hi[g % 2][:, :, j],
                                                   start=False, stop=False, skip_group_check=True)
                        ins.then_inc(hist, 1)

                body(0)
                with pe.Fori(1, blocks) as k:
                    body(k)
                nc.tensor.matmul(d_ps[:, 0:NHI], zeros[:, :], zeros[:, 0:NHI], start=False, stop=True,
                                 skip_group_check=True).then_inc(deg_ok, 1)


def norm_rows(nc, dve_step, act_step, h, t_in, sq, red, rinv, eps_c, n):
    v = nc.vector
    bc = lambda a: a.rearrange("p (r j) -> p r j", j=1).broadcast_to([P, n, X_DIM])
    dve_step(v.tensor_reduce(red, t_in, AX_X, ALU.add))
    dve_step(v.tensor_scalar(red, red, 1.0 / X_DIM, None, ALU.mult))
    dve_step(v.tensor_tensor(h, t_in, bc(red), ALU.subtract))
    dve_step(v.tensor_tensor(sq, h, h, ALU.mult))
    dve_step(v.tensor_reduce(red, sq, AX_X, ALU.add))
    act_step(lambda: nc.scalar.activation(rinv, red, ACT.Sqrt, bias=eps_c[:, 0:1], scale=1.0 / X_DIM))
    dve_step(v.reciprocal(rinv, rinv))
    dve_step(v.tensor_tensor(h, h, bc(rinv), ALU.mult))
    dve_step(v.tensor_scalar(h, h, 0.0, None, ALU.max))


def scaled_senders(nc, x, x1, deg, xg_d, eps_c):
    with ExitStack() as ctx:
        def sb(name, shape, dt=F32):
            return ctx.enter_context(nc.sbuf_tensor("ss_" + name, shape, dt))

        sem = ctx.enter_context(semaphores(nc, "ss_"))

        h, sq = sb("h", [P, HI, X_DIM]), sb("sq", [P, HI, X_DIM])
        red, rinv, rs = sb("red", [P, HI]), sb("rinv", [P, HI]), sb("rs", [P, HI])
        rows = sb("rows", [P, HI, 32])
        x_in, dstep, astep, zeroed, out_done = (sem(k) for k in ("x_in", "dve_step", "act_step", "zeroed", "rows_out"))
        nd, na = [0], [0]
        jobs = []
        full = N_NODES // P
        rest = N_NODES - full * P
        with nc.Block() as block:
            @block.gpsimd
            def _(pool):
                nc.gpsimd.memset(x1[:, full:, :], 0.0).then_inc(zeroed, 1)
                nc.gpsimd.memset(rows[:, :, X_DIM:], 0.0).then_inc(zeroed, 1)

            @block.sync
            def _(sp):
                sp.dma_start(x1[:, 0:full, :], x[0:full * P, :].rearrange("(k p) c -> p k c", p=P)).then_inc(x_in, 16)
                sp.wait_ge(zeroed, 1)
                sp.dma_start(x1[0:rest, full, :], x[full * P:, :]).then_inc(x_in, 16)
                sp.wait_ge(out_done, 1)
                sp.dma_start(xg_d.rearrange("(k p) c -> p k c", p=P), rows[:, :, :]).then_inc(x_in, 16)
                sp.wait_ge(x_in, 48)

            @block.vector
            def _(dve):
                v = nc.vector

                def dve_step(ins):
                    nd[0] += 1
                    ins.then_inc(dstep, 1)
                    dve.wait_ge(dstep, nd[0])

                def act_step(ins):
                    na[0] += 1
                    jobs.append((nd[0], ins))
                    dve.wait_ge(astep, na[0])

                dve.wait_ge(x_in, 32)
                dve.wait_ge(zeroed, 2)
                norm_rows(nc, dve_step, act_step, h[:, :, :], x1[:, :, :], sq[:, :, :], red[:, :], rinv[:, :], eps_c, HI)
                dve_step(v.tensor_scalar(rs[:, :], deg[:, :], 1.0, None, ALU.max))
                act_step(lambda: nc.scalar.activation(rs[:, :], rs[:, :], ACT.Sqrt))
                dve_step(v.reciprocal(rs[:, :], rs[:, :]))
                dve_step(v.memset(rows[:, :, X_DIM:X_DIM + 1], 1.0))
                v.tensor_tensor(rows[:, :, 0:X_DIM], h[:, :, :],
                                rs[:, :].rearrange("p (r j) -> p r j", j=1).broadcast_to([P, HI, X_DIM]),
                                ALU.mult).then_inc(out_done, 1)

            @block.scalar
            def _(act):
                for at, ins in jobs:
                    act.wait_ge(dstep, at)
                    ins().then_inc(astep, 1)


def first_layer(nc, lists_d, attr_d, xg_d, edge_d, base_sb, agg, enc_w0, w_mid, mean_w, ident, row_f, vecs, eps_c, pairs):
    with ExitStack() as ctx:
        def sb(name, shape, dt=F32):
            return ctx.enter_context(nc.sbuf_tensor("fl_" + name, shape, dt))

        def two(name, shape, dt=F32):
            return [sb(f"{name}{i}", shape, dt) for i in range(2)]

        def ps(name):
            return ctx.enter_context(nc.psum_tensor("fl_" + name, [P, 512], F32))

        sem = ctx.enter_context(semaphores(nc, "fl_"))

        idx = two("idx", [P, 8], I32)
        lst = two("lst", [P, 8], I32)
        attr = two("attr", [P, 8, E_DIM])
        attr_t = sb("attr_t", [64, P])
        g = two("g", [P, 8, 32])
        ohb = two("ohb", [P, 8, WIN])
        h, sq, t = (sb(k, [P, CHUNK]) for k in ("h", "sq", "t"))
        sd, rs = sb("sd", [P, 2 * TILES]), sb("rs", [P, 2 * TILES])
        rs_x = two("rs_x", [P, 2 * TILES, D])
        yb = two("yb", [P, CHUNK])
        idle = sb("idle", [P, 1])
        e = two("e", [P, CHUNK])
        at_ps, h_ps, var_ps, agg_ps, r_ps = ps("atps"), ps("hps"), ps("varps"), ps("aggps"), ps("rps")
        y_ps = [ps("yps0"), ps("yps1")]
        idx_in, list_in, attr_in, g_in, e_out = ([sem(f"{k}{i}") for i in range(2)] for k in ("idx_in", "list_in", "attr_in", "g_in", "e_out"))
        passed = sem("passed")
        zeroed, turned, turned_sb, pre, h_ok, y_ok, sq_ok, yb_ok, var_ok, sd_ok, r_ok, rx_ok, spread, t_ok, e_ok, oh_ok, sum_ok, added = (
            sem(k) for k in ("zeroed", "turned", "turned_sb", "pre", "h_ok", "y_ok", "sq_ok", "yb_ok", "var_ok", "sd_ok", "r_ok", "rx_ok", "spread",
                             "t_ok", "e_ok", "oh_ok", "sum_ok", "added"))
        attr_v = attr_d.rearrange("(r j p) c -> r p j c", p=P, j=8)
        col = lambda what: vecs[:, vcol("edge_enc", what):vcol("edge_enc", what) + 1]
        last = Slot(pairs, 0)
        with nc.Block() as block:
            @block.sync
            def _(sp):
                def store(n):
                    if n.exists():
                        wait(sp, e_ok, n)
                        sp.dma_start(edge_d[bass.ds(n.n, 1)].rearrange("a p c -> (a p) c"), e[n.b][:, :]).then_inc(e_out[n.b], 16)

                def body(n):
                    landed(sp, g_in, n.back(2), 128)
                    sp.dma_start(idx[n.b][:, :], lists_d[bass.ds(n.n, 1), :, 0:8].rearrange("a p c -> (a p) c")).then_inc(idx_in[n.b], 16)
                    wait(sp, turned, n.back(2))
                    sp.dma_start(attr[n.b][:, :, :], attr_v[bass.ds(n.n, 1)].rearrange("a p j c -> (a p) j c")).then_inc(attr_in[n.b], 16)
                    wait(sp, oh_ok, n.back(2))
                    sp.dma_start(lst[n.b][:, :], lists_d[bass.ds(n.n, 1), :, 8:16].rearrange("a p c -> (a p) c")).then_inc(list_in[n.b], 16)
                    store(n.back(3))

                rounds(sp, body, pairs, 3)
                store(last.back(3))
                store(last.back(2))
                store(last.back(1))
                landed(sp, e_out, last.back(2))
                landed(sp, e_out, last.back(1))

            @block.gpsimd
            def _(pool):
                def body(n):
                    landed(pool, idx_in, n)
                    wait(pool, sum_ok, n.back(2))
                    held(pool, passed)
                    for j in range(8):
                        pool.indirect_dma_start(
                            out=g[n.b][:, j, :], out_offset=None, in_=xg_d,
                            in_offset=bass.IndirectOffsetOnAxis(ap=idx[n.b][:, j:j + 1].bitcast(U32), axis=0),
                        ).then_inc(g_in[n.b], 16)

                rounds(pool, body, pairs)

            @block.tensor
            def _(pe):
                def spread_out(n):
                    if not n.exists():
                        return
                    wait(pe, rx_ok, n)
                    wait(pe, t_ok, n.back(1))
                    for i in range(TILES):
                        ins = nc.tensor.matmul(r_ps[:, P * i:P * i + P], rs_x[n.b][:, 2 * i:2 * i + 2, :].rearrange(
                            "p c d -> p (c d)"), ident[:, :], start=True, stop=True)
                    ins.then_inc(spread, 1)

                def sums(n):
                    if not n.exists():
                        return
                    landed(pe, g_in, n, 128)
                    wait(pe, oh_ok, n)
                    wait(pe, added, n.back(1))
                    for c in range(2):
                        for i in range(TILES):
                            j = c * TILES + i
                            ins = nc.tensor.matmul(agg_ps[64 * c:64 * c + 32, 0:WIN], g[n.b][:, j, :], ohb[n.b][:, j, :],
                                                   start=i == 0, stop=i == TILES - 1)
                    ins.then_inc(sum_ok, 1)

                def turn_in(n):
                    landed(pe, attr_in, n)
                    wait(pe, turned_sb, n.back(1))
                    held(pe, passed)
                    nc.tensor.transpose(at_ps[0:64, 0:P], attr[n.b][:, :, :].rearrange("p j c -> p (j c)"),
                                        ident[:, :]).then_inc(turned, 1)

                def encode(n):
                    if not n.exists():
                        return
                    wait(pe, turned_sb, n)
                    wait(pe, h_ok, n.back(1))
                    for i in range(TILES):
                        ins = nc.tensor.matmul(h_ps[:, P * i:P * i + P], enc_w0[:, i, :], attr_t[:, :], start=True, stop=True)
                    ins.then_inc(pre, 1)

                def second(n):
                    if not n.exists():
                        return
                    wait(pe, h_ok, n)
                    wait(pe, yb_ok, n.back(2))
                    nc.tensor.matmul(y_ps[n.b][:, :], w_mid[:, :], h[:, :], start=True, stop=True).then_inc(y_ok, 1)
                    wait(pe, sq_ok, n)
                    wait(pe, sd_ok, n.back(1))
                    for i in range(TILES):
                        ins = nc.tensor.matmul(var_ps[:, 2 * i:2 * i + 2], sq[:, P * i:P * i + P], mean_w[:, 0:P:D],
                                               start=True, stop=True)
                    ins.then_inc(var_ok, 1)

                def body(n):
                    encode(n.back(1))
                    turn_in(n)
                    spread_out(n.back(2))
                    sums(n.back(2))
                    second(n.back(1))

                rounds(pe, body, pairs, 3)
                encode(last.back(1))
                spread_out(last.back(2))
                sums(last.back(2))
                second(last.back(1))
                spread_out(last.back(1))
                sums(last.back(1))

            @block.scalar
            def _(act):
                def warm(func):
                    nc.scalar.activation(idle[:, :], eps_c[:, :], func)

                def body(n):
                    warm(ACT.Silu)
                    wait(act, pre, n)
                    wait(act, y_ok, n.back(1))
                    nc.scalar.activation(h[:, :], h_ps[:, :], ACT.Silu, bias=col("b0")).then_inc(h_ok, 1)
                    wait(act, y_ok, n)
                    wait(act, var_ok, n.back(1))
                    nc.scalar.activation(sq[:, :], y_ps[n.b][:, :], ACT.Square, bias=col("b1")).then_inc(sq_ok, 1)
                    warm(ACT.Sqrt)
                    wait(act, var_ok, n)
                    wait(act, r_ok, n.back(1))
                    nc.scalar.activation(sd[:, :], var_ps[:, 0:2 * TILES], ACT.Sqrt, bias=eps_c[:, 0:1]).then_inc(sd_ok, 1)
                    wait(act, r_ok, n)
                    wait(act, spread, n.back(2))
                    nc.scalar.activation(rs_x[n.b][:, :, :], rs[:, :].rearrange("p (i c) -> p i c", c=1).broadcast_to(
                        [P, 2 * TILES, D]), ACT.Copy).then_inc(rx_ok, 1)
                    wait(act, t_ok, n.back(2))
                    nc.scalar.activation(yb[n.b][:, :], y_ps[n.b][:, :], ACT.Identity, bias=col("b1")).then_inc(yb_ok, 1)

                rounds(act, body, pairs, 2)

            @block.vector
            def _(dve):
                v = nc.vector

                def invert(n):
                    if not n.exists():
                        return
                    wait(dve, sd_ok, n)
                    wait(dve, rx_ok, n.back(1))
                    v.reciprocal(rs[:, :], sd[:, :]).then_inc(r_ok, 1)

                def finish(n):
                    if not n.exists():
                        return
                    wait(dve, spread, n)
                    wait(dve, e_ok, n.back(1))
                    wait(dve, yb_ok, n)
                    v.tensor_tensor(t[:, :], yb[n.b][:, :], r_ps[:, :], ALU.mult).then_inc(t_ok, 1)
                    wait(dve, t_ok, n)
                    landed(dve, e_out, n.back(2))
                    v.tensor_scalar(e[n.b][:, :], t[:, :], col("g"), col("beta"), ALU.mult, ALU.add).then_inc(e_ok, 1)

                def add_sums(n):
                    if not n.exists():
                        return
                    at = [dve.value_load(base_sb[0:1, bass.ds(n.n * 2 + c, 1)], min_val=0, max_val=LAST_BASE) for c in range(2)]
                    wait(dve, sum_ok, n)
                    wait(dve, added, n.back(1))
                    for c in range(2):
                        a = agg[64 * c:64 * c + 32, bass.ds(at[c], WIN)]
                        ins = v.tensor_tensor(a, a, agg_ps[64 * c:64 * c + 32, 0:WIN], ALU.add)
                    ins.then_inc(added, 1)

                def one_hots(n):
                    if not n.exists():
                        return
                    landed(dve, list_in, n)
                    wait(dve, sum_ok, n.back(2))
                    for j in range(8):
                        ins = v.tensor_scalar(ohb[n.b][:, j, :], row_f[:, 0:WIN], lst[n.b][:, j:j + 1].bitcast(F32), None,
                                              ALU.is_equal)
                    ins.then_inc(oh_ok, 1)

                def body(n):
                    wait(dve, turned, n)
                    wait(dve, pre, n.back(1))
                    v.tensor_copy(attr_t[:, :], at_ps[0:64, 0:P]).then_inc(turned_sb, 1)
                    one_hots(n.back(1))
                    finish(n.back(2))
                    invert(n.back(1))
                    add_sums(n.back(2))

                v.memset(agg[:, :], 0.0).then_inc(zeroed, 1)
                dve.wait_ge(zeroed, 1)
                rounds(dve, body, pairs, 3)
                one_hots(last.back(1))
                finish(last.back(2))
                invert(last.back(1))
                add_sums(last.back(2))
                finish(last.back(1))
                add_sums(last.back(1))


def edge_step(nc, lists_d, local_d, edge_d, ps_d, pr_d, base_sb, agg, w_in, w_mid, mean_w, ident, row_f, part64,
              vecs, eps_c, mlp, keep, pairs):
    with ExitStack() as ctx:
        tag = mlp + "_"

        def sb(name, shape, dt=F32):
            return ctx.enter_context(nc.sbuf_tensor(tag + name, shape, dt))

        def two(name, shape, dt=F32):
            return [sb(f"{name}{i}", shape, dt) for i in range(2)]

        def ps(name):
            return ctx.enter_context(nc.psum_tensor(tag + name, [P, 512], F32))

        sem = ctx.enter_context(semaphores(nc, tag))

        idx = two("idx", [P, 8], I32)
        lst = two("lst", [P, 8], I32)
        dlb = two("dlb", [P, CHUNK], BF16)
        win = two("win", [P, P])
        g = two("g", [P, TILES, P])
        oha = two("oha", [P, CHUNK])
        ohb = two("ohb", [P, 8, WIN])
        e = two("e", [P, CHUNK])
        eb = two("eb", [P, CHUNK])
        h, sq, t = (sb(k, [P, CHUNK]) for k in ("h", "sq", "t"))
        sd, rs = sb("sd", [P, 2 * TILES]), sb("rs", [P, 2 * TILES])
        rs_x = two("rs_x", [P, 2 * TILES, D])
        yb = two("yb", [P, CHUNK])
        idle = sb("idle", [P, 1])
        new = two("new", [P, CHUNK])
        new_t = sb("new_t", [P, TILES, P])
        y_ps = [ps("yps0"), ps("yps1")]
        h_ps, var_ps, t_ps, agg_ps, r_ps = ps("hps"), ps("varps"), ps("tps"), ps("aggps"), ps("rps")
        idx_in, list_in, dlb_in, win_in, g_in, e_in, e_out = (
            [sem(f"{k}{i}") for i in range(2)] for k in ("idx_in", "list_in", "dlb_in", "win_in", "g_in", "e_in", "e_out"))
        passed = sem("passed")
        zeroed, pre, h_ok, y_ok, sq_ok, yb_ok, var_ok, sd_ok, r_ok, rx_ok, spread, t_ok, new_ok, eb_ok, oha_ok, ohb_ok, turned, turned_sb, sum_ok, added = (
            sem(k) for k in ("zeroed", "pre", "h_ok", "y_ok", "sq_ok", "yb_ok", "var_ok", "sd_ok", "r_ok", "rx_ok", "spread", "t_ok", "new_ok", "eb_ok",
                             "oha_ok", "ohb_ok", "turned", "turned_sb", "sum_ok", "added"))
        local_v = local_d.rearrange("(r c e) -> r c e", e=CHUNK, c=2)
        col = lambda what: vecs[:, vcol(mlp, what):vcol(mlp, what) + 1]
        last = Slot(pairs, 0)
        with nc.Block() as block:
            @block.sync
            def _(sp):
                def store(n):
                    if keep and n.exists():
                        wait(sp, new_ok, n)
                        sp.dma_start(edge_d[bass.ds(n.n, 1)].rearrange("a p c -> (a p) c"), new[n.b][:, :]).then_inc(e_out[n.b], 16)

                def body(n):
                    landed(sp, g_in, n.back(2), 128)
                    sp.dma_start(idx[n.b][:, :], lists_d[bass.ds(n.n, 1), :, 0:8].rearrange("a p c -> (a p) c")).then_inc(idx_in[n.b], 16)
                    wait(sp, oha_ok, n.back(2))
                    for c in range(2):
                        sp.dma_start(dlb[n.b][64 * c:64 * c + 64, :],
                                     local_v[bass.ds(n.n, 1), c, :].broadcast_to([64, CHUNK])).then_inc(dlb_in[n.b], 16)
                    at = [sp.value_load(base_sb[0:1, bass.ds(n.n * 2 + c, 1)], min_val=0, max_val=LAST_BASE) for c in range(2)]
                    wait(sp, pre, n.back(2))
                    wait(sp, eb_ok, n.back(2))
                    sp.dma_start(e[n.b][:, :], edge_d[bass.ds(n.n, 1)].rearrange("a p c -> (a p) c")).then_inc(e_in[n.b], 16)
                    for c in range(2):
                        q = slice(64 * c, 64 * c + 64)
                        sp.dma_start(win[n.b][q, q], pr_d[bass.ds(at[c], WIN), :]).then_inc(win_in[n.b], 16)
                    wait(sp, ohb_ok, n.back(2))
                    sp.dma_start(lst[n.b][:, :], lists_d[bass.ds(n.n, 1), :, 8:16].rearrange("a p c -> (a p) c")).then_inc(list_in[n.b], 16)
                    store(n.back(3))

                sp.wait_ge(zeroed, 1)
                rounds(sp, body, pairs, 3)
                store(last.back(3))
                store(last.back(2))
                store(last.back(1))
                if keep:
                    landed(sp, e_out, last.back(2))
                    landed(sp, e_out, last.back(1))

            @block.gpsimd
            def _(pool):
                def body(n):
                    landed(pool, idx_in, n)
                    wait(pool, pre, n.back(2))
                    held(pool, passed)
                    for j in range(8):
                        c, i = j // TILES, j % TILES
                        pool.indirect_dma_start(
                            out=g[n.b][:, i, 64 * c:64 * c + 64], out_offset=None, in_=ps_d,
                            in_offset=bass.IndirectOffsetOnAxis(ap=idx[n.b][:, j:j + 1].bitcast(U32), axis=0),
                        ).then_inc(g_in[n.b], 16)

                rounds(pool, body, pairs)

            @block.tensor
            def _(pe):
                def spread_out(n):
                    if not n.exists():
                        return
                    wait(pe, rx_ok, n)
                    wait(pe, t_ok, n.back(1))
                    for i in range(TILES):
                        ins = nc.tensor.matmul(r_ps[:, P * i:P * i + P], rs_x[n.b][:, 2 * i:2 * i + 2, :].rearrange(
                            "p c d -> p (c d)"), ident[:, :], start=True, stop=True)
                    ins.then_inc(spread, 1)

                def turn(n):
                    if not n.exists():
                        return
                    wait(pe, new_ok, n)
                    wait(pe, turned_sb, n.back(1))
                    for i in range(TILES):
                        ins = nc.tensor.transpose(t_ps[:, P * i:P * i + P], new[n.b][:, P * i:P * i + P], ident[:, :])
                    ins.then_inc(turned, 1)

                def sums(n):
                    if not n.exists():
                        return
                    wait(pe, turned_sb, n)
                    wait(pe, ohb_ok, n)
                    wait(pe, added, n.back(1))
                    for c in range(2):
                        for i in range(TILES):
                            ins = nc.tensor.matmul(agg_ps[64 * c:64 * c + 64, 0:WIN], new_t[:, i, 64 * c:64 * c + 64],
                                                   ohb[n.b][:, TILES * c + i, :], start=i == 0, stop=i == TILES - 1)
                    ins.then_inc(sum_ok, 1)

                def body(n):
                    wait(pe, h_ok, n.back(1))
                    landed(pe, e_in, n)
                    nc.tensor.matmul(h_ps[:, :], w_in[:, :], e[n.b][:, :], start=True, stop=False)
                    landed(pe, win_in, n, 32)
                    wait(pe, oha_ok, n)
                    nc.tensor.matmul(h_ps[:, :], win[n.b][:, :], oha[n.b][:, :], start=False, stop=False)
                    landed(pe, g_in, n, 128)
                    for i in range(TILES):
                        ins = nc.tensor.matmul(h_ps[:, P * i:P * i + P], g[n.b][:, i, :], ident[:, :], start=False,
                                               stop=i == TILES - 1)
                    ins.then_inc(pre, 1)
                    spread_out(n.back(1))
                    sums(n.back(2))
                    wait(pe, h_ok, n)
                    wait(pe, yb_ok, n.back(2))
                    nc.tensor.matmul(y_ps[n.b][:, :], w_mid[:, :], h[:, :], start=True, stop=True).then_inc(y_ok, 1)
                    turn(n.back(1))
                    wait(pe, sq_ok, n)
                    wait(pe, sd_ok, n.back(1))
                    for i in range(TILES):
                        ins = nc.tensor.matmul(var_ps[:, 2 * i:2 * i + 2], sq[:, P * i:P * i + P], mean_w[:, 0:P:D],
                                               start=True, stop=True)
                    ins.then_inc(var_ok, 1)

                rounds(pe, body, pairs, 3)
                spread_out(last.back(1))
                sums(last.back(2))
                turn(last.back(1))
                sums(last.back(1))

            @block.scalar
            def _(act):
                def warm(func):
                    nc.scalar.activation(idle[:, :], eps_c[:, :], func)

                def body(n):
                    warm(ACT.Silu)
                    wait(act, pre, n)
                    wait(act, y_ok, n.back(1))
                    nc.scalar.activation(h[:, :], h_ps[:, :], ACT.Silu, bias=col("b0")).then_inc(h_ok, 1)
                    landed(act, e_in, n)
                    wait(act, new_ok, n.back(2))
                    nc.scalar.activation(eb[n.b][:, :], e[n.b][:, :], ACT.Identity, bias=col("beta")).then_inc(eb_ok, 1)
                    wait(act, y_ok, n)
                    wait(act, var_ok, n.back(1))
                    nc.scalar.activation(sq[:, :], y_ps[n.b][:, :], ACT.Square, bias=col("b1")).then_inc(sq_ok, 1)
                    warm(ACT.Sqrt)
                    wait(act, var_ok, n)
                    wait(act, r_ok, n.back(1))
                    nc.scalar.activation(sd[:, :], var_ps[:, 0:2 * TILES], ACT.Sqrt, bias=eps_c[:, 0:1]).then_inc(sd_ok, 1)
                    wait(act, r_ok, n)
                    wait(act, spread, n.back(2))
                    nc.scalar.activation(rs_x[n.b][:, :, :], rs[:, :].rearrange("p (i c) -> p i c", c=1).broadcast_to(
                        [P, 2 * TILES, D]), ACT.Copy).then_inc(rx_ok, 1)
                    wait(act, t_ok, n.back(2))
                    nc.scalar.activation(yb[n.b][:, :], y_ps[n.b][:, :], ACT.Identity, bias=col("b1")).then_inc(yb_ok, 1)

                rounds(act, body, pairs, 2)

            @block.vector
            def _(dve):
                v = nc.vector

                def invert(n):
                    if not n.exists():
                        return
                    wait(dve, sd_ok, n)
                    wait(dve, rx_ok, n.back(1))
                    v.reciprocal(rs[:, :], sd[:, :]).then_inc(r_ok, 1)

                def finish(n):
                    if not n.exists():
                        return
                    wait(dve, spread, n)
                    wait(dve, new_ok, n.back(1))
                    wait(dve, yb_ok, n)
                    v.tensor_tensor(t[:, :], yb[n.b][:, :], r_ps[:, :], ALU.mult).then_inc(t_ok, 1)
                    wait(dve, t_ok, n)
                    wait(dve, eb_ok, n)
                    wait(dve, turned, n.back(2))
                    if keep:
                        landed(dve, e_out, n.back(2))
                    v.scalar_tensor_tensor(new[n.b][:, :], t[:, :], col("g"), eb[n.b][:, :], ALU.mult, ALU.add).then_inc(new_ok, 1)

                def rows(n):
                    if not n.exists():
                        return
                    wait(dve, turned, n)
                    wait(dve, sum_ok, n.back(1))
                    v.tensor_copy(new_t[:, :, :], t_ps[:, :].rearrange("p (i q) -> p i q", q=P)).then_inc(turned_sb, 1)

                def add_sums(n):
                    if not n.exists():
                        return
                    at = [dve.value_load(base_sb[0:1, bass.ds(n.n * 2 + c, 1)], min_val=0, max_val=LAST_BASE) for c in range(2)]
                    wait(dve, sum_ok, n)
                    wait(dve, added, n.back(1))
                    for c in range(2):
                        a = agg[64 * c:64 * c + 64, bass.ds(at[c], WIN)]
                        ins = v.tensor_tensor(a, a, agg_ps[64 * c:64 * c + 64, 0:WIN], ALU.add)
                    ins.then_inc(added, 1)

                def one_hots(n):
                    if not n.exists():
                        return
                    landed(dve, list_in, n)
                    wait(dve, sum_ok, n.back(2))
                    for j in range(8):
                        ins = v.tensor_scalar(ohb[n.b][:, j, :], row_f[:, 0:WIN], lst[n.b][:, j:j + 1].bitcast(F32), None,
                                              ALU.is_equal)
                    ins.then_inc(ohb_ok, 1)

                def body(n):
                    landed(dve, dlb_in, n, 32)
                    wait(dve, pre, n.back(2))
                    v.tensor_scalar(oha[n.b][:, :], dlb[n.b][:, :], part64[:, 0:1], None, ALU.is_equal).then_inc(oha_ok, 1)
                    finish(n.back(2))
                    one_hots(n.back(1))
                    rows(n.back(2))
                    invert(n.back(1))
                    add_sums(n.back(3))

                for b in range(2):
                    v.memset(win[b][:, :], 0.0)
                v.memset(agg[:, :], 0.0).then_inc(zeroed, 1)
                dve.wait_ge(zeroed, 1)
                rounds(dve, body, pairs, 3)
                finish(last.back(2))
                one_hots(last.back(1))
                rows(last.back(2))
                invert(last.back(1))
                add_sums(last.back(3))
                finish(last.back(1))
                rows(last.back(1))
                add_sums(last.back(2))
                add_sums(last.back(1))


def node_phase(nc, agg, node, x1, vecs, mean_w, ident, eps_c, ps_d, pr_d, mlp, w_in, w_mid, proj, sum_ab=None, w_agg=None,
               dec=None):
    first = sum_ab is not None
    with ExitStack() as ctx:
        tag = mlp + "_"

        def sb(name, shape, dt=F32):
            return ctx.enter_context(nc.sbuf_tensor(tag + name, shape, dt))

        def ps(name):
            return ctx.enter_context(nc.psum_tensor(tag + name, [P, 512], F32))

        sem = ctx.enter_context(semaphores(nc, tag))

        col = lambda what: vecs[:, vcol(mlp, what):vcol(mlp, what) + 1]
        h, sq, t, hd = (sb(k, [P, 512]) for k in ("h", "sq", "t", "hd"))
        sd, rs = sb("sd", [P, 2 * TILES]), sb("rs", [P, 2 * TILES])
        rs_x = sb("rs_x", [P, 2 * TILES, D])
        idle = sb("idle", [P, 1])
        yb = [sb(f"yb{i}", [P, 512]) for i in range(2)]
        stage = [sb(f"stage{i}", [P, 4, P]) for i in range(2)]
        res = [sb(f"res{i}", [P, 4, OUT_DIM]) for i in range(2)]
        h_ps, var_ps, r_ps, a_ps = ps("hps"), ps("varps"), ps("rps"), ps("aps")
        y_ps = [ps("yps0"), ps("yps1")]
        o_ps = [ps("ops0"), ps("ops1")]
        a_ok, a_taken, dstep, astep, norm_ok, turned, turned_sb, pre, h_ok, y_ok, sq_ok, yb_ok, var_ok, sd_ok, r_ok, rx_ok, spread, t_ok, nb_ok, n_ok, o_ok, st_ok, d_ok, hd_ok = (
            sem(k) for k in ("a_ok", "a_taken", "dve_step", "act_step", "norm_ok", "turned", "turned_sb", "pre", "h_ok",
                             "y_ok", "sq_ok", "yb_ok", "var_ok", "sd_ok", "r_ok", "rx_ok", "spread", "t_ok", "nb_ok", "n_ok", "o_ok", "st_ok", "d_ok", "hd_ok"))
        st_out = [sem("st_out0"), sem("st_out1")]
        if first:
            hn = sb("hn", [P, NT * 4, 2, X_DIM])
            ag = sb("ag", [P, HI, 32])
            sqn = sb("sqn", [P, HI, X_DIM])
            red, rinv, din = sb("red", [P, HI]), sb("rinv", [P, HI]), sb("din", [P, HI])
            ht = sb("ht", [32, 512])
        nd, na, jobs = [0], [0], []

        def stores(q, k):
            if not dec:
                return 2 * (k + 1)
            rows = [max(0, min(512, N_NODES - HALF * q - 512 * i)) for i in range(k + 1)]
            return sum((r >= P) + (r % P > 0) for r in rows)

        AG = HI // 8
        with nc.Block() as block:
            @block.tensor
            def _(pe):
                if first:
                    for k in range(AG):
                        if k >= 2:
                            pe.wait_ge(a_taken, k - 1)
                        for i in range(8):
                            hi = 8 * k + i
                            ins = nc.tensor.matmul(o_ps[k % 2][:, 32 * i:32 * i + 32], agg[:, P * hi:P * hi + P],
                                                   sum_ab[:, :], start=True, stop=True)
                        ins.then_inc(a_ok, 1)
                    pe.wait_ge(norm_ok, 1)
                def spread_out(k):
                    pe.wait_ge(rx_ok, k + 1)
                    if k:
                        pe.wait_ge(t_ok, k)
                    for i in range(TILES):
                        ins = nc.tensor.matmul(r_ps[:, P * i:P * i + P], rs_x[:, 2 * i:2 * i + 2, :].rearrange(
                            "p c d -> p (c d)"), ident[:, :], start=True, stop=True)
                    ins.then_inc(spread, 1)

                def tail(k):
                    pe.wait_ge(n_ok, k + 1)
                    if dec:
                        if k:
                            pe.wait_ge(hd_ok, k)
                        nc.tensor.matmul(a_ps[:, :], dec[0][:, :], node[:, 512 * k:512 * k + 512],
                                         start=True, stop=True).then_inc(d_ok, 1)
                        pe.wait_ge(hd_ok, k + 1)
                    for q in range(2):
                        if k:
                            pe.wait_ge(st_ok, 2 * (k - 1) + q + 1)
                        r = slice(64 * q, 64 * q + 64)
                        for i in range(4):
                            if dec:
                                ins = nc.tensor.matmul(o_ps[q][:, OUT_DIM * i:OUT_DIM * i + OUT_DIM], hd[r, P * i:P * i + P],
                                                       dec[1][r, :], start=True, stop=True)
                            else:
                                ins = nc.tensor.matmul(o_ps[q][:, P * i:P * i + P], node[r, 512 * k + P * i:512 * k + P * i + P],
                                                       proj[r, :], start=True, stop=True)
                        ins.then_inc(o_ok, 1)

                for k in range(NT):
                    c = slice(512 * k, 512 * k + 512)
                    if first:
                        if k:
                            pe.wait_ge(turned_sb, k)
                        for q in range(4):
                            ins = nc.tensor.transpose(a_ps[0:32, P * q:P * q + P],
                                                      hn[:, 4 * k + q, :, :].rearrange("p a c -> p (a c)"), ident[:, :])
                        ins.then_inc(turned, 1)
                        pe.wait_ge(turned_sb, k + 1)
                        if k:
                            pe.wait_ge(h_ok, k)
                        nc.tensor.matmul(h_ps[:, :], w_in[:, :], ht[:, :], start=True, stop=True).then_inc(pre, 1)
                    else:
                        if k:
                            pe.wait_ge(h_ok, k)
                        nc.tensor.matmul(h_ps[:, :], w_in[:, :], node[:, c], start=True, stop=False)
                        for q in range(2):
                            ins = nc.tensor.matmul(h_ps[64 * q:64 * q + 64, :], w_agg[:, :],
                                                   agg[:, HALF * q + 512 * k:HALF * q + 512 * k + 512], start=False, stop=True)
                        ins.then_inc(pre, 1)
                    if k:
                        spread_out(k - 1)
                    pe.wait_ge(h_ok, k + 1)
                    if k >= 2:
                        pe.wait_ge(yb_ok, k - 1)
                    nc.tensor.matmul(y_ps[k % 2][:, :], w_mid[:, :], h[:, :], start=True, stop=True).then_inc(y_ok, 1)
                    pe.wait_ge(sq_ok, k + 1)
                    if k:
                        pe.wait_ge(sd_ok, k)
                    for i in range(TILES):
                        ins = nc.tensor.matmul(var_ps[:, 2 * i:2 * i + 2], sq[:, P * i:P * i + P], mean_w[:, 0:P:D],
                                               start=True, stop=True)
                    ins.then_inc(var_ok, 1)
                    if k:
                        tail(k - 1)
                spread_out(NT - 1)
                tail(NT - 1)

            @block.vector
            def _(dve):
                v = nc.vector

                def dve_step(ins):
                    nd[0] += 1
                    ins.then_inc(dstep, 1)
                    dve.wait_ge(dstep, nd[0])

                def act_step(ins):
                    na[0] += 1
                    jobs.append((nd[0], ins))
                    dve.wait_ge(astep, na[0])

                if first:
                    for k in range(AG):
                        dve.wait_ge(a_ok, k + 1)
                        v.tensor_copy(ag[:, 8 * k:8 * k + 8, :],
                                      o_ps[k % 2][:, 0:256].rearrange("p (i c) -> p i c", c=32)).then_inc(a_taken, 1)
                    dve.wait_ge(a_taken, AG)
                    dve_step(v.tensor_scalar(din[:, :], ag[:, :, X_DIM:X_DIM + 1].rearrange("p r j -> p (r j)"), 1.0, None, ALU.max))
                    act_step(lambda: nc.scalar.activation(din[:, :], din[:, :], ACT.Sqrt))
                    dve_step(v.reciprocal(din[:, :], din[:, :]))
                    dve_step(v.tensor_tensor(ag[:, :, 0:X_DIM], ag[:, :, 0:X_DIM],
                                             din[:, :].rearrange("p (r j) -> p r j", j=1).broadcast_to([P, HI, X_DIM]), ALU.mult))
                    dve_step(v.tensor_tensor(x1[:, :, :], x1[:, :, :], ag[:, :, 0:X_DIM], ALU.add))
                    norm_rows(nc, dve_step, act_step, ag[:, :, 0:X_DIM], x1[:, :, :], sqn[:, :, :], red[:, :], rinv[:, :], eps_c, HI)
                    for q in range(2):
                        ins = v.tensor_copy(hn[:, :, q, :], ag[:, 52 * q:52 * q + 52, 0:X_DIM])
                    ins.then_inc(norm_ok, 1)
                def turn_in(k):
                    dve.wait_ge(turned, k + 1)
                    if k:
                        dve.wait_ge(pre, k)
                    v.tensor_copy(ht[:, :], a_ps[0:32, :]).then_inc(turned_sb, 1)

                def finish(k):
                    c = slice(512 * k, 512 * k + 512)
                    dve.wait_ge(sd_ok, k + 1)
                    if k:
                        dve.wait_ge(rx_ok, k)
                    v.reciprocal(rs[:, :], sd[:, :]).then_inc(r_ok, 1)
                    dve.wait_ge(spread, k + 1)
                    if k:
                        dve.wait_ge(n_ok, k)
                    dve.wait_ge(yb_ok, k + 1)
                    v.tensor_tensor(t[:, :], yb[k % 2][:, :], r_ps[:, :], ALU.mult).then_inc(t_ok, 1)
                    dve.wait_ge(t_ok, k + 1)
                    if first:
                        v.tensor_scalar(node[:, c], t[:, :], col("g"), col("beta"), ALU.mult, ALU.add).then_inc(n_ok, 1)
                    else:
                        dve.wait_ge(nb_ok, k + 1)
                        v.scalar_tensor_tensor(node[:, c], t[:, :], col("g"), node[:, c], ALU.mult, ALU.add).then_inc(n_ok, 1)

                def results(k):
                    for q in range(2):
                        dve.wait_ge(o_ok, 2 * k + q + 1)
                        if k:
                            dve.wait_ge(st_out[q], 16 * stores(q, k - 1))
                        if dec:
                            blk = 52 * q + 4 * k
                            dve_step(v.tensor_tensor(res[q][:, :, :], o_ps[q][:, 0:4 * OUT_DIM].rearrange("p (i c) -> p i c", c=OUT_DIM),
                                                     x1[:, blk:blk + 4, :], ALU.add))
                            for i in range(4):
                                ins = v.tensor_tensor(res[q][:, i, :], res[q][:, i, :], dec[2][:, :], ALU.add)
                            ins.then_inc(st_ok, 1)
                        else:
                            v.tensor_copy(stage[q][:, :, :], o_ps[q][:, :].rearrange("p (i c) -> p i c", c=P)).then_inc(st_ok, 1)
                for k in range(NT):
                    if first:
                        turn_in(k)
                    if k:
                        finish(k - 1)
                        results(k - 1)
                finish(NT - 1)
                results(NT - 1)

            @block.scalar
            def _(act):
                for at, ins in jobs:
                    act.wait_ge(dstep, at)
                    ins().then_inc(astep, 1)
                def warm(func):
                    nc.scalar.activation(idle[:, :], eps_c[:, :], func)

                def decode(k):
                    act.wait_ge(d_ok, k + 1)
                    if k:
                        act.wait_ge(o_ok, 2 * k)
                    nc.scalar.activation(hd[:, :], a_ps[:, :], ACT.Silu, bias=vecs[:, DEC_B0:DEC_B0 + 1]).then_inc(hd_ok, 1)

                for k in range(NT):
                    c = slice(512 * k, 512 * k + 512)
                    warm(ACT.Silu)
                    act.wait_ge(pre, k + 1)
                    if k:
                        act.wait_ge(y_ok, k)
                    nc.scalar.activation(h[:, :], h_ps[:, :], ACT.Silu, bias=col("b0")).then_inc(h_ok, 1)
                    if not first:
                        nc.scalar.activation(node[:, c], node[:, c], ACT.Identity, bias=col("beta")).then_inc(nb_ok, 1)
                    act.wait_ge(y_ok, k + 1)
                    if k:
                        act.wait_ge(var_ok, k)
                    nc.scalar.activation(sq[:, :], y_ps[k % 2][:, :], ACT.Square, bias=col("b1")).then_inc(sq_ok, 1)
                    if k >= 2:
                        act.wait_ge(t_ok, k - 1)
                    nc.scalar.activation(yb[k % 2][:, :], y_ps[k % 2][:, :], ACT.Identity, bias=col("b1")).then_inc(yb_ok, 1)
                    if dec and k:
                        decode(k - 1)
                    act.wait_ge(var_ok, k + 1)
                    if k:
                        act.wait_ge(r_ok, k)
                    nc.scalar.activation(sd[:, :], var_ps[:, 0:2 * TILES], ACT.Sqrt, bias=eps_c[:, 0:1]).then_inc(sd_ok, 1)
                    act.wait_ge(r_ok, k + 1)
                    if k:
                        act.wait_ge(spread, k)
                    nc.scalar.activation(rs_x[:, :, :], rs[:, :].rearrange("p (i c) -> p i c", c=1).broadcast_to(
                        [P, 2 * TILES, D]), ACT.Copy).then_inc(rx_ok, 1)
                if dec:
                    decode(NT - 1)

            @block.sync
            def _(sp):
                for k in range(NT):
                    for q in range(2):
                        sp.wait_ge(st_ok, 2 * k + q + 1)
                        r0 = HALF * q + 512 * k
                        if dec:
                            full = max(0, min(4, (N_NODES - r0) // P))
                            if full:
                                sp.dma_start(dec[3][r0:r0 + P * full, :].rearrange("(i p) c -> p i c", p=P),
                                             res[q][:, 0:full, :]).then_inc(st_out[q], 16)
                            rest = N_NODES - r0 - P * full
                            if full < 4 and 0 < rest < P:
                                sp.dma_start(dec[3][r0 + P * full:N_NODES, :], res[q][0:rest, full, :]).then_inc(st_out[q], 16)
                            continue
                        for i, table in enumerate((ps_d, pr_d)):
                            sp.dma_start(table[r0:r0 + 512, :].rearrange("(i p) c -> p i c", p=P),
                                         stage[q][:, :, D * i:D * i + D]).then_inc(st_out[q], 16)
                for q in range(2):
                    sp.wait_ge(st_out[q], 16 * stores(q, NT - 1))


_W = ["node_enc", "edge_enc", "edge_blk", "node_blk"]
_WNAMES = [f"{k}_{p}" for k in _W for p in ("w0", "b0", "w1", "b1", "g", "beta")] + ["dec_w0", "dec_b0", "dec_w1", "dec_b1"]
_INS = ["x", "src", "dst", "edge_attr_8"] + ["L1_gnn_" + k for k in _WNAMES]


def kernel(**inputs):
    import numpy as np
    import concourse.bacc as bacc
    from concourse.bass_utils import run_bass_kernel_spmd

    nc = bacc.Bacc("TRN2", target_bir_lowering=False, num_devices=1)
    arrays, aps = {}, {}
    for name in _INS:
        a = np.ascontiguousarray(inputs[name])
        arrays[f"in_{name}"] = a
        aps[name] = nc.dram_tensor(f"in_{name}", a.shape, mybir.dt.from_np(a.dtype), kind="ExternalInput").ap()
    out = nc.dram_tensor("out_nodes", (N_NODES, OUT_DIM), F32, kind="ExternalOutput").ap()
    gnn_kernel(nc, aps["x"], aps["src"], aps["dst"], aps["edge_attr_8"], {k: aps["L1_gnn_" + k] for k in _WNAMES}, out)
    r = run_bass_kernel_spmd(nc, [arrays], core_ids=[0])
    return r.results[0]["out_nodes"]
```

```python
from contextlib import ExitStack, contextmanager

import concourse.bass as bass
from concourse import mybir

ALU = mybir.AluOpType
ACT = mybir.ActivationFunctionType
AX_X = mybir.AxisListType.X
F32 = mybir.dt.float32
BF16 = mybir.dt.bfloat16
I32 = mybir.dt.int32
U32 = mybir.dt.uint32
P = 128

N_NODES, N_EDGES, X_DIM, E_DIM, D, OUT_DIM, STEPS = 12500, 400000, 16, 8, 64, 16, 2
TILES = 4
CHUNK = TILES * P
ROUND = 2 * CHUNK
WIN = 64
HALF = 6656
NODES = 2 * HALF
HI = NODES // P
NT = HALF // 512
PAD_NODE = N_NODES
PAD_DST = 20000
LAST_BASE = WIN * (-(-N_NODES // WIN))
BLOCK_E = P * P
FAST_ROUNDS = 2 * -(-N_EDGES // (2 * ROUND))
FAST_BLOCKS = -(-FAST_ROUNDS * ROUND // BLOCK_E)
WINDOWS = -(-N_NODES // WIN)
SLOT_CHUNKS = -(-N_EDGES // CHUNK) + WINDOWS
MAX_BLOCKS = -(-SLOT_CHUNKS * CHUNK // BLOCK_E)
SLOTS = MAX_BLOCKS * BLOCK_E
MAX_ROUNDS = SLOTS // ROUND
EPS = 1e-5

VEC = ["edge_enc", "edge_blk0", "edge_blk1", "node_enc", "node_blk0", "node_blk1"]


def vcol(mlp, what):
    return 4 * VEC.index(mlp) + ["b0", "b1", "g", "beta"].index(what)


DEC_B0 = 4 * len(VEC)
NVEC = DEC_B0 + 1


@contextmanager
def semaphores(nc, tag):
    made = []

    def sem(name):
        made.append(nc.alloc_semaphore(name=tag + name))
        return made[-1]

    yield sem
    nc.clear_and_free_semaphores(made)
    nc.all_engine_barrier()


class Slot:

    def __init__(self, m, b):
        self.m, self.b = m, b

    def back(self, k):
        q = self.b - k
        return Slot(self.m + q // 2, q % 2)

    def exists(self):
        return not isinstance(self.m, int) or self.m >= 0

    @property
    def n(self):
        return self.m * 2 + self.b


def wait(eng, sem, slot, per=1):
    if slot.exists():
        eng.wait_ge(sem, slot.n * per + per)


def landed(eng, sems, slot, per=16):
    if slot.exists():
        eng.wait_ge(sems[slot.b], slot.m * per + per)


def held(eng, passed):
    eng.sem_inc(passed, 1)


def rounds(eng, body, count_sb, first=1):
    pairs = load_count(eng, count_sb, "pairs")
    for m in range(first):
        body(Slot(m, 0))
        body(Slot(m, 1))
    with eng.Fori(first, pairs) as m:
        body(Slot(m, 0))
        body(Slot(m, 1))
    return Slot(pairs, 0)


def load_count(eng, count_sb, what):
    i, low, high = dict(pairs=(1, FAST_ROUNDS // 2, MAX_ROUNDS // 2), blocks=(2, FAST_BLOCKS, MAX_BLOCKS))[what]
    return eng.value_load(count_sb[0:1, i:i + 1], min_val=0, max_val=high - low) + low


def gnn_kernel(nc, x, src, dst, edge_attr, w, out):
    with ExitStack() as ctx:
        def sb(name, shape, dt=F32):
            return ctx.enter_context(nc.sbuf_tensor(name, shape, dt))

        def dram(name, shape, dt=F32):
            return nc.dram_tensor(name, shape, dt, kind="Internal").ap()

        src_d = dram("src_slots", (SLOTS,), I32)
        dst_d = dram("dst_slots", (SLOTS,), I32)
        attr_d = dram("attr_slots", (SLOTS, E_DIM))
        base_d = dram("window_base", (2 * MAX_ROUNDS,), I32)
        local_d = dram("local_dst", (SLOTS,), BF16)
        lists_d = dram("tile_lists", (MAX_ROUNDS, P, 16), I32)
        xg_d = dram("sender_x", (NODES, 32))
        ps_d = dram("sender_part", (NODES, D))
        pr_d = dram("receiver_part", (NODES, D))
        edge_d = dram("edge_state", (MAX_ROUNDS, P, CHUNK))

        part_f = sb("part_f", [P, 1])
        part64 = sb("part64", [P, 1])
        row_f = sb("row_f", [P, P])
        row_bf = sb("row_bf", [P, P], BF16)
        ident = sb("ident", [P, P])
        mean_w = sb("mean_w", [P, P])
        sum_ab = sb("sum_ab", [P, 32])
        eps_c = sb("eps_c", [P, 1])
        vecs = sb("vecs", [P, NVEC])
        vmean = sb("vmean", [P, NVEC])
        dec_b1 = sb("dec_b1", [P, OUT_DIM])
        enc_w0 = sb("enc_w0", [64, TILES, P])
        nenc_w0 = sb("nenc_w0", [32, P])
        w1 = {k: sb("w1_" + k, [P, P]) for k in VEC}
        ew0 = [sb(f"ew0_{s}", [P, P]) for s in range(STEPS)]
        proj_w = [sb(f"proj_w{s}", [P, P]) for s in range(STEPS)]
        nw0 = [sb(f"nw0_{s}", [P, P]) for s in range(STEPS)]
        aw0 = [sb(f"aw0_{s}", [P, D]) for s in range(STEPS)]
        dec_w0 = sb("dec_w0", [P, P])
        dec_w1 = sb("dec_w1", [P, OUT_DIM])
        wmean = sb("wmean", [P, len(VEC)])
        agg = sb("agg", [P, NODES])
        node = sb("node", [P, HALF])
        x1 = sb("x1", [P, HI, X_DIM])
        base_sb = sb("base_sb", [1, 2 * MAX_ROUNDS], I32)
        count_sb = sb("count_sb", [1, 3], I32)
        deg = sb("deg", [P, HI])
        hx = sb("hx", [P, HI, X_DIM])

        def halves(eng, dst_tile, ap, sem):
            eng.dma_start(dst_tile[0:64, 0:64], ap).then_inc(sem, 16)
            eng.dma_start(dst_tile[64:128, 64:128], ap).then_inc(sem, 16)
            return 2

        n_ld = [0]
        with ExitStack() as c1:
            sem = c1.enter_context(semaphores(nc, "set_"))
            s_zero, s_ld, s_io, s_c, s_vm, s_cp, s_pad, s_dst, s_far, s_far_row, s_x0, s_x, s_var, s_dev, s_at = (sem(k) for k in (
                "zeroed", "weights_landed", "iota_done", "const_step", "vec_means", "lists_copied", "pad_made",
                "chunks_in", "far_ok", "far_row", "x_zeroed", "x_in", "x_variance", "x_deviation", "attr_copied"))
            n_full = N_EDGES // CHUNK // P
            n_more = N_EDGES // CHUNK - n_full * P
            n_rest = N_EDGES % CHUNK
            chunk_i = c1.enter_context(nc.sbuf_tensor("chunk_i", [P, n_full + 1, CHUNK], I32))
            chunk_f = c1.enter_context(nc.sbuf_tensor("chunk_f", [P, n_full + 1, CHUNK], F32))
            rest_i = c1.enter_context(nc.sbuf_tensor("rest_i", [1, n_rest], I32))
            rest_f = c1.enter_context(nc.sbuf_tensor("rest_f", [1, n_rest], F32))
            low = c1.enter_context(nc.sbuf_tensor("low", [P, n_full + 2], F32))
            high = c1.enter_context(nc.sbuf_tensor("high", [P, n_full + 2], F32))
            far = c1.enter_context(nc.sbuf_tensor("far", [P, 1], F32))
            first_f = c1.enter_context(nc.sbuf_tensor("first_f", [P, n_full + 2], F32))
            count_f = c1.enter_context(nc.sbuf_tensor("count_f", [1, 3], F32))
            sqx = c1.enter_context(nc.sbuf_tensor("sqx", [P, HI, X_DIM], F32))
            red = c1.enter_context(nc.sbuf_tensor("red_x", [P, HI], F32))
            rinv = c1.enter_context(nc.sbuf_tensor("rinv_x", [P, HI], F32))
            full = N_NODES // P
            far_ps = c1.enter_context(nc.psum_tensor("far_ps", [P, 512], F32))
            iota_i = c1.enter_context(nc.sbuf_tensor("iota_i", [P, P], I32))
            iota_p = c1.enter_context(nc.sbuf_tensor("iota_p", [P, 1], I32))
            tmp = c1.enter_context(nc.sbuf_tensor("tmp", [P, P], F32))
            hi_p = c1.enter_context(nc.sbuf_tensor("hi_p", [P, 1], F32))
            pad_s = c1.enter_context(nc.sbuf_tensor("pad_s", [P, 1024], I32))
            pad_t = c1.enter_context(nc.sbuf_tensor("pad_t", [P, 1024], I32))
            pad_a = c1.enter_context(nc.sbuf_tensor("pad_a", [P, 8 * 1024], F32))
            vm_ps = c1.enter_context(nc.psum_tensor("vm_ps", [P, 512], F32))
            zero_list = [enc_w0, nenc_w0, dec_w0, *w1.values(), *ew0, *nw0]
            with nc.Block() as block:
                @block.sync
                def _(sp):
                    sp.dma_start(chunk_i[:, 0:n_full, :], dst[0:n_full * P * CHUNK].rearrange(
                        "(k p e) -> p k e", p=P, e=CHUNK)).then_inc(s_dst, 16)
                    sp.wait_ge(s_pad, 1)
                    sp.dma_start(chunk_i[0:n_more, n_full, :], dst[n_full * P * CHUNK:N_EDGES - n_rest].rearrange(
                        "(p e) -> p e", e=CHUNK)).then_inc(s_dst, 16)
                    sp.dma_start(rest_i[:, :], dst[N_EDGES - n_rest:].rearrange("(a e) -> a e", a=1)).then_inc(s_dst, 16)

                    sp.dma_start(x1[:, 0:full, :], x[0:full * P, :].rearrange("(k p) c -> p k c", p=P)).then_inc(s_x, 16)
                    sp.wait_ge(s_x0, 1)
                    sp.dma_start(x1[0:N_NODES - full * P, full, :], x[full * P:, :]).then_inc(s_x, 16)

                    def load(t, ap, slow=False):
                        sp.dma_start(t, ap, allow_slow_non_contiguous=slow).then_inc(s_ld, 16)
                        n_ld[0] += 1

                    for what in ("b0", "b1", "g", "beta"):
                        for h in range(2):
                            for key in ("edge_enc", "node_enc"):
                                c = vcol(key, what)
                                load(vecs[64 * h:64 * h + 64, c:c + 1], w[f"{key}_{what}"].rearrange("(d a) -> d a", a=1))
                            for key in ("edge_blk", "node_blk"):
                                c, c_next = vcol(key + "0", what), vcol(key + "1", what)
                                load(vecs[64 * h:64 * h + 64, c:c_next + 1:c_next - c],
                                     w[f"{key}_{what}"].rearrange("s d -> d s"), slow=True)
                    for h in range(2):
                        load(vecs[64 * h:64 * h + 64, DEC_B0:DEC_B0 + 1], w["dec_b0"].rearrange("(d a) -> d a", a=1))
                        load(dec_w1[64 * h:64 * h + 64, :], w["dec_w1"])
                        for s in range(STEPS):
                            for q in range(2):
                                load(proj_w[s][64 * h:64 * h + 64, 64 * q:64 * q + 64],
                                     w["edge_blk_w0"][s, D * (q + 1):D * (q + 2), :])
                            load(aw0[s][64 * h:64 * h + 64, :], w["node_blk_w0"][s, D:2 * D, :])
                    load(dec_b1[:, :], w["dec_b1"].rearrange("(a d) -> a d", a=1).broadcast_to([P, OUT_DIM]))
                    sp.wait_ge(s_zero, len(zero_list))
                    for h in range(2):
                        for t in range(TILES):
                            r = 8 * (t + TILES * h)
                            load(enc_w0[r:r + 8, t, 64 * h:64 * h + 64], w["edge_enc_w0"])
                        load(nenc_w0[16 * h:16 * h + 16, 64 * h:64 * h + 64], w["node_enc_w0"])
                        q = slice(64 * h, 64 * h + 64)
                        load(dec_w0[q, q], w["dec_w0"])
                        load(w1["edge_enc"][q, q], w["edge_enc_w1"])
                        load(w1["node_enc"][q, q], w["node_enc_w1"])
                        for s in range(STEPS):
                            load(ew0[s][q, q], w["edge_blk_w0"][s, 0:D, :])
                            load(nw0[s][q, q], w["node_blk_w0"][s, 0:D, :])
                            load(w1[f"edge_blk{s}"][q, q], w["edge_blk_w1"][s])
                            load(w1[f"node_blk{s}"][q, q], w["node_blk_w1"][s])
                    sp.wait_ge(s_ld, 16 * n_ld[0])

                @block.scalar
                def _(act):
                    q = N_EDGES // P
                    act.dma_start(src_d[0:N_EDGES].rearrange("(p q) -> p q", p=P),
                                  src.rearrange("(p q) -> p q", p=P)).then_inc(s_cp, 16)
                    act.dma_start(dst_d[0:N_EDGES].rearrange("(p q) -> p q", p=P),
                                  dst.rearrange("(p q) -> p q", p=P)).then_inc(s_cp, 16)
                    q = (SLOTS - N_EDGES) // P
                    act.wait_ge(s_pad, 4)
                    act.dma_start(src_d[N_EDGES:].rearrange("(p q) -> p q", p=P), pad_s[:, 0:q]).then_inc(s_cp, 16)
                    act.dma_start(dst_d[N_EDGES:].rearrange("(p q) -> p q", p=P), pad_t[:, 0:q]).then_inc(s_cp, 16)
                    act.dma_start(attr_d[N_EDGES:, :].rearrange("(p q) c -> p (q c)", p=P),
                                  pad_a[:, 0:E_DIM * q]).then_inc(s_at, 16)
                    act.wait_ge(s_cp, 64)
                    act.dma_start(base_d.rearrange("(a c) -> a c", a=1), dst_d.rearrange("(c e) -> e c", e=CHUNK)[0:1, :],
                                  allow_slow_non_contiguous=True).then_inc(s_cp, 16)
                    act.wait_ge(s_dst, 48)
                    act.dma_start(attr_d[0:N_EDGES, :].rearrange("(p q) c -> p (q c)", p=P),
                                  edge_attr.rearrange("(p q) c -> p (q c)", p=P)).then_inc(s_at, 16)
                    act.wait_ge(s_var, 1)
                    nc.scalar.activation(rinv[:, :], red[:, :], ACT.Sqrt, bias=eps_c[:, 0:1], scale=1.0 / X_DIM).then_inc(s_dev, 1)
                    act.wait_ge(s_cp, 80)
                    act.wait_ge(s_at, 32)

                @block.gpsimd
                def _(pool):
                    nc.gpsimd.iota(iota_i[:, :], pattern=[[1, P]], base=0, channel_multiplier=0).then_inc(s_io, 1)
                    nc.gpsimd.iota(iota_p[:, :], pattern=[[0, 1]], base=0, channel_multiplier=1).then_inc(s_io, 1)
                    nc.gpsimd.memset(chunk_i[:, n_full, :], 0).then_inc(s_pad, 1)
                    nc.gpsimd.memset(x1[:, full:, :], 0.0).then_inc(s_x0, 1)
                    nc.gpsimd.memset(pad_s[:, :], PAD_NODE).then_inc(s_pad, 1)
                    nc.gpsimd.memset(pad_t[:, :], PAD_DST).then_inc(s_pad, 1)
                    nc.gpsimd.memset(pad_a[:, :], 0.0).then_inc(s_pad, 1)
                    for t in zero_list:
                        nc.gpsimd.memset(t[:], 0.0).then_inc(s_zero, 1)

                @block.vector
                def _(dve):
                    k = [0]

                    def step(ins):
                        k[0] += 1
                        ins.then_inc(s_c, 1)
                        dve.wait_ge(s_c, k[0])

                    v = nc.vector
                    dve.wait_ge(s_io, 2)
                    step(v.memset(eps_c[:, :], EPS))
                    step(v.tensor_copy(row_f[:, :], iota_i[:, :]))
                    step(v.tensor_copy(row_bf[:, :], iota_i[:, :]))
                    step(v.tensor_copy(part_f[:, :], iota_p[:, :]))
                    step(v.tensor_scalar(ident[:, :], row_f[:, :], part_f[:, 0:1], None, ALU.is_equal))
                    step(v.tensor_scalar(hi_p[:, :], part_f[:, :], 64.0, None, ALU.is_ge))
                    step(v.scalar_tensor_tensor(part64[:, :], hi_p[:, :], -64.0, part_f[:, :], ALU.mult, ALU.add))
                    step(v.tensor_scalar(tmp[:, :], row_f[:, :], 64.0, None, ALU.is_ge))
                    step(v.tensor_scalar(mean_w[:, :], tmp[:, :], hi_p[:, 0:1], 1.0 / D, ALU.is_equal, ALU.mult))
                    step(v.tensor_scalar(sum_ab[:, :], row_f[:, 0:32], part64[:, 0:1], None, ALU.is_equal))
                    dve.wait_ge(s_dst, 48)
                    step(v.tensor_copy(chunk_f[:, :, :], chunk_i[:, :, :]))
                    step(v.tensor_copy(rest_f[:, :], rest_i[:, :]))
                    for t in (low, high, first_f):
                        step(v.memset(t[:, :], 0.0))
                    for t, op in ((low, ALU.min), (high, ALU.max)):
                        step(v.tensor_reduce(t[:, 0:n_full + 1], chunk_f[:, :, :], AX_X, op))
                        step(v.tensor_reduce(t[0:1, n_full + 1:], rest_f[:, :], AX_X, op))
                    step(v.tensor_copy(first_f[:, 0:n_full + 1], chunk_f[:, :, 0:1].rearrange("p k e -> p (k e)")))
                    step(v.tensor_copy(first_f[0:1, n_full + 1:], rest_f[:, 0:1]))
                    step(v.tensor_tensor(high[:, :], high[:, :], first_f[:, :], ALU.subtract))
                    step(v.tensor_tensor(low[:, :], first_f[:, :], low[:, :], ALU.subtract))
                    step(v.scalar_tensor_tensor(high[:, :], low[:, :], float(WIN), high[:, :], ALU.mult, ALU.max))
                    step(v.tensor_reduce(far[:, :], high[:, :], AX_X, ALU.max))
                    v.memset(count_f[:, :], 0.0).then_inc(s_far, 1)
                    dve.wait_ge(s_far_row, 1)
                    step(v.tensor_reduce(far[0:1, :], far_ps[0:1, 0:P], AX_X, ALU.max))
                    dve.wait_ge(s_far, 1)
                    step(v.tensor_scalar(count_f[:, 0:1], far[0:1, :], float(WIN), None, ALU.is_ge))
                    for i, (fast, most) in enumerate(((FAST_ROUNDS // 2, MAX_ROUNDS // 2), (FAST_BLOCKS, MAX_BLOCKS))):
                        step(v.tensor_scalar(count_f[:, i + 1:i + 2], count_f[:, 0:1], float(most - fast), None, ALU.mult))
                    step(v.tensor_copy(count_sb[:, :], count_f[:, :]))
                    dve.wait_ge(s_x, 32)
                    dve.wait_ge(s_x0, 1)
                    norm_rows(nc, step, lambda act_part: dve.wait_ge(s_dev, 1), hx[:, :, :], x1[:, :, :], sqx[:, :, :],
                              red[:, :], rinv[:, :], eps_c, HI, s_var)
                    dve.wait_ge(s_ld, 16 * n_ld[0])
                    for i, name in enumerate(VEC):
                        step(v.tensor_reduce(wmean[:, i:i + 1], w1[name][:, :], AX_X, ALU.add))
                    step(v.tensor_scalar(wmean[:, :], wmean[:, :], -1.0 / D, None, ALU.mult))
                    for i, name in enumerate(VEC):
                        for h in range(2):
                            q = slice(64 * h, 64 * h + 64)
                            step(v.tensor_scalar(w1[name][q, q], w1[name][q, q], wmean[q, i:i + 1], None, ALU.add))
                    dve.wait_ge(s_vm, 1)
                    step(v.tensor_copy(vmean[:, :], vm_ps[:, 0:NVEC]))
                    for name in VEC:
                        c = vcol(name, "b1")
                        step(v.tensor_tensor(vecs[:, c:c + 1], vecs[:, c:c + 1], vmean[:, c:c + 1], ALU.subtract))

                @block.tensor
                def _(pe):
                    pe.wait_ge(s_far, 1)
                    nc.tensor.matmul(far_ps[0:1, 0:P], far[:, 0:1], ident[:, :], start=True, stop=True).then_inc(s_far_row, 1)
                    pe.wait_ge(s_ld, 16 * n_ld[0])
                    nc.tensor.matmul(vm_ps[:, 0:NVEC], mean_w[:, :], vecs[:, :], start=True, stop=True).then_inc(s_vm, 1)

        sort_by_window(nc, src, dst, edge_attr, src_d, dst_d, attr_d, base_d, count_sb, row_f, part_f, ident)
        edge_lists(nc, src_d, dst_d, base_d, local_d, lists_d, base_sb, deg, row_bf, ident, count_sb)
        scaled_senders(nc, hx, deg, xg_d)
        first_layer(nc, lists_d, attr_d, xg_d, edge_d, base_sb, agg, enc_w0, w1["edge_enc"], mean_w, ident,
                    row_f, vecs, eps_c, count_sb)
        vv = dict(nc=nc, agg=agg, node=node, x1=x1, vecs=vecs, mean_w=mean_w, ident=ident, eps_c=eps_c,
                  ps_d=ps_d, pr_d=pr_d)
        node_phase(**vv, mlp="node_enc", w_in=nenc_w0, w_mid=w1["node_enc"], proj=proj_w[0], sum_ab=sum_ab)
        for s in range(STEPS):
            edge_step(nc, lists_d, local_d, edge_d, ps_d, pr_d, base_sb, agg, ew0[s], w1[f"edge_blk{s}"], mean_w,
                      ident, row_f, part64, vecs, eps_c, f"edge_blk{s}", s < STEPS - 1, count_sb)
            node_phase(**vv, mlp=f"node_blk{s}", w_in=nw0[s], w_mid=w1[f"node_blk{s}"], w_agg=aw0[s],
                       proj=proj_w[s + 1] if s < STEPS - 1 else None,
                       dec=(dec_w0, dec_w1, dec_b1, out) if s == STEPS - 1 else None)


def sort_by_window(nc, src, dst, edge_attr, src_d, dst_d, attr_d, base_d, count_sb, row_f, part_f, ident):
    with ExitStack() as ctx:
        def sb(name, shape, dt=F32):
            return ctx.enter_context(nc.sbuf_tensor("so_" + name, shape, dt))

        def ps(name):
            return ctx.enter_context(nc.psum_tensor("so_ps_" + name, [P, 512], F32))

        sem = ctx.enter_context(semaphores(nc, "so_"))
        W = 2 * P
        N_TILES = N_EDGES // P
        FILL = 8
        src_all, dst_all = sb("src_all", [P, N_TILES], I32), sb("dst_all", [P, N_TILES], I32)
        win_f = sb("win_f", [P, N_TILES])
        row_i, row_w = sb("row_i", [P, 2 * MAX_ROUNDS], I32), sb("row_w", [P, 2 * MAX_ROUNDS])
        ones = sb("ones", [P, P])
        before = sb("before", [P, P])
        fill_s, fill_t = (sb(k, [P, SLOTS // P // FILL], I32) for k in ("fill_s", "fill_t"))
        fill_a = sb("fill_a", [P, E_DIM * SLOTS // P // FILL])
        onehot, picked = sb("onehot", [P, W]), sb("picked", [P, W])
        size_i, size_f = sb("size_i", [P, 2], I32), sb("size_f", [P, 2])
        start = sb("start", [P, 2])
        cursor = sb("cursor", [1, W])
        begun = [sb(f"begun{i}", [P, 2 * MAX_ROUNDS]) for i in range(2)]
        base = sb("base", [1, 2 * MAX_ROUNDS], I32)
        base_f = sb("base_f", [1, 2 * MAX_ROUNDS])
        pos_f, pos = sb("pos_f", [P, 1]), sb("pos", [P, 1], I32)
        s_val, d_val, a_val = sb("s_val", [P, 1], I32), sb("d_val", [P, 1], I32), sb("a_val", [P, E_DIM])
        size_ps, start_ps, rank_ps, more_ps = ps("size"), ps("start"), ps("rank"), ps("more")
        base_ps = [ps("base0"), ps("base1")]
        made, fills, edges_in, attr_in, dstep, onehot_ok, binned, sized, started, curs_ok, based, base_out, ranked, pos_step, pos_ok = (
            sem(k) for k in ("made", "fills", "edges_in", "attr_in", "dve_step", "onehot_ok", "binned", "sized", "started",
                             "cursor_ok", "based", "base_out", "ranked", "pos_step", "pos_ok"))
        put = [sem(f"put_{k}") for k in ("src", "dst", "attr")]
        passed = sem("passed")
        attr_v = edge_attr.rearrange("(p t) c -> p t c", t=N_TILES)
        with nc.Block() as block:
            @block.sync
            def _(sp):
                sort = sp.value_load(count_sb[0:1, 0:1], min_val=0, max_val=1)
                with sp.If(sort > 0):
                    sp.dma_start(src_all[:, :], src.rearrange("(p t) -> p t", t=N_TILES)).then_inc(edges_in, 16)
                    sp.dma_start(dst_all[:, :], dst.rearrange("(p t) -> p t", t=N_TILES)).then_inc(edges_in, 16)
                    sp.wait_ge(made, 5)
                    for table, fill in ((src_d, fill_s), (dst_d, fill_t)):
                        for part in range(FILL):
                            sp.dma_start(table.rearrange("(f p q) -> f p q", f=FILL, p=P)[part], fill[:, :]).then_inc(fills, 16)
                    for part in range(FILL):
                        sp.dma_start(attr_d.rearrange("(f p q) c -> f p (q c)", f=FILL, p=P)[part],
                                     fill_a[:, :]).then_inc(fills, 16)
                    sp.wait_ge(based, 1)
                    sp.dma_start(base_d.rearrange("(a c) -> a c", a=1), base[:, :]).then_inc(base_out, 16)

                    def body(t, first):
                        if not first:
                            sp.wait_ge(put[2], t * 16)
                            held(sp, passed)
                        sp.dma_start(a_val[:, :], attr_v[:, bass.ds(t, 1), :].rearrange("p t c -> p (t c)"),
                                     allow_slow_non_contiguous=True).then_inc(attr_in, 16)

                    body(0, True)
                    with sp.Fori(1, N_TILES) as t:
                        body(t, False)
                    sp.wait_ge(fills, 3 * FILL * 16)
                    sp.wait_ge(base_out, 16)
                    for arrived in put:
                        sp.wait_ge(arrived, N_TILES * 16)

            @block.gpsimd
            def _(pool):
                sort = pool.value_load(count_sb[0:1, 0:1], min_val=0, max_val=1)
                with pool.If(sort > 0):
                    nc.gpsimd.memset(fill_s[:, :], PAD_NODE).then_inc(made, 1)
                    nc.gpsimd.memset(fill_t[:, :], PAD_DST).then_inc(made, 1)
                    nc.gpsimd.memset(fill_a[:, :], 0.0).then_inc(made, 1)
                    nc.gpsimd.memset(ones[:, :], 1.0).then_inc(made, 1)
                    nc.gpsimd.iota(row_i[:, :], pattern=[[1, 2 * MAX_ROUNDS]], base=0, channel_multiplier=0).then_inc(made, 1)
                    pool.wait_ge(fills, 3 * FILL * 16)

                    def body(t):
                        pool.wait_ge(pos_ok, t + 1)
                        pool.wait_ge(attr_in, t * 16 + 16)
                        held(pool, passed)
                        for table, value, arrived in ((src_d.rearrange("(e a) -> e a", a=1), s_val, put[0]),
                                                      (dst_d.rearrange("(e a) -> e a", a=1), d_val, put[1]),
                                                      (attr_d, a_val, put[2])):
                            pool.indirect_dma_start(
                                out=table, out_offset=bass.IndirectOffsetOnAxis(ap=pos[:, 0:1].bitcast(U32), axis=0),
                                in_=value[:, :], in_offset=None).then_inc(arrived, 16)

                    body(0)
                    with pool.Fori(1, N_TILES) as t:
                        body(t)

            @block.tensor
            def _(pe):
                sort = pe.value_load(count_sb[0:1, 0:1], min_val=0, max_val=1)
                with pe.If(sort > 0):
                    pe.wait_ge(dstep, 4)

                    def count(t, first):
                        pe.wait_ge(onehot_ok, t + 1)
                        for q in range(2):
                            ins = nc.tensor.matmul(size_ps[:, q:q + 1], onehot[:, P * q:P * q + P], ones[:, 0:1],
                                                   start=first and q == 0, stop=False, skip_group_check=True)
                        ins.then_inc(binned, 1)

                    count(0, True)
                    with pe.Fori(1, N_TILES) as t:
                        count(t, False)
                    pe.wait_ge(sized, 1)
                    nc.tensor.matmul(start_ps[:, 0:1], before[:, :], size_f[:, 0:1], start=True, stop=True)
                    nc.tensor.matmul(start_ps[:, 1:2], before[:, :], size_f[:, 1:2], start=True, stop=False)
                    nc.tensor.matmul(start_ps[:, 1:2], ones[:, :], size_f[:, 0:1], start=False, stop=True).then_inc(started, 1)
                    pe.wait_ge(curs_ok, 1)
                    for q in range(2):
                        nc.tensor.matmul(rank_ps[0:1, P * q:P * q + P], start[:, q:q + 1], ident[:, :], start=True, stop=True)
                    for half in range(2):
                        c = slice(MAX_ROUNDS * half, MAX_ROUNDS * half + MAX_ROUNDS)
                        for q in range(2):
                            ins = nc.tensor.matmul(base_ps[half][0:1, 0:MAX_ROUNDS], ones[:, 0:1], begun[q][:, c],
                                                   start=q == 0, stop=q == 1)
                    ins.then_inc(started, 1)

                    def rank(t):
                        pe.wait_ge(onehot_ok, t + (N_TILES + 1))
                        nc.tensor.matmul(rank_ps[:, 0:W], before[:, :], onehot[:, :], start=True, stop=False)
                        nc.tensor.matmul(rank_ps[:, 0:W], ones[0:1, :], cursor[:, :], start=False, stop=True)
                        nc.tensor.matmul(more_ps[0:1, 0:W], ones[:, 0:1], onehot[:, :], start=True, stop=True).then_inc(ranked, 1)

                    rank(0)
                    with pe.Fori(1, N_TILES) as t:
                        rank(t)

            @block.vector
            def _(dve):
                v = nc.vector
                sort = dve.value_load(count_sb[0:1, 0:1], min_val=0, max_val=1)
                with dve.If(sort > 0):
                    k = [0]

                    def step(ins):
                        k[0] += 1
                        ins.then_inc(dstep, 1)
                        dve.wait_ge(dstep, k[0])

                    dve.wait_ge(made, 5)
                    dve.wait_ge(edges_in, 32)
                    step(v.tensor_copy(row_w[:, :], row_i[:, :]))
                    step(v.tensor_scalar(before[:, :], row_f[:, :], part_f[:, 0:1], None, ALU.is_gt))
                    step(v.tensor_scalar(win_f[:, :].bitcast(I32), dst_all[:, :], 6, None, ALU.logical_shift_right))
                    step(v.tensor_copy(win_f[:, :], win_f[:, :].bitcast(I32)))

                    def bins(t):
                        v.tensor_scalar(onehot[:, :], row_w[:, 0:W], win_f[:, bass.ds(t, 1)], None,
                                        ALU.is_equal).then_inc(onehot_ok, 1)

                    bins(0)
                    with dve.Fori(1, N_TILES) as t:
                        dve.wait_ge(binned, t)
                        bins(t)
                    dve.wait_ge(binned, N_TILES)
                    step(v.tensor_copy(size_i[:, :], size_ps[:, 0:2]))
                    step(v.tensor_scalar(size_i[:, :], size_i[:, :], CHUNK - 1, None, ALU.add))
                    step(v.tensor_scalar(size_i[:, :], size_i[:, :], CHUNK.bit_length() - 1, None, ALU.logical_shift_right))
                    v.tensor_copy(size_f[:, :], size_i[:, :]).then_inc(sized, 1)
                    dve.wait_ge(started, 1)
                    step(v.tensor_copy(start[:, :], start_ps[:, 0:2]))
                    for q in range(2):
                        ins = v.tensor_scalar(begun[q][:, :], row_w[:, :], start[:, q:q + 1], None, ALU.is_ge)
                    ins.then_inc(curs_ok, 1)
                    dve.wait_ge(started, 2)
                    step(v.tensor_scalar(cursor[:, :], rank_ps[0:1, 0:W], float(CHUNK), None, ALU.mult))
                    for half in range(2):
                        step(v.tensor_scalar(base_f[:, MAX_ROUNDS * half:MAX_ROUNDS * half + MAX_ROUNDS],
                                             base_ps[half][0:1, 0:MAX_ROUNDS], float(WIN), float(-WIN), ALU.mult, ALU.add))
                    v.tensor_scalar(base[:, :], base_f[:, :], float(LAST_BASE), None, ALU.min).then_inc(based, 1)

                    def place(t, first):
                        if not first:
                            dve.wait_ge(curs_ok, t + 1)
                            for arrived in put:
                                dve.wait_ge(arrived, t * 16)
                                held(dve, passed)
                        bins_at = bass.ds(t, 1)
                        v.tensor_copy(s_val[:, :], src_all[:, bins_at])
                        v.tensor_copy(d_val[:, :], dst_all[:, bins_at])
                        bins(t)
                        dve.wait_ge(ranked, t + 1)
                        v.tensor_tensor(picked[:, :], onehot[:, :], rank_ps[:, 0:W], ALU.mult).then_inc(pos_step, 1)
                        dve.wait_ge(pos_step, t * 2 + 1)
                        v.tensor_reduce(pos_f[:, :], picked[:, :], AX_X, ALU.add).then_inc(pos_step, 1)
                        dve.wait_ge(pos_step, t * 2 + 2)
                        v.tensor_copy(pos[:, :], pos_f[:, :]).then_inc(pos_ok, 1)
                        v.tensor_tensor(cursor[:, :], cursor[:, :], more_ps[0:1, 0:W], ALU.add).then_inc(curs_ok, 1)

                    place(0, True)
                    with dve.Fori(1, N_TILES) as t:
                        place(t, False)


def edge_lists(nc, src_d, dst_d, base_d, local_d, lists_d, base_sb, deg, row_bf, ident, count_sb):
    with ExitStack() as ctx:
        def sb(name, shape, dt=F32):
            return ctx.enter_context(nc.sbuf_tensor("el_" + name, shape, dt))

        sem = ctx.enter_context(semaphores(nc, "el_"))

        base_col = sb("base_col", [P, MAX_BLOCKS], I32)
        base_f = sb("base_f", [P, MAX_BLOCKS])
        srow = sb("srow", [P, P], I32)
        drow = sb("drow", [P, P], I32)
        srow_f = sb("srow_f", [P, P])
        local_f = sb("local_f", [P, P])
        local_bf = sb("local_bf", [P, P], BF16)
        lists = sb("lists", [P, 16, 16], I32)
        s_lo = sb("s_lo", [P, P], I32)
        s_hi = sb("s_hi", [P, P], I32)
        lo_b = sb("lo_b", [P, P], BF16)
        hi_b = sb("hi_b", [P, P], BF16)
        GT = 16
        NHI = -(-(N_NODES + 1) // P)
        value = sb("value", [P, P, GT], BF16)
        one_lo = [sb(f"one_lo{i}", [P, P, GT], BF16) for i in range(2)]
        one_hi = [sb(f"one_hi{i}", [P, NHI, GT], BF16) for i in range(2)]
        zeros = sb("zeros", [P, P], BF16)
        t_ps = ctx.enter_context(nc.psum_tensor("el_tps", [P, 512], F32))
        d_ps = ctx.enter_context(nc.psum_tensor("el_dps", [P, 512], F32))
        base_in, base_ok, rows_in, rows_f, tr_done, lists_ok, idx_ok, lists_out, onehots, hist, local_ok, zero_ok, deg_ok = (
            sem(k) for k in ("base_in", "base_ok", "rows_in", "rows_f", "transposed", "lists_ok", "idx_ok", "lists_out",
                             "onehots", "hist", "local_ok", "zero_ok", "deg_ok"))
        passed = sem("passed")
        G = P // GT
        with nc.Block() as block:
            @block.sync
            def _(sp):
                sp.dma_start(base_sb[0:1, :], base_d.rearrange("(a c) -> a c", a=1)).then_inc(base_in, 16)
                for j in range(TILES):
                    sp.dma_start(base_col[j:P:TILES, :], base_d.rearrange("(k c) -> c k", k=MAX_BLOCKS),
                                 allow_slow_non_contiguous=True).then_inc(base_in, 16)
                blocks = load_count(sp, count_sb, "blocks")

                def body(k):
                    at = bass.ds(k, 1)
                    if not (isinstance(k, int) and k == 0):
                        for waited, value in ((tr_done, k), (local_ok, k), (lists_out, k * 32)):
                            sp.wait_ge(waited, value)
                            held(sp, passed)
                    sp.dma_start(srow[:, :], src_d.rearrange("(k t p) -> k t p", p=P, t=P)[at].rearrange(
                        "a t p -> (a t) p")).then_inc(rows_in, 16)
                    sp.dma_start(drow[:, :], dst_d.rearrange("(k t p) -> k t p", p=P, t=P)[at].rearrange(
                        "a t p -> (a t) p")).then_inc(rows_in, 16)
                    sp.wait_ge(local_ok, k + 1)
                    held(sp, passed)
                    sp.dma_start(local_d.rearrange("(k t p) -> k t p", p=P, t=P)[at].rearrange(
                        "a t p -> (a t) p"), local_bf[:, :]).then_inc(lists_out, 16)
                    sp.wait_ge(lists_ok, k + 1)
                    held(sp, passed)
                    sp.dma_start(lists_d.rearrange("r p c -> p r c")[:, bass.ds(k * 16, 16), :],
                                 lists[:, :, :]).then_inc(lists_out, 16)

                body(0)
                with sp.Fori(1, blocks) as k:
                    body(k)
                sp.wait_ge(lists_out, blocks * 32)
                held(sp, passed)

            @block.vector
            def _(dve):
                v = nc.vector
                v.memset(zeros[:, :], 0.0).then_inc(zero_ok, 1)
                v.tensor_copy(value[:, :, :], row_bf[:, :].rearrange("p (w t) -> p w t", t=1).broadcast_to(
                    [P, P, GT])).then_inc(zero_ok, 1)
                v.memset(deg[:, NHI:], 0.0).then_inc(zero_ok, 1)
                dve.wait_ge(zero_ok, 3)
                dve.wait_ge(base_in, 16 * (TILES + 1))
                v.tensor_scalar(base_sb[:, :], base_sb[:, :], LAST_BASE, None, ALU.min)
                v.tensor_scalar(base_f[:, :], base_col[:, :], LAST_BASE, None, ALU.min).then_inc(base_ok, 1)
                dve.wait_ge(base_ok, 1)

                def wide(a, n):
                    return a.rearrange("p (w t) -> p w t", w=1).broadcast_to([P, n, GT])

                def body(k):
                    later = not (isinstance(k, int) and k == 0)
                    dve.wait_ge(rows_in, k * 32 + 32)
                    if later:
                        dve.wait_ge(lists_out, k * 32)
                        dve.wait_ge(tr_done, k)
                    v.tensor_copy(srow_f[:, :], srow[:, :])
                    v.tensor_tensor(local_f[:, :], drow[:, :], base_f[:, bass.ds(k, 1)].broadcast_to([P, P]),
                                    ALU.subtract).then_inc(rows_f, 1)
                    dve.wait_ge(rows_f, k + 1)
                    v.tensor_copy(local_bf[:, :], local_f[:, :]).then_inc(local_ok, 1)
                    dve.wait_ge(tr_done, k + 1)
                    v.tensor_copy(lists[:, :, 0:8], t_ps[:, 0:P].rearrange("p (r j) -> p r j", j=8)).then_inc(idx_ok, 1)
                    v.tensor_copy(lists[:, :, 8:16].bitcast(F32),
                                  t_ps[:, P:2 * P].rearrange("p (r j) -> p r j", j=8)).then_inc(lists_ok, 1)
                    dve.wait_ge(idx_ok, k * 3 + 1)
                    v.tensor_scalar(s_lo[:, :].rearrange("p (r j) -> p r j", j=8), lists[:, :, 0:8], 127, None,
                                    ALU.bitwise_and)
                    v.tensor_scalar(s_hi[:, :].rearrange("p (r j) -> p r j", j=8), lists[:, :, 0:8], 7, None,
                                    ALU.logical_shift_right).then_inc(idx_ok, 1)
                    dve.wait_ge(idx_ok, k * 3 + 2)
                    v.tensor_copy(lo_b[:, :], s_lo[:, :])
                    v.tensor_copy(hi_b[:, :], s_hi[:, :]).then_inc(idx_ok, 1)
                    dve.wait_ge(idx_ok, k * 3 + 3)
                    for g in range(G):
                        if g >= 2 or later:
                            dve.wait_ge(hist, k * G + (g - 1))
                        at = slice(GT * g, GT * g + GT)
                        v.tensor_tensor(one_lo[g % 2][:, :, :], value[:, :, :], wide(lo_b[:, at], P), ALU.is_equal)
                        v.tensor_tensor(one_hi[g % 2][:, :, :], value[:, 0:NHI, :], wide(hi_b[:, at], NHI),
                                        ALU.is_equal).then_inc(onehots, 1)

                blocks = load_count(dve, count_sb, "blocks")
                body(0)
                with dve.Fori(1, blocks) as k:
                    body(k)
                dve.wait_ge(deg_ok, 1)
                v.tensor_copy(deg[:, 0:NHI], d_ps[:, 0:NHI]).then_inc(zero_ok, 1)
                dve.wait_ge(zero_ok, 4)

            @block.tensor
            def _(pe):
                pe.wait_ge(zero_ok, 3)
                nc.tensor.matmul(d_ps[:, 0:NHI], zeros[:, :], zeros[:, 0:NHI], start=True, stop=False, skip_group_check=True)

                def body(k):
                    pe.wait_ge(rows_f, k + 1)
                    if not (isinstance(k, int) and k == 0):
                        pe.wait_ge(idx_ok, k * 3)
                        pe.wait_ge(lists_ok, k)
                    nc.tensor.transpose(t_ps[:, 0:P], srow_f[:, :], ident[:, :])
                    nc.tensor.transpose(t_ps[:, P:2 * P], local_f[:, :], ident[:, :]).then_inc(tr_done, 1)
                    for g in range(G):
                        pe.wait_ge(onehots, k * G + (g + 1))
                        for j in range(GT):
                            ins = nc.tensor.matmul(d_ps[:, 0:NHI], one_lo[g % 2][:, :, j], one_hi[g % 2][:, :, j],
                                                   start=False, stop=False, skip_group_check=True)
                        ins.then_inc(hist, 1)

                blocks = load_count(pe, count_sb, "blocks")
                body(0)
                with pe.Fori(1, blocks) as k:
                    body(k)
                nc.tensor.matmul(d_ps[:, 0:NHI], zeros[:, :], zeros[:, 0:NHI], start=False, stop=True,
                                 skip_group_check=True).then_inc(deg_ok, 1)


def norm_rows(nc, dve_step, act_step, h, t_in, sq, red, rinv, eps_c, n, var_ok=None):
    v = nc.vector
    bc = lambda a: a.rearrange("p (r j) -> p r j", j=1).broadcast_to([P, n, X_DIM])
    dve_step(v.tensor_reduce(red, t_in, AX_X, ALU.add))
    dve_step(v.tensor_scalar(red, red, 1.0 / X_DIM, None, ALU.mult))
    dve_step(v.tensor_tensor(h, t_in, bc(red), ALU.subtract))
    dve_step(v.tensor_tensor(sq, h, h, ALU.mult))
    ins = v.tensor_reduce(red, sq, AX_X, ALU.add)
    if var_ok is None:
        dve_step(ins)
    else:
        ins.then_inc(var_ok, 1)
    act_step(lambda: nc.scalar.activation(rinv, red, ACT.Sqrt, bias=eps_c[:, 0:1], scale=1.0 / X_DIM))
    dve_step(v.reciprocal(rinv, rinv))
    dve_step(v.tensor_tensor(h, h, bc(rinv), ALU.mult))
    dve_step(v.tensor_scalar(h, h, 0.0, None, ALU.max))


def scaled_senders(nc, hx, deg, xg_d):
    with ExitStack() as ctx:
        def sb(name, shape, dt=F32):
            return ctx.enter_context(nc.sbuf_tensor("ss_" + name, shape, dt))

        sem = ctx.enter_context(semaphores(nc, "ss_"))

        rs, rows = sb("rs", [P, HI]), sb("rows", [P, HI, 32])
        dstep, root_ok, zeroed, rows_ok, out_done = (sem(k) for k in ("dve_step", "root_ok", "zeroed", "rows_ok", "rows_out"))
        with nc.Block() as block:
            @block.gpsimd
            def _(pool):
                nc.gpsimd.memset(rows[:, :, X_DIM:], 0.0).then_inc(zeroed, 1)

            @block.sync
            def _(sp):
                sp.wait_ge(rows_ok, 1)
                sp.dma_start(xg_d.rearrange("(k p) c -> p k c", p=P), rows[:, :, :]).then_inc(out_done, 16)
                sp.wait_ge(out_done, 16)

            @block.vector
            def _(dve):
                v = nc.vector
                v.tensor_scalar(rs[:, :], deg[:, :], 1.0, None, ALU.max).then_inc(dstep, 1)
                dve.wait_ge(zeroed, 1)
                v.memset(rows[:, :, X_DIM:X_DIM + 1], 1.0)
                dve.wait_ge(root_ok, 1)
                v.reciprocal(rs[:, :], rs[:, :]).then_inc(dstep, 1)
                dve.wait_ge(dstep, 2)
                v.tensor_tensor(rows[:, :, 0:X_DIM], hx[:, :, :],
                                rs[:, :].rearrange("p (r j) -> p r j", j=1).broadcast_to([P, HI, X_DIM]),
                                ALU.mult).then_inc(rows_ok, 1)

            @block.scalar
            def _(act):
                act.wait_ge(dstep, 1)
                nc.scalar.activation(rs[:, :], rs[:, :], ACT.Sqrt).then_inc(root_ok, 1)


def first_layer(nc, lists_d, attr_d, xg_d, edge_d, base_sb, agg, enc_w0, w_mid, mean_w, ident, row_f, vecs, eps_c, count_sb):
    with ExitStack() as ctx:
        def sb(name, shape, dt=F32):
            return ctx.enter_context(nc.sbuf_tensor("fl_" + name, shape, dt))

        def two(name, shape, dt=F32):
            return [sb(f"{name}{i}", shape, dt) for i in range(2)]

        def ps(name):
            return ctx.enter_context(nc.psum_tensor("fl_" + name, [P, 512], F32))

        sem = ctx.enter_context(semaphores(nc, "fl_"))

        idx = two("idx", [P, 8], I32)
        lst = two("lst", [P, 8], I32)
        attr = two("attr", [P, 8, E_DIM])
        attr_t = sb("attr_t", [64, P])
        g = two("g", [P, 8, 32])
        ohb = two("ohb", [P, 8, WIN])
        h, sq, t = (sb(k, [P, CHUNK]) for k in ("h", "sq", "t"))
        sd, rs = sb("sd", [P, 2 * TILES]), sb("rs", [P, 2 * TILES])
        rs_x = two("rs_x", [P, 2 * TILES, D])
        yb = two("yb", [P, CHUNK])
        idle = sb("idle", [P, 1])
        e = two("e", [P, CHUNK])
        at_ps, h_ps, var_ps, agg_ps, r_ps = ps("atps"), ps("hps"), ps("varps"), ps("aggps"), ps("rps")
        y_ps = [ps("yps0"), ps("yps1")]
        idx_in, list_in, attr_in, g_in, e_out = ([sem(f"{k}{i}") for i in range(2)] for k in ("idx_in", "list_in", "attr_in", "g_in", "e_out"))
        passed = sem("passed")
        zeroed, turned, turned_sb, pre, h_ok, y_ok, sq_ok, yb_ok, var_ok, sd_ok, r_ok, rx_ok, spread, t_ok, e_ok, oh_ok, sum_ok, added = (
            sem(k) for k in ("zeroed", "turned", "turned_sb", "pre", "h_ok", "y_ok", "sq_ok", "yb_ok", "var_ok", "sd_ok", "r_ok", "rx_ok", "spread",
                             "t_ok", "e_ok", "oh_ok", "sum_ok", "added"))
        attr_v = attr_d.rearrange("(r j p) c -> r p j c", p=P, j=8)
        col = lambda what: vecs[:, vcol("edge_enc", what):vcol("edge_enc", what) + 1]
        with nc.Block() as block:
            @block.sync
            def _(sp):
                def store(n):
                    if n.exists():
                        wait(sp, e_ok, n)
                        sp.dma_start(edge_d[bass.ds(n.n, 1)].rearrange("a p c -> (a p) c"), e[n.b][:, :]).then_inc(e_out[n.b], 16)

                def body(n):
                    landed(sp, g_in, n.back(2), 128)
                    sp.dma_start(idx[n.b][:, :], lists_d[bass.ds(n.n, 1), :, 0:8].rearrange("a p c -> (a p) c")).then_inc(idx_in[n.b], 16)
                    wait(sp, turned, n.back(2))
                    sp.dma_start(attr[n.b][:, :, :], attr_v[bass.ds(n.n, 1)].rearrange("a p j c -> (a p) j c")).then_inc(attr_in[n.b], 16)
                    wait(sp, oh_ok, n.back(2))
                    sp.dma_start(lst[n.b][:, :], lists_d[bass.ds(n.n, 1), :, 8:16].rearrange("a p c -> (a p) c")).then_inc(list_in[n.b], 16)
                    store(n.back(3))

                last = rounds(sp, body, count_sb, 3)
                store(last.back(3))
                store(last.back(2))
                store(last.back(1))
                landed(sp, e_out, last.back(2))
                held(sp, passed)
                landed(sp, e_out, last.back(1))
                held(sp, passed)

            @block.gpsimd
            def _(pool):
                def body(n):
                    landed(pool, idx_in, n)
                    wait(pool, sum_ok, n.back(2))
                    held(pool, passed)
                    for j in range(8):
                        pool.indirect_dma_start(
                            out=g[n.b][:, j, :], out_offset=None, in_=xg_d,
                            in_offset=bass.IndirectOffsetOnAxis(ap=idx[n.b][:, j:j + 1].bitcast(U32), axis=0),
                        ).then_inc(g_in[n.b], 16)

                rounds(pool, body, count_sb)

            @block.tensor
            def _(pe):
                def spread_out(n):
                    if not n.exists():
                        return
                    wait(pe, rx_ok, n)
                    wait(pe, t_ok, n.back(1))
                    for i in range(TILES):
                        ins = nc.tensor.matmul(r_ps[:, P * i:P * i + P], rs_x[n.b][:, 2 * i:2 * i + 2, :].rearrange(
                            "p c d -> p (c d)"), ident[:, :], start=True, stop=True)
                    ins.then_inc(spread, 1)

                def sums(n):
                    if not n.exists():
                        return
                    landed(pe, g_in, n, 128)
                    wait(pe, oh_ok, n)
                    wait(pe, added, n.back(1))
                    for c in range(2):
                        for i in range(TILES):
                            j = c * TILES + i
                            ins = nc.tensor.matmul(agg_ps[64 * c:64 * c + 32, 0:WIN], g[n.b][:, j, :], ohb[n.b][:, j, :],
                                                   start=i == 0, stop=i == TILES - 1)
                    ins.then_inc(sum_ok, 1)

                def turn_in(n):
                    landed(pe, attr_in, n)
                    wait(pe, turned_sb, n.back(1))
                    held(pe, passed)
                    nc.tensor.transpose(at_ps[0:64, 0:P], attr[n.b][:, :, :].rearrange("p j c -> p (j c)"),
                                        ident[:, :]).then_inc(turned, 1)

                def encode(n):
                    if not n.exists():
                        return
                    wait(pe, turned_sb, n)
                    wait(pe, h_ok, n.back(1))
                    for i in range(TILES):
                        ins = nc.tensor.matmul(h_ps[:, P * i:P * i + P], enc_w0[:, i, :], attr_t[:, :], start=True, stop=True)
                    ins.then_inc(pre, 1)

                def second(n):
                    if not n.exists():
                        return
                    wait(pe, h_ok, n)
                    wait(pe, yb_ok, n.back(2))
                    nc.tensor.matmul(y_ps[n.b][:, :], w_mid[:, :], h[:, :], start=True, stop=True).then_inc(y_ok, 1)
                    wait(pe, sq_ok, n)
                    wait(pe, sd_ok, n.back(1))
                    for i in range(TILES):
                        ins = nc.tensor.matmul(var_ps[:, 2 * i:2 * i + 2], sq[:, P * i:P * i + P], mean_w[:, 0:P:D],
                                               start=True, stop=True)
                    ins.then_inc(var_ok, 1)

                def body(n):
                    encode(n.back(1))
                    turn_in(n)
                    spread_out(n.back(2))
                    sums(n.back(2))
                    second(n.back(1))

                last = rounds(pe, body, count_sb, 3)
                encode(last.back(1))
                spread_out(last.back(2))
                sums(last.back(2))
                second(last.back(1))
                spread_out(last.back(1))
                sums(last.back(1))

            @block.scalar
            def _(act):
                def warm(func):
                    nc.scalar.activation(idle[:, :], eps_c[:, :], func)

                def body(n):
                    warm(ACT.Silu)
                    wait(act, pre, n)
                    wait(act, y_ok, n.back(1))
                    nc.scalar.activation(h[:, :], h_ps[:, :], ACT.Silu, bias=col("b0")).then_inc(h_ok, 1)
                    wait(act, y_ok, n)
                    wait(act, var_ok, n.back(1))
                    nc.scalar.activation(sq[:, :], y_ps[n.b][:, :], ACT.Square, bias=col("b1")).then_inc(sq_ok, 1)
                    warm(ACT.Sqrt)
                    wait(act, var_ok, n)
                    wait(act, r_ok, n.back(1))
                    nc.scalar.activation(sd[:, :], var_ps[:, 0:2 * TILES], ACT.Sqrt, bias=eps_c[:, 0:1]).then_inc(sd_ok, 1)
                    wait(act, r_ok, n)
                    wait(act, spread, n.back(2))
                    nc.scalar.activation(rs_x[n.b][:, :, :], rs[:, :].rearrange("p (i c) -> p i c", c=1).broadcast_to(
                        [P, 2 * TILES, D]), ACT.Copy).then_inc(rx_ok, 1)
                    wait(act, t_ok, n.back(2))
                    nc.scalar.activation(yb[n.b][:, :], y_ps[n.b][:, :], ACT.Identity, bias=col("b1")).then_inc(yb_ok, 1)

                rounds(act, body, count_sb, 2)

            @block.vector
            def _(dve):
                v = nc.vector

                def invert(n):
                    if not n.exists():
                        return
                    wait(dve, sd_ok, n)
                    wait(dve, rx_ok, n.back(1))
                    v.reciprocal(rs[:, :], sd[:, :]).then_inc(r_ok, 1)

                def finish(n):
                    if not n.exists():
                        return
                    wait(dve, spread, n)
                    wait(dve, e_ok, n.back(1))
                    wait(dve, yb_ok, n)
                    v.tensor_tensor(t[:, :], yb[n.b][:, :], r_ps[:, :], ALU.mult).then_inc(t_ok, 1)
                    wait(dve, t_ok, n)
                    landed(dve, e_out, n.back(2))
                    v.tensor_scalar(e[n.b][:, :], t[:, :], col("g"), col("beta"), ALU.mult, ALU.add).then_inc(e_ok, 1)

                def add_sums(n):
                    if not n.exists():
                        return
                    at = [dve.value_load(base_sb[0:1, bass.ds(n.n * 2 + c, 1)], min_val=0, max_val=LAST_BASE) for c in range(2)]
                    wait(dve, sum_ok, n)
                    wait(dve, added, n.back(1))
                    for c in range(2):
                        a = agg[64 * c:64 * c + 32, bass.ds(at[c], WIN)]
                        ins = v.tensor_tensor(a, a, agg_ps[64 * c:64 * c + 32, 0:WIN], ALU.add)
                    ins.then_inc(added, 1)

                def one_hots(n):
                    if not n.exists():
                        return
                    landed(dve, list_in, n)
                    wait(dve, sum_ok, n.back(2))
                    for j in range(8):
                        ins = v.tensor_scalar(ohb[n.b][:, j, :], row_f[:, 0:WIN], lst[n.b][:, j:j + 1].bitcast(F32), None,
                                              ALU.is_equal)
                    ins.then_inc(oh_ok, 1)

                def body(n):
                    wait(dve, turned, n)
                    wait(dve, pre, n.back(1))
                    v.tensor_copy(attr_t[:, :], at_ps[0:64, 0:P]).then_inc(turned_sb, 1)
                    one_hots(n.back(1))
                    finish(n.back(2))
                    invert(n.back(1))
                    add_sums(n.back(2))

                v.memset(agg[:, :], 0.0).then_inc(zeroed, 1)
                dve.wait_ge(zeroed, 1)
                last = rounds(dve, body, count_sb, 3)
                one_hots(last.back(1))
                finish(last.back(2))
                invert(last.back(1))
                add_sums(last.back(2))
                finish(last.back(1))
                add_sums(last.back(1))


def edge_step(nc, lists_d, local_d, edge_d, ps_d, pr_d, base_sb, agg, w_in, w_mid, mean_w, ident, row_f, part64,
              vecs, eps_c, mlp, keep, count_sb):
    with ExitStack() as ctx:
        tag = mlp + "_"

        def sb(name, shape, dt=F32):
            return ctx.enter_context(nc.sbuf_tensor(tag + name, shape, dt))

        def two(name, shape, dt=F32):
            return [sb(f"{name}{i}", shape, dt) for i in range(2)]

        def ps(name):
            return ctx.enter_context(nc.psum_tensor(tag + name, [P, 512], F32))

        sem = ctx.enter_context(semaphores(nc, tag))

        idx = two("idx", [P, 8], I32)
        lst = two("lst", [P, 8], I32)
        dlb = two("dlb", [P, CHUNK], BF16)
        win = two("win", [P, P])
        g = two("g", [P, TILES, P])
        oha = two("oha", [P, CHUNK])
        ohb = two("ohb", [P, 8, WIN])
        e = two("e", [P, CHUNK])
        eb = two("eb", [P, CHUNK])
        h, sq, t = (sb(k, [P, CHUNK]) for k in ("h", "sq", "t"))
        sd, rs = sb("sd", [P, 2 * TILES]), sb("rs", [P, 2 * TILES])
        rs_x = two("rs_x", [P, 2 * TILES, D])
        yb = two("yb", [P, CHUNK])
        idle = sb("idle", [P, 1])
        new = two("new", [P, CHUNK])
        new_t = sb("new_t", [P, TILES, P])
        y_ps = [ps("yps0"), ps("yps1")]
        h_ps, var_ps, t_ps, agg_ps, r_ps = ps("hps"), ps("varps"), ps("tps"), ps("aggps"), ps("rps")
        idx_in, list_in, dlb_in, win_in, g_in, e_in, e_out = (
            [sem(f"{k}{i}") for i in range(2)] for k in ("idx_in", "list_in", "dlb_in", "win_in", "g_in", "e_in", "e_out"))
        passed = sem("passed")
        zeroed, pre, h_ok, y_ok, sq_ok, yb_ok, var_ok, sd_ok, r_ok, rx_ok, spread, t_ok, new_ok, eb_ok, oha_ok, ohb_ok, turned, turned_sb, sum_ok, added = (
            sem(k) for k in ("zeroed", "pre", "h_ok", "y_ok", "sq_ok", "yb_ok", "var_ok", "sd_ok", "r_ok", "rx_ok", "spread", "t_ok", "new_ok", "eb_ok",
                             "oha_ok", "ohb_ok", "turned", "turned_sb", "sum_ok", "added"))
        local_v = local_d.rearrange("(r c e) -> r c e", e=CHUNK, c=2)
        col = lambda what: vecs[:, vcol(mlp, what):vcol(mlp, what) + 1]
        with nc.Block() as block:
            @block.sync
            def _(sp):
                def store(n):
                    if keep and n.exists():
                        wait(sp, new_ok, n)
                        sp.dma_start(edge_d[bass.ds(n.n, 1)].rearrange("a p c -> (a p) c"), new[n.b][:, :]).then_inc(e_out[n.b], 16)

                def body(n):
                    landed(sp, g_in, n.back(2), 128)
                    sp.dma_start(idx[n.b][:, :], lists_d[bass.ds(n.n, 1), :, 0:8].rearrange("a p c -> (a p) c")).then_inc(idx_in[n.b], 16)
                    wait(sp, oha_ok, n.back(2))
                    for c in range(2):
                        sp.dma_start(dlb[n.b][64 * c:64 * c + 64, :],
                                     local_v[bass.ds(n.n, 1), c, :].broadcast_to([64, CHUNK])).then_inc(dlb_in[n.b], 16)
                    at = [sp.value_load(base_sb[0:1, bass.ds(n.n * 2 + c, 1)], min_val=0, max_val=LAST_BASE) for c in range(2)]
                    wait(sp, pre, n.back(2))
                    wait(sp, eb_ok, n.back(2))
                    sp.dma_start(e[n.b][:, :], edge_d[bass.ds(n.n, 1)].rearrange("a p c -> (a p) c")).then_inc(e_in[n.b], 16)
                    for c in range(2):
                        q = slice(64 * c, 64 * c + 64)
                        sp.dma_start(win[n.b][q, q], pr_d[bass.ds(at[c], WIN), :]).then_inc(win_in[n.b], 16)
                    wait(sp, ohb_ok, n.back(2))
                    sp.dma_start(lst[n.b][:, :], lists_d[bass.ds(n.n, 1), :, 8:16].rearrange("a p c -> (a p) c")).then_inc(list_in[n.b], 16)
                    store(n.back(3))

                sp.wait_ge(zeroed, 1)
                last = rounds(sp, body, count_sb, 3)
                store(last.back(3))
                store(last.back(2))
                store(last.back(1))
                if keep:
                    landed(sp, e_out, last.back(2))
                    held(sp, passed)
                    landed(sp, e_out, last.back(1))
                    held(sp, passed)

            @block.gpsimd
            def _(pool):
                def body(n):
                    landed(pool, idx_in, n)
                    wait(pool, pre, n.back(2))
                    held(pool, passed)
                    for j in range(8):
                        c, i = j // TILES, j % TILES
                        pool.indirect_dma_start(
                            out=g[n.b][:, i, 64 * c:64 * c + 64], out_offset=None, in_=ps_d,
                            in_offset=bass.IndirectOffsetOnAxis(ap=idx[n.b][:, j:j + 1].bitcast(U32), axis=0),
                        ).then_inc(g_in[n.b], 16)

                rounds(pool, body, count_sb)

            @block.tensor
            def _(pe):
                def spread_out(n):
                    if not n.exists():
                        return
                    wait(pe, rx_ok, n)
                    wait(pe, t_ok, n.back(1))
                    for i in range(TILES):
                        ins = nc.tensor.matmul(r_ps[:, P * i:P * i + P], rs_x[n.b][:, 2 * i:2 * i + 2, :].rearrange(
                            "p c d -> p (c d)"), ident[:, :], start=True, stop=True)
                    ins.then_inc(spread, 1)

                def turn(n):
                    if not n.exists():
                        return
                    wait(pe, new_ok, n)
                    wait(pe, turned_sb, n.back(1))
                    for i in range(TILES):
                        ins = nc.tensor.transpose(t_ps[:, P * i:P * i + P], new[n.b][:, P * i:P * i + P], ident[:, :])
                    ins.then_inc(turned, 1)

                def sums(n):
                    if not n.exists():
                        return
                    wait(pe, turned_sb, n)
                    wait(pe, ohb_ok, n)
                    wait(pe, added, n.back(1))
                    for c in range(2):
                        for i in range(TILES):
                            ins = nc.tensor.matmul(agg_ps[64 * c:64 * c + 64, 0:WIN], new_t[:, i, 64 * c:64 * c + 64],
                                                   ohb[n.b][:, TILES * c + i, :], start=i == 0, stop=i == TILES - 1)
                    ins.then_inc(sum_ok, 1)

                def body(n):
                    wait(pe, h_ok, n.back(1))
                    landed(pe, e_in, n)
                    nc.tensor.matmul(h_ps[:, :], w_in[:, :], e[n.b][:, :], start=True, stop=False)
                    landed(pe, win_in, n, 32)
                    wait(pe, oha_ok, n)
                    nc.tensor.matmul(h_ps[:, :], win[n.b][:, :], oha[n.b][:, :], start=False, stop=False)
                    landed(pe, g_in, n, 128)
                    for i in range(TILES):
                        ins = nc.tensor.matmul(h_ps[:, P * i:P * i + P], g[n.b][:, i, :], ident[:, :], start=False,
                                               stop=i == TILES - 1)
                    ins.then_inc(pre, 1)
                    spread_out(n.back(1))
                    sums(n.back(2))
                    wait(pe, h_ok, n)
                    wait(pe, yb_ok, n.back(2))
                    nc.tensor.matmul(y_ps[n.b][:, :], w_mid[:, :], h[:, :], start=True, stop=True).then_inc(y_ok, 1)
                    turn(n.back(1))
                    wait(pe, sq_ok, n)
                    wait(pe, sd_ok, n.back(1))
                    for i in range(TILES):
                        ins = nc.tensor.matmul(var_ps[:, 2 * i:2 * i + 2], sq[:, P * i:P * i + P], mean_w[:, 0:P:D],
                                               start=True, stop=True)
                    ins.then_inc(var_ok, 1)

                last = rounds(pe, body, count_sb, 3)
                spread_out(last.back(1))
                sums(last.back(2))
                turn(last.back(1))
                sums(last.back(1))

            @block.scalar
            def _(act):
                def warm(func):
                    nc.scalar.activation(idle[:, :], eps_c[:, :], func)

                def body(n):
                    warm(ACT.Silu)
                    wait(act, pre, n)
                    wait(act, y_ok, n.back(1))
                    nc.scalar.activation(h[:, :], h_ps[:, :], ACT.Silu, bias=col("b0")).then_inc(h_ok, 1)
                    landed(act, e_in, n)
                    wait(act, new_ok, n.back(2))
                    nc.scalar.activation(eb[n.b][:, :], e[n.b][:, :], ACT.Identity, bias=col("beta")).then_inc(eb_ok, 1)
                    wait(act, y_ok, n)
                    wait(act, var_ok, n.back(1))
                    nc.scalar.activation(sq[:, :], y_ps[n.b][:, :], ACT.Square, bias=col("b1")).then_inc(sq_ok, 1)
                    warm(ACT.Sqrt)
                    wait(act, var_ok, n)
                    wait(act, r_ok, n.back(1))
                    nc.scalar.activation(sd[:, :], var_ps[:, 0:2 * TILES], ACT.Sqrt, bias=eps_c[:, 0:1]).then_inc(sd_ok, 1)
                    wait(act, r_ok, n)
                    wait(act, spread, n.back(2))
                    nc.scalar.activation(rs_x[n.b][:, :, :], rs[:, :].rearrange("p (i c) -> p i c", c=1).broadcast_to(
                        [P, 2 * TILES, D]), ACT.Copy).then_inc(rx_ok, 1)
                    wait(act, t_ok, n.back(2))
                    nc.scalar.activation(yb[n.b][:, :], y_ps[n.b][:, :], ACT.Identity, bias=col("b1")).then_inc(yb_ok, 1)

                rounds(act, body, count_sb, 2)

            @block.vector
            def _(dve):
                v = nc.vector

                def invert(n):
                    if not n.exists():
                        return
                    wait(dve, sd_ok, n)
                    wait(dve, rx_ok, n.back(1))
                    v.reciprocal(rs[:, :], sd[:, :]).then_inc(r_ok, 1)

                def finish(n):
                    if not n.exists():
                        return
                    wait(dve, spread, n)
                    wait(dve, new_ok, n.back(1))
                    wait(dve, yb_ok, n)
                    v.tensor_tensor(t[:, :], yb[n.b][:, :], r_ps[:, :], ALU.mult).then_inc(t_ok, 1)
                    wait(dve, t_ok, n)
                    wait(dve, eb_ok, n)
                    wait(dve, turned, n.back(2))
                    if keep:
                        landed(dve, e_out, n.back(2))
                    v.scalar_tensor_tensor(new[n.b][:, :], t[:, :], col("g"), eb[n.b][:, :], ALU.mult, ALU.add).then_inc(new_ok, 1)

                def rows(n):
                    if not n.exists():
                        return
                    wait(dve, turned, n)
                    wait(dve, sum_ok, n.back(1))
                    v.tensor_copy(new_t[:, :, :], t_ps[:, :].rearrange("p (i q) -> p i q", q=P)).then_inc(turned_sb, 1)

                def add_sums(n):
                    if not n.exists():
                        return
                    at = [dve.value_load(base_sb[0:1, bass.ds(n.n * 2 + c, 1)], min_val=0, max_val=LAST_BASE) for c in range(2)]
                    wait(dve, sum_ok, n)
                    wait(dve, added, n.back(1))
                    for c in range(2):
                        a = agg[64 * c:64 * c + 64, bass.ds(at[c], WIN)]
                        ins = v.tensor_tensor(a, a, agg_ps[64 * c:64 * c + 64, 0:WIN], ALU.add)
                    ins.then_inc(added, 1)

                def one_hots(n):
                    if not n.exists():
                        return
                    landed(dve, list_in, n)
                    wait(dve, sum_ok, n.back(2))
                    for j in range(8):
                        ins = v.tensor_scalar(ohb[n.b][:, j, :], row_f[:, 0:WIN], lst[n.b][:, j:j + 1].bitcast(F32), None,
                                              ALU.is_equal)
                    ins.then_inc(ohb_ok, 1)

                def body(n):
                    landed(dve, dlb_in, n, 32)
                    wait(dve, pre, n.back(2))
                    v.tensor_scalar(oha[n.b][:, :], dlb[n.b][:, :], part64[:, 0:1], None, ALU.is_equal).then_inc(oha_ok, 1)
                    finish(n.back(2))
                    one_hots(n.back(1))
                    rows(n.back(2))
                    invert(n.back(1))
                    add_sums(n.back(3))

                for b in range(2):
                    v.memset(win[b][:, :], 0.0)
                v.memset(agg[:, :], 0.0).then_inc(zeroed, 1)
                dve.wait_ge(zeroed, 1)
                last = rounds(dve, body, count_sb, 3)
                finish(last.back(2))
                one_hots(last.back(1))
                rows(last.back(2))
                invert(last.back(1))
                add_sums(last.back(3))
                finish(last.back(1))
                rows(last.back(1))
                add_sums(last.back(2))
                add_sums(last.back(1))


def node_phase(nc, agg, node, x1, vecs, mean_w, ident, eps_c, ps_d, pr_d, mlp, w_in, w_mid, proj, sum_ab=None, w_agg=None,
               dec=None):
    first = sum_ab is not None
    with ExitStack() as ctx:
        tag = mlp + "_"

        def sb(name, shape, dt=F32):
            return ctx.enter_context(nc.sbuf_tensor(tag + name, shape, dt))

        def ps(name):
            return ctx.enter_context(nc.psum_tensor(tag + name, [P, 512], F32))

        sem = ctx.enter_context(semaphores(nc, tag))

        col = lambda what: vecs[:, vcol(mlp, what):vcol(mlp, what) + 1]
        h, sq, t, hd = (sb(k, [P, 512]) for k in ("h", "sq", "t", "hd"))
        sd, rs = sb("sd", [P, 2 * TILES]), sb("rs", [P, 2 * TILES])
        rs_x = sb("rs_x", [P, 2 * TILES, D])
        idle = sb("idle", [P, 1])
        yb = [sb(f"yb{i}", [P, 512]) for i in range(2)]
        stage = [sb(f"stage{i}", [P, 4, P]) for i in range(2)]
        res = [sb(f"res{i}", [P, 4, OUT_DIM]) for i in range(2)]
        h_ps, var_ps, r_ps, a_ps = ps("hps"), ps("varps"), ps("rps"), ps("aps")
        y_ps = [ps("yps0"), ps("yps1")]
        o_ps = [ps("ops0"), ps("ops1")]
        a_ok, a_taken, dstep, astep, norm_ok, turned, turned_sb, pre, h_ok, y_ok, sq_ok, yb_ok, var_ok, sd_ok, r_ok, rx_ok, spread, t_ok, nb_ok, n_ok, o_ok, st_ok, d_ok, hd_ok = (
            sem(k) for k in ("a_ok", "a_taken", "dve_step", "act_step", "norm_ok", "turned", "turned_sb", "pre", "h_ok",
                             "y_ok", "sq_ok", "yb_ok", "var_ok", "sd_ok", "r_ok", "rx_ok", "spread", "t_ok", "nb_ok", "n_ok", "o_ok", "st_ok", "d_ok", "hd_ok"))
        st_out = [sem("st_out0"), sem("st_out1")]
        if first:
            hn = sb("hn", [P, NT * 4, 2, X_DIM])
            ag = sb("ag", [P, HI, 32])
            sqn = sb("sqn", [P, HI, X_DIM])
            red, rinv, din = sb("red", [P, HI]), sb("rinv", [P, HI]), sb("din", [P, HI])
            ht = sb("ht", [32, 512])
        nd, na, jobs = [0], [0], []

        def stores(q, k):
            if not dec:
                return 2 * (k + 1)
            rows = [max(0, min(512, N_NODES - HALF * q - 512 * i)) for i in range(k + 1)]
            return sum((r >= P) + (r % P > 0) for r in rows)

        AG = HI // 8
        with nc.Block() as block:
            @block.tensor
            def _(pe):
                if first:
                    for k in range(AG):
                        if k >= 2:
                            pe.wait_ge(a_taken, k - 1)
                        for i in range(8):
                            hi = 8 * k + i
                            ins = nc.tensor.matmul(o_ps[k % 2][:, 32 * i:32 * i + 32], agg[:, P * hi:P * hi + P],
                                                   sum_ab[:, :], start=True, stop=True)
                        ins.then_inc(a_ok, 1)
                    pe.wait_ge(norm_ok, 1)
                def spread_out(k):
                    pe.wait_ge(rx_ok, k + 1)
                    if k:
                        pe.wait_ge(t_ok, k)
                    for i in range(TILES):
                        ins = nc.tensor.matmul(r_ps[:, P * i:P * i + P], rs_x[:, 2 * i:2 * i + 2, :].rearrange(
                            "p c d -> p (c d)"), ident[:, :], start=True, stop=True)
                    ins.then_inc(spread, 1)

                def tail(k):
                    pe.wait_ge(n_ok, k + 1)
                    if dec:
                        if k:
                            pe.wait_ge(hd_ok, k)
                        nc.tensor.matmul(a_ps[:, :], dec[0][:, :], node[:, 512 * k:512 * k + 512],
                                         start=True, stop=True).then_inc(d_ok, 1)
                        pe.wait_ge(hd_ok, k + 1)
                    for q in range(2):
                        if k:
                            pe.wait_ge(st_ok, 2 * (k - 1) + q + 1)
                        r = slice(64 * q, 64 * q + 64)
                        for i in range(4):
                            if dec:
                                ins = nc.tensor.matmul(o_ps[q][:, OUT_DIM * i:OUT_DIM * i + OUT_DIM], hd[r, P * i:P * i + P],
                                                       dec[1][r, :], start=True, stop=True)
                            else:
                                ins = nc.tensor.matmul(o_ps[q][:, P * i:P * i + P], node[r, 512 * k + P * i:512 * k + P * i + P],
                                                       proj[r, :], start=True, stop=True)
                        ins.then_inc(o_ok, 1)

                for k in range(NT):
                    c = slice(512 * k, 512 * k + 512)
                    if first:
                        if k:
                            pe.wait_ge(turned_sb, k)
                        for q in range(4):
                            ins = nc.tensor.transpose(a_ps[0:32, P * q:P * q + P],
                                                      hn[:, 4 * k + q, :, :].rearrange("p a c -> p (a c)"), ident[:, :])
                        ins.then_inc(turned, 1)
                        pe.wait_ge(turned_sb, k + 1)
                        if k:
                            pe.wait_ge(h_ok, k)
                        nc.tensor.matmul(h_ps[:, :], w_in[:, :], ht[:, :], start=True, stop=True).then_inc(pre, 1)
                    else:
                        if k:
                            pe.wait_ge(h_ok, k)
                        nc.tensor.matmul(h_ps[:, :], w_in[:, :], node[:, c], start=True, stop=False)
                        for q in range(2):
                            ins = nc.tensor.matmul(h_ps[64 * q:64 * q + 64, :], w_agg[:, :],
                                                   agg[:, HALF * q + 512 * k:HALF * q + 512 * k + 512], start=False, stop=True)
                        ins.then_inc(pre, 1)
                    if k:
                        spread_out(k - 1)
                    pe.wait_ge(h_ok, k + 1)
                    if k >= 2:
                        pe.wait_ge(yb_ok, k - 1)
                    nc.tensor.matmul(y_ps[k % 2][:, :], w_mid[:, :], h[:, :], start=True, stop=True).then_inc(y_ok, 1)
                    pe.wait_ge(sq_ok, k + 1)
                    if k:
                        pe.wait_ge(sd_ok, k)
                    for i in range(TILES):
                        ins = nc.tensor.matmul(var_ps[:, 2 * i:2 * i + 2], sq[:, P * i:P * i + P], mean_w[:, 0:P:D],
                                               start=True, stop=True)
                    ins.then_inc(var_ok, 1)
                    if k:
                        tail(k - 1)
                spread_out(NT - 1)
                tail(NT - 1)

            @block.vector
            def _(dve):
                v = nc.vector

                def dve_step(ins):
                    nd[0] += 1
                    ins.then_inc(dstep, 1)
                    dve.wait_ge(dstep, nd[0])

                def act_step(ins):
                    na[0] += 1
                    jobs.append((nd[0], ins))
                    dve.wait_ge(astep, na[0])

                if first:
                    for k in range(AG):
                        dve.wait_ge(a_ok, k + 1)
                        v.tensor_copy(ag[:, 8 * k:8 * k + 8, :],
                                      o_ps[k % 2][:, 0:256].rearrange("p (i c) -> p i c", c=32)).then_inc(a_taken, 1)
                    dve.wait_ge(a_taken, AG)
                    dve_step(v.tensor_scalar(din[:, :], ag[:, :, X_DIM:X_DIM + 1].rearrange("p r j -> p (r j)"), 1.0, None, ALU.max))
                    act_step(lambda: nc.scalar.activation(din[:, :], din[:, :], ACT.Sqrt))
                    dve_step(v.reciprocal(din[:, :], din[:, :]))
                    dve_step(v.tensor_tensor(ag[:, :, 0:X_DIM], ag[:, :, 0:X_DIM],
                                             din[:, :].rearrange("p (r j) -> p r j", j=1).broadcast_to([P, HI, X_DIM]), ALU.mult))
                    dve_step(v.tensor_tensor(x1[:, :, :], x1[:, :, :], ag[:, :, 0:X_DIM], ALU.add))
                    norm_rows(nc, dve_step, act_step, ag[:, :, 0:X_DIM], x1[:, :, :], sqn[:, :, :], red[:, :], rinv[:, :], eps_c, HI)
                    for q in range(2):
                        ins = v.tensor_copy(hn[:, :, q, :], ag[:, 52 * q:52 * q + 52, 0:X_DIM])
                    ins.then_inc(norm_ok, 1)
                def turn_in(k):
                    dve.wait_ge(turned, k + 1)
                    if k:
                        dve.wait_ge(pre, k)
                    v.tensor_copy(ht[:, :], a_ps[0:32, :]).then_inc(turned_sb, 1)

                def finish(k):
                    c = slice(512 * k, 512 * k + 512)
                    dve.wait_ge(sd_ok, k + 1)
                    if k:
                        dve.wait_ge(rx_ok, k)
                    v.reciprocal(rs[:, :], sd[:, :]).then_inc(r_ok, 1)
                    dve.wait_ge(spread, k + 1)
                    if k:
                        dve.wait_ge(n_ok, k)
                    dve.wait_ge(yb_ok, k + 1)
                    v.tensor_tensor(t[:, :], yb[k % 2][:, :], r_ps[:, :], ALU.mult).then_inc(t_ok, 1)
                    dve.wait_ge(t_ok, k + 1)
                    if first:
                        v.tensor_scalar(node[:, c], t[:, :], col("g"), col("beta"), ALU.mult, ALU.add).then_inc(n_ok, 1)
                    else:
                        dve.wait_ge(nb_ok, k + 1)
                        v.scalar_tensor_tensor(node[:, c], t[:, :], col("g"), node[:, c], ALU.mult, ALU.add).then_inc(n_ok, 1)

                def results(k):
                    for q in range(2):
                        dve.wait_ge(o_ok, 2 * k + q + 1)
                        if k:
                            dve.wait_ge(st_out[q], 16 * stores(q, k - 1))
                        if dec:
                            blk = 52 * q + 4 * k
                            dve_step(v.tensor_tensor(res[q][:, :, :], o_ps[q][:, 0:4 * OUT_DIM].rearrange("p (i c) -> p i c", c=OUT_DIM),
                                                     x1[:, blk:blk + 4, :], ALU.add))
                            for i in range(4):
                                ins = v.tensor_tensor(res[q][:, i, :], res[q][:, i, :], dec[2][:, :], ALU.add)
                            ins.then_inc(st_ok, 1)
                        else:
                            v.tensor_copy(stage[q][:, :, :], o_ps[q][:, :].rearrange("p (i c) -> p i c", c=P)).then_inc(st_ok, 1)
                for k in range(NT):
                    if first:
                        turn_in(k)
                    if k:
                        finish(k - 1)
                        results(k - 1)
                finish(NT - 1)
                results(NT - 1)

            @block.scalar
            def _(act):
                for at, ins in jobs:
                    act.wait_ge(dstep, at)
                    ins().then_inc(astep, 1)
                def warm(func):
                    nc.scalar.activation(idle[:, :], eps_c[:, :], func)

                def decode(k):
                    act.wait_ge(d_ok, k + 1)
                    if k:
                        act.wait_ge(o_ok, 2 * k)
                    nc.scalar.activation(hd[:, :], a_ps[:, :], ACT.Silu, bias=vecs[:, DEC_B0:DEC_B0 + 1]).then_inc(hd_ok, 1)

                for k in range(NT):
                    c = slice(512 * k, 512 * k + 512)
                    warm(ACT.Silu)
                    act.wait_ge(pre, k + 1)
                    if k:
                        act.wait_ge(y_ok, k)
                    nc.scalar.activation(h[:, :], h_ps[:, :], ACT.Silu, bias=col("b0")).then_inc(h_ok, 1)
                    if not first:
                        nc.scalar.activation(node[:, c], node[:, c], ACT.Identity, bias=col("beta")).then_inc(nb_ok, 1)
                    act.wait_ge(y_ok, k + 1)
                    if k:
                        act.wait_ge(var_ok, k)
                    nc.scalar.activation(sq[:, :], y_ps[k % 2][:, :], ACT.Square, bias=col("b1")).then_inc(sq_ok, 1)
                    if k >= 2:
                        act.wait_ge(t_ok, k - 1)
                    nc.scalar.activation(yb[k % 2][:, :], y_ps[k % 2][:, :], ACT.Identity, bias=col("b1")).then_inc(yb_ok, 1)
                    if dec and k:
                        decode(k - 1)
                    act.wait_ge(var_ok, k + 1)
                    if k:
                        act.wait_ge(r_ok, k)
                    nc.scalar.activation(sd[:, :], var_ps[:, 0:2 * TILES], ACT.Sqrt, bias=eps_c[:, 0:1]).then_inc(sd_ok, 1)
                    act.wait_ge(r_ok, k + 1)
                    if k:
                        act.wait_ge(spread, k)
                    nc.scalar.activation(rs_x[:, :, :], rs[:, :].rearrange("p (i c) -> p i c", c=1).broadcast_to(
                        [P, 2 * TILES, D]), ACT.Copy).then_inc(rx_ok, 1)
                if dec:
                    decode(NT - 1)

            @block.sync
            def _(sp):
                for k in range(NT):
                    for q in range(2):
                        sp.wait_ge(st_ok, 2 * k + q + 1)
                        r0 = HALF * q + 512 * k
                        if dec:
                            full = max(0, min(4, (N_NODES - r0) // P))
                            if full:
                                sp.dma_start(dec[3][r0:r0 + P * full, :].rearrange("(i p) c -> p i c", p=P),
                                             res[q][:, 0:full, :]).then_inc(st_out[q], 16)
                            rest = N_NODES - r0 - P * full
                            if full < 4 and 0 < rest < P:
                                sp.dma_start(dec[3][r0 + P * full:N_NODES, :], res[q][0:rest, full, :]).then_inc(st_out[q], 16)
                            continue
                        for i, table in enumerate((ps_d, pr_d)):
                            sp.dma_start(table[r0:r0 + 512, :].rearrange("(i p) c -> p i c", p=P),
                                         stage[q][:, :, D * i:D * i + D]).then_inc(st_out[q], 16)
                for q in range(2):
                    sp.wait_ge(st_out[q], 16 * stores(q, NT - 1))


_W = ["node_enc", "edge_enc", "edge_blk", "node_blk"]
_WNAMES = [f"{k}_{p}" for k in _W for p in ("w0", "b0", "w1", "b1", "g", "beta")] + ["dec_w0", "dec_b0", "dec_w1", "dec_b1"]
_INS = ["x", "src", "dst", "edge_attr_8"] + ["L1_gnn_" + k for k in _WNAMES]


def kernel(**inputs):
    import numpy as np
    import concourse.bacc as bacc
    from concourse.bass_utils import run_bass_kernel_spmd

    nc = bacc.Bacc("TRN2", target_bir_lowering=False, num_devices=1)
    arrays, aps = {}, {}
    for name in _INS:
        a = np.ascontiguousarray(inputs[name])
        arrays[f"in_{name}"] = a
        aps[name] = nc.dram_tensor(f"in_{name}", a.shape, mybir.dt.from_np(a.dtype), kind="ExternalInput").ap()
    out = nc.dram_tensor("out_nodes", (N_NODES, OUT_DIM), F32, kind="ExternalOutput").ap()
    gnn_kernel(nc, aps["x"], aps["src"], aps["dst"], aps["edge_attr_8"], {k: aps["L1_gnn_" + k] for k in _WNAMES}, out)
    r = run_bass_kernel_spmd(nc, [arrays], core_ids=[0])
    return r.results[0]["out_nodes"]
```
